# Optimizing a Trainium2 kernel written in Bass

```python
import numpy as np
import jax
import jax.numpy as jnp

def _softmax(x, axis=-1):
    return jax.nn.softmax(x, axis=axis)

def _gelu(x):
    return jax.nn.gelu(x, approximate=True)

def _silu(x):
    return jax.nn.silu(x)

def _sigmoid(x):
    return jax.nn.sigmoid(x)

def _layernorm(x, axis=-1, eps=1e-05):
    m = jnp.mean(x, axis=axis, keepdims=True)
    v = jnp.var(x, axis=axis, keepdims=True)
    return (x - m) / jnp.sqrt(v + eps)

def _scatter_add(tgt, idx, src, axis=0):
    return tgt.at[idx].add(src)

def _segment_sum(src, seg, n):
    return jax.ops.segment_sum(src, seg, n)
kernel_name = 'mk_vit_tower_cls_d1_tok_img768_r4_bedf93'

def setup_inputs(seed: int=0):
    np.random.seed(seed)
    _w = jnp.asarray

    def _rec_inputs():
        import jax
        import jax.numpy as jnp
        _rk = jax.random.key(seed)
        x = -9.30917e-05 + 1.0002 * jax.random.normal(jax.random.fold_in(_rk, 1), (32, 3, 112, 112), jnp.float32)
        cls_tok = 0.02 * jax.random.normal(jax.random.fold_in(_rk, 5), (1, 1, 192), jnp.float32)
        return (x, cls_tok)
    x, cls_tok = _rec_inputs()

    def _L0_tok_setup():
        import jax, jax.numpy as jnp
        import numpy as np
        DN = ('NCHW', 'OIHW', 'NCHW')
        G = 7

        def conv(x, w, stride, pad, groups=1):
            return jax.lax.conv_general_dilated(x, w, (stride, stride), [(pad, pad), (pad, pad)], feature_group_count=groups, dimension_numbers=DN)

        def gelu(x):
            return jax.nn.gelu(x, approximate=False)

        def bn(x, s, b):
            return x * s[None, :, None, None] + b[None, :, None, None]

        def region_layer_dw(x, wdw, sdw, bdw, wpw, spw, bpw):
            B, C, H, W = x.shape
            h, w = (H // G, W // G)
            xr = x.reshape(B, C, G, h, G, w).transpose(0, 2, 4, 1, 3, 5).reshape(B, G * G * C, h, w)
            y = gelu(bn(conv(xr, wdw, 1, 1, groups=G * G * C), sdw, bdw))
            y = bn(conv(y, wpw, 1, 0, groups=G * G), spw, bpw)
            xr = y + xr
            return xr.reshape(B, G, G, C, h, w).transpose(0, 3, 1, 4, 2, 5).reshape(B, C, H, W)
        key = jax.random.key(seed)
        ks = jax.random.split(key, 8)
        B, C0, H, W = (32, 3, 224, 224)
        E = 192
        C1 = E // 16
        C2 = E // 4
        R = G * G
        rn = lambda k, shp, sc: jax.random.normal(k, shp, jnp.float32) * sc
        return {'x': rn(ks[0], (B, C0, H, W), 1.0), 'w0': rn(ks[1], (C1, C0, 3, 3), 0.2), 's0': jnp.ones((C1,), jnp.float32), 'b0': jnp.zeros((C1,), jnp.float32), 'wdw': rn(ks[2], (R * C1, 1, 3, 3), 0.2), 'sdw': jnp.ones((R * C1,), jnp.float32), 'bdw': jnp.zeros((R * C1,), jnp.float32), 'wpw': rn(ks[3], (R * C1, C1, 1, 1), 0.1), 'spw': jnp.ones((R * C1,), jnp.float32), 'bpw': jnp.zeros((R * C1,), jnp.float32), 'w1': rn(ks[4], (C2, C1, 4, 4), 0.05), 's1': jnp.ones((C2,), jnp.float32), 'b1': jnp.zeros((C2,), jnp.float32), 'w2': rn(ks[5], (C2, C2, 2, 2), 0.05), 's2': jnp.ones((C2,), jnp.float32), 'b2': jnp.zeros((C2,), jnp.float32), 'w3': rn(ks[6], (E, C2, 2, 2), 0.05), 's3': jnp.ones((E,), jnp.float32), 'b3': jnp.zeros((E,), jnp.float32)}
    _L0_tok_all = _L0_tok_setup()
    _L0_tok_in = {k: v for k, v in _L0_tok_all.items() if k in ('w0', 's0', 'b0', 'wdw', 'sdw', 'bdw', 'wpw', 'spw', 'bpw', 'w1', 's1', 'b1', 'w2', 's2', 'b2', 'w3', 's3', 'b3')}
    del _L0_tok_all

    def _L0_attn_setup():
        import jax, jax.numpy as jnp
        import numpy as np
        SEQ_LEN = 1024
        EMB = 3
        FILTER_ORDER = 16
        CH = 192
        BATCH = 16
        SHIFT = 0.0
        MODULATE = True
        USE_BIAS = True
        FAST_DECAY_PCT = 0.3
        SLOW_DECAY_PCT = 1.5
        TARGET = 0.01

        def _pos_emb(L):
            t = jnp.linspace(0.0, 1.0, L)
            bands = (EMB - 1) // 2
            t_rescaled = jnp.linspace(0.0, float(L - 1), L)
            w = 2.0 * jnp.pi * t_rescaled / L
            f = jnp.linspace(0.0001, float(max(bands - 1, 0)), bands)
            z_c = jnp.exp(-1j * f[None, :] * w[:, None])
            z = jnp.concatenate([t[:, None], jnp.real(z_c), jnp.imag(z_c)], axis=-1)
            return (z.astype(jnp.float32), t.astype(jnp.float32))

        def _implicit_filter(L, w1, b1, w2, b2, w3, b3, freq, deltas_abs):
            z, t = _pos_emb(L)
            h = jnp.sin(freq * (z @ w1.T + b1))
            h = jnp.sin(freq * (h @ w2.T + b2))
            h = h @ w3.T + b3
            if MODULATE:
                decay = jnp.exp(-t[:, None] * deltas_abs[None, :])
                h = h * (decay + SHIFT)
            return h

        def fft_conv(u, k):
            seqlen = u.shape[-2]
            fft_size = 2 * seqlen
            u_f = jnp.fft.rfft(u.astype(jnp.float32), n=fft_size, axis=-2)
            k_f = jnp.fft.rfft(k.astype(jnp.float32), n=fft_size, axis=-2) / fft_size
            y = jnp.fft.irfft(u_f * k_f, n=fft_size, axis=-2)[..., :seqlen, :]
            return y.astype(u.dtype)
        key = jax.random.key(seed)
        ks = jax.random.split(key, 8)
        u = jax.random.normal(ks[0], (BATCH, SEQ_LEN, CH), dtype=jnp.float32)
        w1 = jax.random.normal(ks[1], (FILTER_ORDER, EMB), dtype=jnp.float32) * 0.5
        b1 = jax.random.normal(ks[2], (FILTER_ORDER,), dtype=jnp.float32) * 0.1
        w2 = jax.random.normal(ks[3], (FILTER_ORDER, FILTER_ORDER), dtype=jnp.float32) * 0.25
        b2 = jax.random.normal(ks[4], (FILTER_ORDER,), dtype=jnp.float32) * 0.1
        w3 = jax.random.normal(ks[5], (CH, FILTER_ORDER), dtype=jnp.float32) * 0.25
        b3 = jax.random.normal(ks[6], (CH,), dtype=jnp.float32) * 0.1
        freq = jnp.ones((FILTER_ORDER,), dtype=jnp.float32)
        max_decay = np.log(TARGET) / FAST_DECAY_PCT
        min_decay = np.log(TARGET) / SLOW_DECAY_PCT
        deltas_abs = jnp.abs(jnp.linspace(min_decay, max_decay, CH)).astype(jnp.float32)
        bias = jax.random.normal(ks[7], (CH,), dtype=jnp.float32)
        return {'u': u, 'w1': w1, 'b1': b1, 'w2': w2, 'b2': b2, 'w3': w3, 'b3': b3, 'freq': freq, 'deltas_abs': deltas_abs, 'bias': bias}
    _L0_attn_all = _L0_attn_setup()
    _L0_attn_in = {k: v for k, v in _L0_attn_all.items() if k in ('w1', 'b1', 'w2', 'b2', 'w3', 'b3', 'freq', 'deltas_abs', 'bias')}
    del _L0_attn_all

    def _L0_ffn_setup():
        import jax, jax.numpy as jnp
        import numpy as np
        B, N, DIM, HEADS = (4, 256, 192, 12)
        HIDDEN, E, TOPK = (768, 8, 2)
        EPS = 1e-05

        def _layernorm(x, g, b):
            mu = jnp.mean(x, axis=-1, keepdims=True)
            var = jnp.var(x, axis=-1, keepdims=True)
            return (x - mu) * jax.lax.rsqrt(var + EPS) * g + b
        key = jax.random.key(seed)
        ks = jax.random.split(key, 10)
        s = 0.02
        return {'x': jax.random.normal(ks[0], (B, N, DIM), dtype=jnp.float32), 'ln1_g': jnp.ones((DIM,), jnp.float32), 'ln1_b': jnp.zeros((DIM,), jnp.float32), 'qkv_w': jax.random.normal(ks[1], (3 * DIM, DIM), jnp.float32) * s, 'proj_w': jax.random.normal(ks[2], (DIM, DIM), jnp.float32) * s, 'proj_b': jnp.zeros((DIM,), jnp.float32), 'ln2_g': jnp.ones((DIM,), jnp.float32), 'ln2_b': jnp.zeros((DIM,), jnp.float32), 'gate_w': jax.random.normal(ks[3], (E, DIM), jnp.float32) * s, 'gate_b': jnp.zeros((E,), jnp.float32), 'w1': jax.random.normal(ks[4], (E, HIDDEN, DIM), jnp.float32) * s, 'b1': jnp.zeros((E, HIDDEN), jnp.float32), 'w2': jax.random.normal(ks[5], (E, DIM, HIDDEN), jnp.float32) * s, 'b2': jnp.zeros((E, DIM), jnp.float32)}
    _L0_ffn_all = _L0_ffn_setup()
    _L0_ffn_in = {k: v for k, v in _L0_ffn_all.items() if k in ('ln1_g', 'ln1_b', 'qkv_w', 'proj_w', 'proj_b', 'ln2_g', 'ln2_b', 'gate_w', 'gate_b', 'w1', 'b1', 'w2', 'b2')}
    del _L0_ffn_all
    return {'x': x, 'cls_tok': cls_tok, 'L0_tok_w0': _L0_tok_in['w0'], 'L0_tok_s0': _L0_tok_in['s0'], 'L0_tok_b0': _L0_tok_in['b0'], 'L0_tok_wdw': _L0_tok_in['wdw'], 'L0_tok_sdw': _L0_tok_in['sdw'], 'L0_tok_bdw': _L0_tok_in['bdw'], 'L0_tok_wpw': _L0_tok_in['wpw'], 'L0_tok_spw': _L0_tok_in['spw'], 'L0_tok_bpw': _L0_tok_in['bpw'], 'L0_tok_w1': _L0_tok_in['w1'], 'L0_tok_s1': _L0_tok_in['s1'], 'L0_tok_b1': _L0_tok_in['b1'], 'L0_tok_w2': _L0_tok_in['w2'], 'L0_tok_s2': _L0_tok_in['s2'], 'L0_tok_b2': _L0_tok_in['b2'], 'L0_tok_w3': _L0_tok_in['w3'], 'L0_tok_s3': _L0_tok_in['s3'], 'L0_tok_b3': _L0_tok_in['b3'], 'L0_attn_w1': _L0_attn_in['w1'], 'L0_attn_b1': _L0_attn_in['b1'], 'L0_attn_w2': _L0_attn_in['w2'], 'L0_attn_b2': _L0_attn_in['b2'], 'L0_attn_w3': _L0_attn_in['w3'], 'L0_attn_b3': _L0_attn_in['b3'], 'L0_attn_freq': _L0_attn_in['freq'], 'L0_attn_deltas_abs': _L0_attn_in['deltas_abs'], 'L0_attn_bias': _L0_attn_in['bias'], 'L0_ffn_ln1_g': _L0_ffn_in['ln1_g'], 'L0_ffn_ln1_b': _L0_ffn_in['ln1_b'], 'L0_ffn_qkv_w': _L0_ffn_in['qkv_w'], 'L0_ffn_proj_w': _L0_ffn_in['proj_w'], 'L0_ffn_proj_b': _L0_ffn_in['proj_b'], 'L0_ffn_ln2_g': _L0_ffn_in['ln2_g'], 'L0_ffn_ln2_b': _L0_ffn_in['ln2_b'], 'L0_ffn_gate_w': _L0_ffn_in['gate_w'], 'L0_ffn_gate_b': _L0_ffn_in['gate_b'], 'L0_ffn_w1': _L0_ffn_in['w1'], 'L0_ffn_b1': _L0_ffn_in['b1'], 'L0_ffn_w2': _L0_ffn_in['w2'], 'L0_ffn_b2': _L0_ffn_in['b2']}

def reference(x, cls_tok, L0_tok_w0, L0_tok_s0, L0_tok_b0, L0_tok_wdw, L0_tok_sdw, L0_tok_bdw, L0_tok_wpw, L0_tok_spw, L0_tok_bpw, L0_tok_w1, L0_tok_s1, L0_tok_b1, L0_tok_w2, L0_tok_s2, L0_tok_b2, L0_tok_w3, L0_tok_s3, L0_tok_b3, L0_attn_w1, L0_attn_b1, L0_attn_w2, L0_attn_b2, L0_attn_w3, L0_attn_b3, L0_attn_freq, L0_attn_deltas_abs, L0_attn_bias, L0_ffn_ln1_g, L0_ffn_ln1_b, L0_ffn_qkv_w, L0_ffn_proj_w, L0_ffn_proj_b, L0_ffn_ln2_g, L0_ffn_ln2_b, L0_ffn_gate_w, L0_ffn_gate_b, L0_ffn_w1, L0_ffn_b1, L0_ffn_w2, L0_ffn_b2):
    import jax
    import jax.numpy as jnp

    def _L0_tok_ref(x, w0, s0, b0, wdw, sdw, bdw, wpw, spw, bpw, w1, s1, b1, w2, s2, b2, w3, s3, b3):
        import jax, jax.numpy as jnp
        import numpy as np
        DN = ('NCHW', 'OIHW', 'NCHW')
        G = 7

        def conv(x, w, stride, pad, groups=1):
            return jax.lax.conv_general_dilated(x, w, (stride, stride), [(pad, pad), (pad, pad)], feature_group_count=groups, dimension_numbers=DN)

        def gelu(x):
            return jax.nn.gelu(x, approximate=False)

        def bn(x, s, b):
            return x * s[None, :, None, None] + b[None, :, None, None]

        def region_layer_dw(x, wdw, sdw, bdw, wpw, spw, bpw):
            B, C, H, W = x.shape
            h, w = (H // G, W // G)
            xr = x.reshape(B, C, G, h, G, w).transpose(0, 2, 4, 1, 3, 5).reshape(B, G * G * C, h, w)
            y = gelu(bn(conv(xr, wdw, 1, 1, groups=G * G * C), sdw, bdw))
            y = bn(conv(y, wpw, 1, 0, groups=G * G), spw, bpw)
            xr = y + xr
            return xr.reshape(B, G, G, C, h, w).transpose(0, 3, 1, 4, 2, 5).reshape(B, C, H, W)
        x = gelu(bn(conv(x, w0, 1, 1), s0, b0))
        x = region_layer_dw(x, wdw, sdw, bdw, wpw, spw, bpw)
        x = gelu(x)
        x = gelu(bn(conv(x, w1, 4, 0), s1, b1))
        x = gelu(bn(conv(x, w2, 2, 0), s2, b2))
        x = bn(conv(x, w3, 2, 0), s3, b3)
        B, E, Hp, Wp = x.shape
        return x.reshape(B, E, Hp * Wp).transpose(0, 2, 1)

    def _L0_attn_ref(u, w1, b1, w2, b2, w3, b3, freq, deltas_abs, bias):
        import jax, jax.numpy as jnp
        import numpy as np
        SEQ_LEN = 1024
        EMB = 3
        FILTER_ORDER = 16
        CH = 192
        BATCH = 16
        SHIFT = 0.0
        MODULATE = True
        USE_BIAS = True
        FAST_DECAY_PCT = 0.3
        SLOW_DECAY_PCT = 1.5
        TARGET = 0.01

        def _pos_emb(L):
            t = jnp.linspace(0.0, 1.0, L)
            bands = (EMB - 1) // 2
            t_rescaled = jnp.linspace(0.0, float(L - 1), L)
            w = 2.0 * jnp.pi * t_rescaled / L
            f = jnp.linspace(0.0001, float(max(bands - 1, 0)), bands)
            z_c = jnp.exp(-1j * f[None, :] * w[:, None])
            z = jnp.concatenate([t[:, None], jnp.real(z_c), jnp.imag(z_c)], axis=-1)
            return (z.astype(jnp.float32), t.astype(jnp.float32))

        def _implicit_filter(L, w1, b1, w2, b2, w3, b3, freq, deltas_abs):
            z, t = _pos_emb(L)
            h = jnp.sin(freq * (z @ w1.T + b1))
            h = jnp.sin(freq * (h @ w2.T + b2))
            h = h @ w3.T + b3
            if MODULATE:
                decay = jnp.exp(-t[:, None] * deltas_abs[None, :])
                h = h * (decay + SHIFT)
            return h

        def fft_conv(u, k):
            seqlen = u.shape[-2]
            fft_size = 2 * seqlen
            u_f = jnp.fft.rfft(u.astype(jnp.float32), n=fft_size, axis=-2)
            k_f = jnp.fft.rfft(k.astype(jnp.float32), n=fft_size, axis=-2) / fft_size
            y = jnp.fft.irfft(u_f * k_f, n=fft_size, axis=-2)[..., :seqlen, :]
            return y.astype(u.dtype)
        L = u.shape[-2]
        k = _implicit_filter(L, w1, b1, w2, b2, w3, b3, freq, deltas_abs)
        y = fft_conv(u, k)
        if USE_BIAS:
            y = y + u * bias
        return y

    def _L0_ffn_ref(x, ln1_g, ln1_b, qkv_w, proj_w, proj_b, ln2_g, ln2_b, gate_w, gate_b, w1, b1, w2, b2):
        import jax, jax.numpy as jnp
        import numpy as np
        B, N, DIM, HEADS = (4, 256, 192, 12)
        HIDDEN, E, TOPK = (768, 8, 2)
        EPS = 1e-05

        def _layernorm(x, g, b):
            mu = jnp.mean(x, axis=-1, keepdims=True)
            var = jnp.var(x, axis=-1, keepdims=True)
            return (x - mu) * jax.lax.rsqrt(var + EPS) * g + b
        b, n, d = x.shape
        hd = d // HEADS
        scale = hd ** (-0.5)
        h = _layernorm(x, ln1_g, ln1_b)
        qkv = h @ qkv_w.T
        qkv = qkv.reshape(b, n, 3, HEADS, hd).transpose(2, 0, 3, 1, 4)
        q, k, v = (qkv[0], qkv[1], qkv[2])
        attn = jax.nn.softmax(jnp.einsum('bhnd,bhmd->bhnm', q, k) * scale, axis=-1)
        a = jnp.einsum('bhnm,bhmd->bhnd', attn, v)
        a = a.transpose(0, 2, 1, 3).reshape(b, n, d)
        a = a @ proj_w.T + proj_b
        x = x + a
        h2 = _layernorm(x, ln2_g, ln2_b)
        t = h2.reshape(-1, d)
        T = t.shape[0]
        logits = t @ gate_w.T + gate_b
        top_val, top_idx = jax.lax.top_k(logits, TOPK)
        score = jax.nn.softmax(top_val, axis=-1)
        cw = jnp.zeros((T, E), t.dtype).at[jnp.arange(T)[:, None], top_idx].add(score)
        out = jnp.zeros_like(t)
        for e in range(E):
            he = jax.nn.gelu(t @ w1[e].T + b1[e], approximate=False)
            ye = he @ w2[e].T + b2[e]
            out = out + cw[:, e:e + 1] * ye
        return x + out.reshape(b, n, d)
    h = _L0_tok_ref(x, L0_tok_w0, L0_tok_s0, L0_tok_b0, L0_tok_wdw, L0_tok_sdw, L0_tok_bdw, L0_tok_wpw, L0_tok_spw, L0_tok_bpw, L0_tok_w1, L0_tok_s1, L0_tok_b1, L0_tok_w2, L0_tok_s2, L0_tok_b2, L0_tok_w3, L0_tok_s3, L0_tok_b3)
    h = jnp.concatenate([jnp.broadcast_to(cls_tok, (h.shape[0], 1, h.shape[2])), h], axis=1)
    h = h + _L0_attn_ref(_layernorm(h, axis=-1), L0_attn_w1, L0_attn_b1, L0_attn_w2, L0_attn_b2, L0_attn_w3, L0_attn_b3, L0_attn_freq, L0_attn_deltas_abs, L0_attn_bias)
    h = h + _L0_ffn_ref(_layernorm(h, axis=-1), L0_ffn_ln1_g, L0_ffn_ln1_b, L0_ffn_qkv_w, L0_ffn_proj_w, L0_ffn_proj_b, L0_ffn_ln2_g, L0_ffn_ln2_b, L0_ffn_gate_w, L0_ffn_gate_b, L0_ffn_w1, L0_ffn_b1, L0_ffn_w2, L0_ffn_b2)
    return h

_drawn_inputs = setup_inputs


def setup_inputs(seed=0):
    import zlib

    import numpy as np

    out = dict(_drawn_inputs(seed))
    spreads = {'L0_tok_s0': (1.0, 0.2),
     'L0_tok_b0': (0.0, 0.1),
     'L0_tok_sdw': (1.0, 0.6),
     'L0_tok_bdw': (0.0, 0.68),
     'L0_tok_spw': (1.0, 0.6),
     'L0_tok_bpw': (0.0, 0.1),
     'L0_tok_s1': (1.0, 0.2),
     'L0_tok_b1': (0.0, 0.1),
     'L0_tok_s2': (1.0, 0.2),
     'L0_tok_b2': (0.0, 0.1),
     'L0_tok_s3': (1.0, 0.2),
     'L0_tok_b3': (0.0, 0.1),
     'L0_attn_freq': (1.0, 0.6),
     'L0_ffn_ln1_g': (1.0, 0.6),
     'L0_ffn_ln1_b': (0.0, 0.8),
     'L0_ffn_proj_b': (0.0, 0.1),
     'L0_ffn_ln2_g': (1.0, 0.6),
     'L0_ffn_ln2_b': (0.0, 0.8),
     'L0_ffn_gate_b': (0.0, 0.301),
     'L0_ffn_b1': (0.0, 0.758),
     'L0_ffn_b2': (0.0, 0.1)}
    factors = {'L0_attn_w1': 2.845,
     'L0_attn_b1': 23.737,
     'L0_attn_b2': 8.0,
     'L0_attn_w3': 3.165,
     'L0_attn_b3': 32.996,
     'L0_attn_deltas_abs': 27.992,
     'L0_attn_w2': 3.091}
    for name, (base, spread) in spreads.items():
        noise = np.random.default_rng([zlib.crc32(name.encode()), seed]).standard_normal(out[name].shape)
        drawn = base * np.exp(spread * noise) if base else spread * noise
        out[name] = jnp.asarray(drawn.astype(out[name].dtype))
    for name, factor in factors.items():
        out[name] = (out[name] * factor).astype(out[name].dtype)
    return out
```

```python
import numpy as np
import concourse.bass as bass
from concourse import mybir
from contextlib import ExitStack

F32 = mybir.dt.float32
U32 = mybir.dt.uint32
ALU = mybir.AluOpType
ACT = mybir.ActivationFunctionType
AX = mybir.AxisListType

B = 32
CI, C1, C2, D = 3, 12, 48, 192
G = 7
RS = 16
HW = RS // 2
NT = 2 * G
KX = 3 * (HW + 4) * CI
MA = C1 * (HW + 2)
MI = C1 * HW
N = B * RS
WR = 4 * MI + 4
TOK = G * G + 1
P2 = 64
PR = P2 + TOK
PT = 2 * TOK
NP = B // 2
DC = D // 2
NH, HD = 12, 16
HH = NH // 2
HID, NE = 768, 8
FC = HID // 128
TG = 4
GT = NP // TG
GN = GT * PT
KL = 2 * TOK
EPS = 1e-5
MAGIC = 12582912.0
TWO_PI_HI = 6.28125
TWO_PI_LO = 2 * np.pi - 6.28125
PI_MAX = 3.1415925

PK = dict(w0=(0, MA), w1=(120, 4 * 96), w2=(504, 2 * C2), w3=(600, 2 * D), eye=(984, 128), v=(1112, 12))
PKW = 1124
QK = dict(qkv=(0, 2 * 3 * D), pw=(1152, 2 * D), gate=(1536, 2 * NE), ln=(1552, 8), mask=(1560, HH),
          k3=(1566, 6), t=(1572, TOK), w3=(1622, D), f=(1814, 85))
QKW = 1899
HV = HD + 1


def tower(nc, xh, wreg, pack, qpack, rows, ew1, ew2, cls, s3, b3, iota, kd, td, hd, rd, out):
    ctx = ExitStack()
    with ctx:
        def sb(name, shape, dt=F32):
            return ctx.enter_context(nc.sbuf_tensor(name, shape, dt))

        def sem(name):
            return ctx.enter_context(nc.semaphore(name))

        pk = sb("pk", [128, PKW])
        qk = sb("qk", [96, QKW])
        row = sb("row", [1, D + NE + 128])
        b2e = sb("b2e", [NE, D])
        s3bc = sb("s3bc", [128, D])
        b3bc = sb("b3bc", [128, D])
        iot = sb("iot", [128, NE])
        xin_hT = sb("xin_hT", [128, G * 2 * N])
        wr_w2 = sb("wr_w2", [128, G * WR])
        A_w1 = sb("A_w1", [128, G * B * (RS + 2)])
        xin = xin_hT[0:KX, :].rearrange("p (g s n) -> p g s n", g=G, s=2)
        wr = wr_w2[0:MA, :].rearrange("p (g n) -> p g n", g=G)
        A = A_w1[0:MA, :].rearrange("p (g b r) -> p g b r", g=G, b=B)
        Bt = sb("Bt", [MI, 2, N])
        Ct = sb("Ct", [MI, 2, N])
        Dt = sb("Dt", [MI, 2, B, RS])
        Et = sb("Et", [96, G, 2, B, 4])
        Ft = sb("Ft", [112, G, 2 * B])
        hs = sb("hs", [128, 2, D])
        fa = sb("fa", [16, 6, TOK])
        kp = sb("kp", [DC, 2, KL])
        kt = sb("kt", [DC, 2, 2, TOK])
        T_x2 = sb("T_x2", [PR, D * TOK])
        T = T_x2[:, :].rearrange("p (c t) -> p c t", c=D)
        x2T = T_x2[0:DC, 0:2 * NP * PT].rearrange("p (h n) -> p h n", h=2)
        acc = T_x2[0:PT, 2 * NP * PT:2 * NP * PT + NP * D].rearrange("p (i c) -> p i c", i=NP)
        H = sb("H", [PR, NP, D])
        U = sb("U", [PR, D, NP])
        X1 = sb("X1", [PR, NP, D])
        cT = X1[0:NE, 0:9, :].rearrange("e i c -> e (i c)")[:, 0:NP * PT].rearrange("e (i n) -> e i n", i=NP)
        st = sb("st", [PR, NP, 6])
        mv = sb("mv", [PR, NP, 2])
        va = sb("va", [PR, NP])
        rs = sb("rs", [PR, NP])
        nhalf = sb("nhalf", [PR, NP])
        z1 = sb("z1", [PR, D])
        xT = sb("xT", [DC, 2, PR])
        qT = sb("qT", [DC, 2, PR])
        kb = sb("kb", [DC, 2, HH, PR])
        V = sb("V", [PR, NP, NH, HV])
        mx = sb("mx", [PR, NH])
        Sc = xin_hT[0:PR, 2 * FC * GN:2 * FC * GN + NH * TOK].rearrange("p (h m) -> p h m", h=NH)
        ri = sb("ri", [PR, NH])
        Pb = sb("Pb", [PR, NH, PR])
        Pt = xin_hT[0:PR, 2 * FC * GN + NH * TOK:2 * FC * GN + NH * (TOK + PR)].rearrange("p (h m) -> p h m", h=NH)
        o1 = sb("o1", [PR, D])
        oT = sb("oT", [DC, 2, PR])
        x1 = sb("x1", [PR, D])
        st2 = sb("st2", [PR, 12])
        z2 = sb("z2", [PR, D])
        lg = sb("lg", [PT, NP, NE])
        m8 = sb("m8", [PT, NP, 8])
        i8 = sb("i8", [PT, NP, 8], U32)
        f8 = sb("f8", [PT, NP, 2])
        sc = sb("sc", [PT, NP, 4])
        oh = sb("oh", [PT, 2, NP, NE])
        cw = sb("cw", [PT, NP, NE])
        w1e = A_w1[0:DC, 0:4 * HID].rearrange("p (e k n) -> p e k n", e=2, k=2)
        w2e = wr_w2[:, 0:2 * (FC * D + FC)].rearrange("p (e n) -> p e n", e=2)
        hT = xin_hT[:, 0:2 * FC * GN].rearrange("p (s c n) -> p s c n", s=2, c=FC)
        ps = ctx.enter_context(nc.psum_tensor("ps", [128, 8, 512], F32))

        def pkc(name, r, a=0, b=None):
            o, w = PK[name]
            return pk[0:r, o + a:o + (w if b is None else b)]

        def qkc(name, a=0, b=None, r=96):
            o, w = QK[name]
            return qk[0:r, o + a:o + (w if b is None else b)]

        s_const = sem("s_const")
        s_cls = sem("s_cls")
        s_x = [sem(f"s_xin{g}") for g in range(G)]
        s_w = [sem(f"s_wreg{g}") for g in range(G)]
        s_init = sem("s_init")
        s_conv0, s_dw, s_pw, s_conv1, s_conv2, s_conv3 = (sem(n) for n in
            ("s_conv0", "s_dw", "s_pw", "s_conv1", "s_conv2", "s_conv3"))
        s_A, s_B, s_C, s_D, s_E, s_F = (sem(n) for n in ("s_A", "s_B", "s_C", "s_D", "s_E", "s_F"))
        s_hs = sem("s_hs")
        s_hd = sem("s_hd")
        s_fpe, s_fdve, s_fact = sem("s_fpe"), sem("s_fdve"), sem("s_fact")
        s_kd, s_td, s_T = sem("s_kd"), sem("s_td"), sem("s_T")
        s_H = sem("s_H")
        s_ch = sem("s_ch")
        s_U = sem("s_U")
        s_va, s_rs, s_pow = sem("s_va"), sem("s_rs"), sem("s_pow")
        s_lc, s_lcv = sem("s_lc"), sem("s_lcv")
        s_z, s_zT, s_xT = sem("s_z"), sem("s_zT"), sem("s_xT")
        s_k, s_v, s_q, s_kb, s_V = (sem(n) for n in ("s_k", "s_v", "s_q", "s_kb", "s_V"))
        s_S, s_mx, s_sub, s_exp = (sem(n) for n in ("s_S", "s_mx", "s_sub", "s_exp"))
        s_PT, s_Pt, s_O, s_ri, s_o1, s_OT, s_oT = (sem(n) for n in ("s_PT", "s_Pt", "s_O", "s_ri", "s_o1", "s_OT", "s_oT"))
        s_pj, s_x1, s_st, s_R, s_z2, s_z2T, s_x2T = (sem(n) for n in
            ("s_pj", "s_x1", "s_st", "s_R", "s_z2", "s_z2T", "s_x2T"))
        s_rd, s_rl = sem("s_rd"), sem("s_rl")
        s_lg, s_lgc, s_d21, s_cwe, s_cw, s_ct, s_cT, s_b2 = (sem(n) for n in
            ("s_lg", "s_lgc", "s_d21", "s_cwe", "s_cw", "s_ct", "s_cT", "s_b2"))
        s_acc0 = sem("s_acc0")
        s_we = [sem(f"s_ew{e}") for e in range(2)]
        s_l1, s_h, s_l2, s_acc = sem("s_l1"), sem("s_h"), sem("s_l2"), sem("s_acc")
        s_out = sem("s_out")

        def stages(i):
            return [not isinstance(i, int) or 0 <= i - j < NP for j in range(5)]

        def step_value(step):
            return step[0] * (2 * TG) + step[1]

        def first(step):
            return isinstance(step[0], int) and step == (0, 0)

        def we_count(step):
            return (step[0] + step[1] // (2 * TG) + 1) * 32

        block = ctx.enter_context(nc.Block())

        @block.sync
        def _(sp):
            def load_region(gy, it):
                r = it * G + gy
                sp.dma_start(xin[:, gy], xh[bass.ds(r, 1)].rearrange("o p (s n) -> (o p) s n", s=2)).then_inc(s_x[gy], 16)
                sp.dma_start(wr[:, gy], wreg[bass.ds(r, 1)].rearrange("o p n -> (o p) n")).then_inc(s_w[gy], 16)

            def store_tokens(it):
                sp.wait_ge(s_hs, it + 1)
                for g in range(G):
                    sp.dma_start(hd[:, bass.ds(it + 1 + g * G, 1), :],
                                 hs[32 * (g % 4):32 * (g % 4) + B, g // 4, :].rearrange("b (o c) -> b o c", o=1)
                                 ).then_inc(s_hd, 16)

            sp.dma_start(pk[:, :], pack).then_inc(s_const, 16)
            load_region(0, 0)
            sp.dma_start(qk[:, :], qpack).then_inc(s_const, 16)
            sp.dma_start(row[:, :], rows[0:1, :]).then_inc(s_const, 16)
            sp.dma_start(b2e[:, :], rows[1:1 + NE, 0:D]).then_inc(s_const, 16)
            sp.dma_start(s3bc[:, :], s3.to_broadcast([128, D])).then_inc(s_const, 16)
            sp.dma_start(b3bc[:, :], b3.to_broadcast([128, D])).then_inc(s_const, 16)
            sp.dma_start(iot[:, :], iota).then_inc(s_const, 16)
            for gy in range(1, G):
                load_region(gy, 0)
            sp.wait_ge(s_fdve, 15)
            sp.dma_start(kd.rearrange("(h c) l -> c h l", h=2), kp[:, :, :]).then_inc(s_kd, 16)
            sp.wait_ge(s_init, 2)
            for p in range(2):
                sp.dma_start(H[p * P2:p * P2 + 1, :, :], cls.to_broadcast([1, NP, D])).then_inc(s_cls, 16)
            with sp.Fori(0, G - 1) as it:
                for gy in range(G):
                    sp.wait_ge(s_D, it * NT + 2 * gy + 2)
                    if gy == G - 1:
                        store_tokens(it)
                        sp.wait_ge(s_hd, (it + 1) * 16 * G)
                    load_region(gy, it + 1)
            store_tokens(G - 1)
            sp.wait_ge(s_D, G * NT)
            for e in range(2):
                sp.dma_start(w1e[:, e], ew1[e].rearrange("p (k n) -> p k n", k=2)).then_inc(s_we[e], 16)
                sp.dma_start(w2e[:, e], ew2[e]).then_inc(s_we[e], 16)
            sp.wait_ge(s_hd, 16 * G * G)
            sp.wait_ge(s_cls, 32)
            hv = hd.rearrange("(i q) t c -> q t i c", q=2)
            for p in range(2):
                sp.dma_start(H[p * P2 + 1:p * P2 + TOK, :, :], hv[p, 1:TOK]).then_inc(s_H, 16)
            sp.wait_ge(s_R, NP)
            rv = rd.rearrange("(i q) t c -> q t i c", q=2)
            for p in range(2):
                sp.dma_start(rv[p], H[p * P2:p * P2 + TOK, :, :]).then_inc(s_rd, 16)
            sp.wait_ge(s_rd, 32)
            sp.dma_start(acc[:, :, :], rd.rearrange("(i q) t c -> (q t) i c", q=2)).then_inc(s_rl, 16)
            with sp.Fori(0, NE // 2 - 1) as ep:
                for e in range(2):
                    sp.wait_ge(s_l1, (ep * 2 + e + 1) * TG * FC)
                    sp.dma_start(w1e[:, e], ew1[bass.ds(ep * 2 + 2 + e, 1)].rearrange("o p (k n) -> (o p) k n", k=2)).then_inc(s_we[e], 16)
                    sp.wait_ge(s_l2, (ep * 2 + e + 1) * NP)
                    sp.dma_start(w2e[:, e], ew2[bass.ds(ep * 2 + 2 + e, 1)].rearrange("o p n -> (o p) n")).then_inc(s_we[e], 16)
            sp.wait_ge(s_acc, NE * NP)
            sp.dma_start(out.rearrange("(i q) t c -> (q t) i c", q=2), acc[:, :, :]).then_inc(s_out, 16)
            sp.wait_ge(s_out, 16)

        @block.tensor
        def _(pe):
            mm = nc.tensor.matmul

            def conv0(k, it):
                t = it * NT + k
                gy, half = k % NT // 2, k % 2
                if half == 0:
                    pe.wait_ge(s_x[gy], (it + k // NT + 1) * 16)
                if k >= 2:
                    pe.wait_ge(s_A, t - 1)
                mm(ps[0:MA, k % 2, 0:N], pkc("w0", KX), xin[:, gy, half, :], start=True, stop=True).then_inc(s_conv0, 1)

            def depthwise(k, it):
                t = it * NT + k
                gy = k % NT // 2
                if k % 2 == 0:
                    pe.wait_ge(s_w[gy], (it + k // NT + 1) * 16)
                pe.wait_ge(s_A, t + 1)
                if k >= 2:
                    pe.wait_ge(s_B, t - 1)
                for dy in range(3):
                    last = mm(ps[0:MI, 2 + k % 2, 0:N], wr[:, gy, dy * MI:(dy + 1) * MI],
                              A[:, k % G, :, dy:dy + RS], start=(dy == 0), stop=(dy == 2))
                last.then_inc(s_dw, 1)

            def pointwise(k, it):
                t = it * NT + k
                gy = k % NT // 2
                pe.wait_ge(s_B, t + 1)
                if k >= 1:
                    pe.wait_ge(s_C, t)
                mm(ps[0:MI, 4, 0:N], wr[0:MI, gy, 3 * MI:4 * MI], Bt[:, k % 2, :],
                   start=True, stop=True).then_inc(s_pw, 1)

            def conv1(k, it):
                t = it * NT + k
                gy, half = k // 2, k % 2
                pe.wait_ge(s_D, t + 1)
                if half == 0 and gy >= 2:
                    pe.wait_ge(s_E, it * G + gy - 1)
                for dy in range(4):
                    last = mm(ps[0:96, 5 + gy % 2, half * 128:half * 128 + 128], pkc("w1", MI, dy * 96, dy * 96 + 96),
                              Dt[:, k % 2, :, dy:RS:4], start=(dy == 0), stop=(dy == 3))
                if half:
                    last.then_inc(s_conv1, 1)

            def conv2(it):
                pe.wait_ge(s_E, (it + 1) * G)
                for half in range(2):
                    for dy in range(2):
                        last = mm(ps[64 * half:64 * half + C2, 7, 0:G * 64], pkc("w2", 96, dy * C2, dy * C2 + C2),
                                  Et[:, :, half].rearrange("p g b (o d) -> p g (b o) d", d=2)[:, :, :, dy],
                                  start=(dy == 0), stop=(dy == 1))
                last.then_inc(s_conv2, 1)

            def conv3(it):
                pe.wait_ge(s_F, it + 1)
                for g, n in ((0, 4), (1, 3)):
                    for dy in range(2):
                        last = mm(ps[0:32 * n, 7, g * D:(g + 1) * D],
                                  Ft[:, 4 * g:4 * g + n, :].rearrange("p g (b d) -> p (g b) d", d=2)[:, :, dy],
                                  pkc("w3", 112, dy * D, dy * D + D), start=(dy == 0), stop=(dy == 1))
                last.then_inc(s_conv3, 1)

            pe.wait_ge(s_const, 16 * 7)
            mm(ps[0:16, 7, 0:TOK], qkc("f", 0, 16, 3), qkc("f", 16, 16 + TOK, 3), start=True, stop=True).then_inc(s_fpe, 1)
            pe.wait_ge(s_fact, 1)
            mm(ps[0:16, 7, 64:64 + TOK], qkc("f", 66, 82, 16), fa[:, 5, :], start=True, stop=True).then_inc(s_fpe, 1)
            pe.wait_ge(s_fact, 2)
            for h in range(2):
                last = mm(ps[0:DC, 7, 128 + 64 * h:128 + 64 * h + TOK], qkc("w3", h * DC, h * DC + DC, 16), fa[:, 4, :],
                          start=True, stop=True)
            last.then_inc(s_fpe, 1)
            pe.wait_ge(s_init, 2)
            conv0(0, 0)
            conv0(1, 0)
            depthwise(0, 0)
            conv0(2, 0)
            depthwise(1, 0)
            pointwise(0, 0)
            pe.wait_ge(s_fdve, 15)

            def column(it, last):
                for k in range(NT):
                    more = [k + j < NT or not last for j in range(4)]
                    if k < NT - 1:
                        if more[3]:
                            conv0(k + 3, it)
                        if more[2]:
                            depthwise(k + 2, it)
                        if more[1]:
                            pointwise(k + 1, it)
                        conv1(k, it)
                    else:
                        conv1(k, it)
                        if not last:
                            conv0(k + 3, it)
                        conv2(it)
                        if not last:
                            depthwise(k + 2, it)
                            pointwise(k + 1, it)
                        conv3(it)

            with pe.Fori(0, G - 1) as it:
                column(it, False)
            column(G - 1, True)

            pe.wait_ge(s_T, 32)
            pe.wait_ge(s_U, 1)
            pe.wait_ge(s_hs, G)
            for j in range(D // 32):
                for p in range(2):
                    n = 2 * j + p
                    if n >= 8:
                        pe.wait_ge(s_lcv, n - 7)
                    for c in range(32):
                        ch = j * 32 + c
                        last = mm(ps[p * P2:p * P2 + TOK, n % 8, c * NP:(c + 1) * NP], T[p * P2:p * P2 + TOK, ch, :],
                                  U[p * P2:p * P2 + TOK, ch, :], start=True, stop=True)
                    last.then_inc(s_lc, 1)
            pe.wait_ge(s_lcv, 12)

            eye = pkc("eye", PR, 0, PR)

            def scores(i):
                pe.wait_ge(s_q, i + 1)
                pe.wait_ge(s_kb, i + 1)
                for p, m in ((0, P2), (1, TOK)):
                    for h in range(2):
                        last = mm(ps[p * P2:p * P2 + m, 3 + h, 0:HH * TOK], qT[:, h, p * P2:p * P2 + m],
                                  kb[:, h, :, p * P2:p * P2 + TOK], start=True, stop=True)
                last.then_inc(s_S, 1)

            def z_transpose(i):
                pe.wait_ge(s_z, i + 1)
                for h in range(2):
                    last = nc.tensor.transpose(ps[0:DC, 0, h * PR:(h + 1) * PR], z1[:, h * DC:(h + 1) * DC], eye)
                last.then_inc(s_zT, 1)

            def p_transpose(i):
                pe.wait_ge(s_exp, i + 1)
                for b in range(3):
                    for h in range(4):
                        last = nc.tensor.transpose(ps[0:PR, 5 + b, h * PR:(h + 1) * PR], Pb[:, b * 4 + h, :], eye)
                    last.then_inc(s_PT, 1)

            def o_transpose(i):
                pe.wait_ge(s_o1, i + 1)
                for h in range(2):
                    last = nc.tensor.transpose(ps[0:DC, 2, h * PR:(h + 1) * PR], o1[:, h * DC:(h + 1) * DC], eye)
                last.then_inc(s_OT, 1)

            def project(c, bank, at):
                for h in range(2):
                    last = mm(ps[0:DC, bank, at:at + PR], qkc("qkv", h * 3 * D + c * DC, h * 3 * D + (c + 1) * DC),
                              xT[:, h, :], start=(h == 0), stop=(h == 1))
                return last

            def project_k(i):
                pe.wait_ge(s_xT, i + 1)
                project(2, 1, 0)
                project(3, 1, PR).then_inc(s_k, 1)

            def project_qv(i):
                project(0, 2, 0)
                project(1, 2, PR)
                for h in range(2):
                    last = mm(ps[0:PR, 2, 256:256 + D], xT[:, h, :], qkc("qkv", h * 3 * D + 2 * D, (h + 1) * 3 * D),
                              start=(h == 0), stop=(h == 1))
                last.then_inc(s_v, 1)

            def project_out(i):
                for h in range(2):
                    mm(ps[0:PR, 0, 0:D], oT[:, h, :], qkc("pw", h * D, (h + 1) * D), start=(h == 0), stop=False)
                mm(ps[0:PR, 0, 0:D], row[0:1, D + NE:D + NE + PR], row[0:1, 0:D], start=False, stop=True).then_inc(s_pj, 1)

            def attend(i):
                pe.wait_ge(s_V, i + 1)
                pe.wait_ge(s_Pt, 3 * i + 3)
                for h in range(NH):
                    last = mm(ps[0:PR, 5, h * HV:(h + 1) * HV], Pt[:, h, :],
                              V[:, bass.ds(i, 1), h, :].rearrange("p o d -> p (o d)"), start=True, stop=True)
                last.then_inc(s_O, 1)

            def z2_transpose(i):
                pe.wait_ge(s_z2, i + 1)
                for h in range(2):
                    last = nc.tensor.transpose(ps[0:DC, 1, h * PR:(h + 1) * PR], z2[:, h * DC:(h + 1) * DC], eye)
                last.then_inc(s_z2T, 1)

            def tile(i):
                a, b, c, d, e = stages(i)
                if b:
                    scores(i - 1)
                if a:
                    if e:
                        pe.wait_ge(s_x1, i - 3)
                    z_transpose(i)
                if c:
                    if d:
                        pe.wait_ge(s_o1, i - 2)
                    p_transpose(i - 2)
                if d:
                    if b:
                        pe.wait_ge(s_V, i)
                    o_transpose(i - 3)
                if a:
                    if b and e:
                        pe.wait_ge(s_x2T, i - 4)
                    project_k(i)
                if d:
                    pe.wait_ge(s_oT, i - 2)
                if a:
                    project_qv(i)
                if d:
                    if a:
                        pe.wait_ge(s_xT, i + 1)
                    else:
                        pe.wait_ge(s_x1, i - 3)
                    project_out(i - 3)
                if c:
                    attend(i - 2)
                if e:
                    if a:
                        pe.wait_ge(s_kb, i + 1)
                    else:
                        pe.wait_ge(s_x2T, i - 4)
                    z2_transpose(i - 4)

            for i in range(4):
                tile(i)
            with pe.Fori(4, NP) as i:
                tile(i)
            for i in range(NP, NP + 4):
                tile(i)

            pe.wait_ge(s_x2T, NP)
            for i in range(NP):
                o = ps[0:PT, 1, i * NE:(i + 1) * NE]
                for h in range(2):
                    mm(o, x2T[:, h, i * PT:(i + 1) * PT], qkc("gate", h * NE, (h + 1) * NE), start=(h == 0), stop=False)
                last = mm(o, row[0:1, D + NE:D + NE + PT], row[0:1, D:D + NE], start=False, stop=True)
            last.then_inc(s_lg, 1)

            def layer1(e, g, step):
                if g == 0:
                    pe.wait_ge(s_we[e], we_count(step))
                for c in range(FC):
                    n = step_value(step) * FC + c
                    if not first(step) or c >= 4:
                        pe.wait_ge(s_h, n - 3)
                    b = (step[1] * FC + c) % 4
                    for h in range(2):
                        last = mm(ps[:, b, 0:GN], w1e[:, e, h, c * 128:(c + 1) * 128],
                                  x2T[:, h, g * GN:(g + 1) * GN], start=(h == 0), stop=(h == 1))
                    last.then_inc(s_l1, 1)

            def layer2(e, g, step):
                n = step_value(step)
                pe.wait_ge(s_h, n * FC + FC)
                for j in range(GT):
                    b = 4 + j
                    if not first(step):
                        pe.wait_ge(s_acc, n * GT + j - (GT - 1))
                    for c in range(FC):
                        last = mm(ps[0:PT, b, 0:D], hT[:, step[1] % 2, c, j * PT:(j + 1) * PT],
                                  w2e[:, e, c * D:(c + 1) * D], start=(c == 0), stop=(c == FC - 1))
                    last.then_inc(s_l2, 1)

            pe.wait_ge(s_lgc, 1)
            layer1(0, 0, (0, 0))
            pe.wait_ge(s_cw, 1)
            for i in range(NP):
                nc.tensor.transpose(ps[0:NE, 4 + i // 4, (i % 4) * PT:(i % 4 + 1) * PT], cw[:, i, :], pkc("eye", PT, 0, PT)
                                    ).then_inc(s_ct, 1)
            for i in range(NP):
                pe.wait_ge(s_cT, 4)
                if i >= 4:
                    pe.wait_ge(s_b2, i - 3)
                mm(ps[0:PT, 4 + i % 4, 0:D], cT[:, i, :], b2e[:, :], start=True, stop=True).then_inc(s_acc0, 1)

            def experts(ep, last):
                for s in range(2 * TG):
                    n = s + 1
                    if not (last and n == 2 * TG):
                        layer1(n // TG % 2, n % TG, (ep, n))
                    if s == 0 and isinstance(ep, int) and ep == 0:
                        pe.wait_ge(s_b2, NP)
                    layer2(s // TG, s % TG, (ep, s))

            experts(0, False)
            with pe.Fori(1, NE // 2 - 1) as ep:
                experts(ep, False)
            experts(NE // 2 - 1, True)

        @block.scalar
        def _(act):
            fn = nc.scalar.activation

            def gelu_conv0(k, it):
                half = k % 2
                act.wait_ge(s_conv0, it * NT + k + 1)
                fn(A[:, k % G, :, 1:1 + RS], ps[0:MA, k % 2, 0:N].rearrange("p (b r) -> p b r", b=B), ACT.Gelu,
                   scale=pkc("v", MA, 2 * half, 2 * half + 1), bias=pkc("v", MA, 2 * half + 1, 2 * half + 2)).then_inc(s_A, 1)

            def gelu_dw(k, it):
                gy = k % NT // 2
                act.wait_ge(s_dw, it * NT + k + 1)
                fn(Bt[:, k % 2, :], ps[0:MI, 2 + k % 2, 0:N], ACT.Gelu, scale=wr[0:MI, gy, 4 * MI:4 * MI + 1],
                   bias=wr[0:MI, gy, 4 * MI + 1:4 * MI + 2]).then_inc(s_B, 1)

            def gelu_region(k, it):
                gy = k % NT // 2
                act.wait_ge(s_C, it * NT + k + 1)
                fn(Dt[:, k % 2], Ct[:, k % 2, :].rearrange("p (b r) -> p b r", b=B), ACT.Gelu,
                   bias=wr[0:MI, gy, 4 * MI + 3:4 * MI + 4]).then_inc(s_D, 1)

            def gelu_conv1(gy, it):
                act.wait_ge(s_conv1, it * G + gy + 1)
                fn(Et[:, gy], ps[0:96, 5 + gy % 2, 0:256].rearrange("p (s b o) -> p s b o", s=2, b=B), ACT.Gelu,
                   scale=pkc("v", 96, 4, 5), bias=pkc("v", 96, 5, 6)).then_inc(s_E, 1)

            def gelu_conv2(it):
                act.wait_ge(s_conv2, it + 1)
                for half in range(2):
                    p = slice(64 * half, 64 * half + C2)
                    last = fn(Ft[p, :, :], ps[p, 7, 0:G * 64].rearrange("p (g n) -> p g n", g=G), ACT.Gelu,
                              scale=pk[p, PK["v"][0] + 6:PK["v"][0] + 7], bias=pk[p, PK["v"][0] + 7:PK["v"][0] + 8])
                last.then_inc(s_F, 1)

            act.wait_ge(s_fdve, 6)
            fn(fa[:, 5, :], fa[:, 3, :], ACT.Sin).then_inc(s_fact, 1)
            act.wait_ge(s_fdve, 12)
            fn(fa[:, 4, :], fa[:, 3, :], ACT.Sin).then_inc(s_fact, 1)
            for h in range(2):
                last = fn(kt[:, 1, h, :], qkc("t"), ACT.Exp, scale=kt[:, 0, 0, h:h + 1])
            last.then_inc(s_fact, 1)
            gelu_conv0(0, 0)
            gelu_conv0(1, 0)
            gelu_dw(0, 0)
            gelu_conv0(2, 0)
            gelu_dw(1, 0)
            gelu_region(0, 0)

            def column(it, last):
                for k in range(NT):
                    more = [k + j < NT or not last for j in range(4)]
                    if k == NT - 1:
                        gelu_conv1(G - 1, it)
                    if more[3]:
                        gelu_conv0(k + 3, it)
                    if k == NT - 1:
                        gelu_conv2(it)
                    if more[2]:
                        gelu_dw(k + 2, it)
                    if more[1]:
                        gelu_region(k + 1, it)
                    if k % 2 and k < NT - 1:
                        gelu_conv1(k // 2, it)

            with act.Fori(0, G - 1) as it:
                column(it, False)
            column(G - 1, True)

            def xT_copy(i):
                act.wait_ge(s_zT, i + 1)
                for h in range(2):
                    last = fn(xT[:, h, :], ps[0:DC, 0, h * PR:(h + 1) * PR], ACT.Identity,
                              scale=qkc("ln", h, h + 1), bias=qkc("ln", 2 + h, 3 + h))
                last.then_inc(s_xT, 1)

            def pt_copy(i):
                for b in range(3):
                    act.wait_ge(s_PT, 3 * i + b + 1)
                    fn(Pt[:, b * 4:b * 4 + 4, :], ps[0:PR, 5 + b, 0:4 * PR].rearrange("p (h n) -> p h n", h=4),
                       ACT.Copy).then_inc(s_Pt, 1)

            def oT_copy(i):
                act.wait_ge(s_OT, i + 1)
                fn(oT[:, :, :], ps[0:DC, 2, 0:2 * PR].rearrange("p (h n) -> p h n", h=2), ACT.Copy).then_inc(s_oT, 1)

            def q_copy(i):
                act.wait_ge(s_v, i + 1)
                if not (isinstance(i, int) and i == 0):
                    act.wait_ge(s_S, i)
                fn(qT[:, :, :], ps[0:DC, 2, 0:2 * PR].rearrange("p (h n) -> p h n", h=2), ACT.Copy).then_inc(s_q, 1)

            def v_copy(i):
                fn(V[:, bass.ds(i, 1), :, 0:HD].rearrange("p o h d -> p (o h) d"),
                   ps[0:PR, 2, 256:256 + D].rearrange("p (h d) -> p h d", h=NH), ACT.Copy).then_inc(s_V, 1)

            def exps(i):
                act.wait_ge(s_sub, i + 1)
                for p in range(2):
                    r = slice(p * P2, p * P2 + TOK)
                    last = fn(Pb[r, :, r], Sc[r, :, :], ACT.Exp, scale=HD ** -0.5)
                last.then_inc(s_exp, 1)

            def x2T_copy(i):
                act.wait_ge(s_z2T, i + 1)
                for h in range(2):
                    src = ps[0:DC, 1, h * PR:h * PR + 2 * P2].rearrange("p (q t) -> p q t", q=2)[:, :, 0:TOK]
                    last = fn(x2T[:, h, bass.ds(i * PT, PT)].rearrange("p (q t) -> p q t", q=2), src, ACT.Identity,
                              scale=qkc("ln", 4 + h, 5 + h), bias=qkc("ln", 6 + h, 7 + h))
                last.then_inc(s_x2T, 1)

            def tile(i):
                a, b, c, d, e = stages(i)
                if a:
                    xT_copy(i)
                if c:
                    pt_copy(i - 2)
                if d:
                    oT_copy(i - 3)
                if a:
                    q_copy(i)
                    v_copy(i)
                if b:
                    exps(i - 1)
                if e:
                    x2T_copy(i - 4)

            for i in range(4):
                tile(i)
            with act.Fori(4, NP) as i:
                tile(i)
            for i in range(NP, NP + 4):
                tile(i)

            act.wait_ge(s_d21, 1)
            fn(sc[:, :, 1], sc[:, :, 0], ACT.Exp).then_inc(s_cwe, 1)

            def hidden(e, g, step):
                n = step[0] * (2 * TG) + step[1]
                for c in range(FC):
                    act.wait_ge(s_l1, n * FC + c + 1)
                    if c == 0 and not (isinstance(step[0], int) and step[0] == 0 and step[1] < 2):
                        act.wait_ge(s_l2, (n - 1) * GT)
                    fn(hT[:, step[1] % 2, c, :], ps[:, (step[1] * FC + c) % 4, 0:GN], ACT.Gelu,
                       bias=w2e[:, e, FC * D + c:FC * D + c + 1]).then_inc(s_h, 1)

            def experts(ep):
                for s in range(2 * TG):
                    hidden(s // TG, s % TG, (ep, s))

            experts(0)
            with act.Fori(1, NE // 2) as ep:
                experts(ep)

        @block.gpsimd
        def _(pool):
            pool.wait_ge(s_kd, 16)
            with pool.Fori(0, TOK) as s:
                pool.dma_start(td[bass.ds(s, 1)], kd[:, bass.ds(TOK - 1 - s, TOK)].rearrange("c (o t) -> o c t", o=1)
                               ).then_inc(s_td, 16)
            pool.wait_ge(s_td, 16 * TOK)
            for p in range(2):
                pool.dma_start(T[p * P2:p * P2 + TOK, :, :], td).then_inc(s_T, 16)
            pool.wait_ge(s_init, 2)
            for n in range(3):
                pool.wait_ge(s_va, n + 1)
                nc.gpsimd.tensor_tensor(rs[:, :], va[:, :], nhalf[:, :], ALU.pow).then_inc(s_rs, 1)
            with pool.Fori(0, NP) as i:
                pool.wait_ge(s_st, 3 * i + 3)
                nc.gpsimd.tensor_tensor(st2[:, 9:10], st2[:, 8:9], nhalf[:, 0:1], ALU.pow).then_inc(s_pow, 1)
                pool.wait_ge(s_x1, i + 1)
                nc.gpsimd.tensor_tensor(H[:, bass.ds(i, 1), :], H[:, bass.ds(i, 1), :],
                                        x1[:, :].unsqueeze(1), ALU.add).then_inc(s_R, 1)

        @block.vector
        def _(dve):
            ve = nc.vector
            chain = [0, 0]

            def link(ins):
                chain[1] += 1
                ins.then_inc(s_ch, 1)
                dve.wait_ge(s_ch, chain[0] + chain[1])

            ve.memset(A[:, :, :, 0:RS + 2:RS + 1], 0.0)
            ve.memset(Ft[:, :, :], 0.0)
            ve.memset(kp[:, :, :], 0.0)
            ve.memset(nhalf[:, :], -0.5)
            ve.memset(Pb[:, :, :], 0.0).then_inc(s_init, 1)
            dve.wait_ge(s_init, 1)
            ve.memset(Pb[P2 // 2:P2, :, 0:1], 1.0)
            ve.memset(V[:, :, :, HD:HV], 1.0)
            ve.memset(H[:, :, :], 0.0).then_inc(s_init, 1)
            dve.wait_ge(s_init, 2)
            dve.wait_ge(s_const, 16 * 7)
            for h in range(2):
                ve.tensor_scalar(kt[:, 0, 0, h:h + 1], qkc("k3", 2 + h, 3 + h), -1.0, None, ALU.mult)

            done = [0]

            def mark(ins):
                done[0] += 1
                ins.then_inc(s_fdve, 1)
                dve.wait_ge(s_fdve, done[0])

            for layer in range(2):
                dve.wait_ge(s_fpe, layer + 1)
                mark(ve.tensor_scalar(fa[:, 0, :], ps[0:16, 7, 64 * layer:64 * layer + TOK],
                                      qkc("f", 82 + 2 * layer, 83 + 2 * layer, 16),
                                      qkc("f", 83, 84, 16), ALU.add, ALU.mult))
                mark(ve.tensor_scalar(fa[:, 1, :], fa[:, 0, :], float(1 / (2 * np.pi)), MAGIC, ALU.mult, ALU.add))
                mark(ve.tensor_scalar(fa[:, 1, :], fa[:, 1, :], MAGIC, None, ALU.subtract))
                mark(ve.scalar_tensor_tensor(fa[:, 2, :], fa[:, 1, :], -TWO_PI_HI, fa[:, 0, :], ALU.mult, ALU.add))
                mark(ve.scalar_tensor_tensor(fa[:, 0, :], fa[:, 1, :], -TWO_PI_LO, fa[:, 2, :], ALU.mult, ALU.add))
                mark(ve.tensor_scalar(fa[:, 3, :], fa[:, 0, :], PI_MAX, -PI_MAX, ALU.min, ALU.max))
            dve.wait_ge(s_fpe, 3)
            dve.wait_ge(s_fact, 3)
            for h in range(2):
                last = ve.scalar_tensor_tensor(kp[:, h, TOK - 1:2 * TOK - 1], ps[0:DC, 7, 128 + 64 * h:128 + 64 * h + TOK],
                                               qkc("k3", h, h + 1), kt[:, 1, h, :], ALU.add, ALU.mult)
            mark(last)
            mark(ve.tensor_scalar(kp[:, :, :], kp[:, :, :], 1.0 / KL, None, ALU.mult))
            mark(ve.tensor_tensor(kp[:, :, TOK - 1:TOK], kp[:, :, TOK - 1:TOK],
                                  qkc("k3", 4, 6).unsqueeze(2), ALU.add))

            def add_input(k, it):
                dve.wait_ge(s_pw, it * NT + k + 1)
                gy = k % NT // 2
                ve.scalar_tensor_tensor(Ct[:, k % 2, :].rearrange("p (b r) -> p b r", b=B),
                                        ps[0:MI, 4, 0:N].rearrange("p (b r) -> p b r", b=B),
                                        wr[0:MI, gy, 4 * MI + 2:4 * MI + 3], A[0:MI, k % G, :, 1:1 + RS],
                                        ALU.mult, ALU.add).then_inc(s_C, 1)

            def tokens(it):
                dve.wait_ge(s_conv3, it + 1)
                for g, n in ((0, 128), (1, 96)):
                    last = ve.tensor_tensor(hs[0:n, g, :], ps[0:n, 7, g * D:(g + 1) * D], s3bc[0:n, :], ALU.mult)
                link(last)
                for g, n in ((0, 128), (1, 96)):
                    last = ve.tensor_tensor(hs[0:n, g, :], hs[0:n, g, :], b3bc[0:n, :], ALU.add)
                last.then_inc(s_hs, 1)

            def column(it, last):
                for k in range(NT):
                    if k + 1 < NT or not last:
                        add_input(k + 1, it)
                tokens(it)

            add_input(0, 0)
            with dve.Fori(0, G - 1) as it:
                chain[0], chain[1] = it, 0
                column(it, False)
            chain[0], chain[1] = G - 1, 0
            column(G - 1, True)
            chain[0], chain[1] = G, 0

            dve.wait_ge(s_H, 32)
            dve.wait_ge(s_cls, 32)
            for i in range(NP):
                last = ve.bn_stats(st[:, i, :], H[:, i, :])
            link(last)
            for i in range(NP):
                last = ve.bn_aggr(mv[:, i, :], st[:, i, :])
            link(last)
            ve.tensor_scalar(va[:, :], mv[:, :, 1], EPS, None, ALU.add).then_inc(s_va, 1)
            dve.wait_ge(s_rs, 1)
            for i in range(NP):
                last = ve.tensor_scalar(U[:, :, i], H[:, i, :], mv[:, i, 0:1], rs[:, i:i + 1], ALU.subtract, ALU.mult)
            last.then_inc(s_U, 1)
            for j in range(D // 32):
                for p in range(2):
                    n = 2 * j + p
                    dve.wait_ge(s_lc, n + 1)
                    r = slice(p * P2, p * P2 + TOK)
                    ve.tensor_tensor(H[r, :, j * 32:(j + 1) * 32], ps[r, n % 8, :].rearrange("p (c i) -> p i c", c=32),
                                     H[r, :, j * 32:(j + 1) * 32], ALU.add).then_inc(s_lcv, 1)
            dve.wait_ge(s_lcv, 12)
            for i in range(NP):
                last = ve.bn_stats(st[:, i, :], H[:, i, :])
            link(last)
            for i in range(NP):
                last = ve.bn_aggr(mv[:, i, :], st[:, i, :])
            link(last)
            ve.tensor_scalar(va[:, :], mv[:, :, 1], EPS, None, ALU.add).then_inc(s_va, 1)
            dve.wait_ge(s_rs, 2)
            for i in range(NP):
                last = ve.tensor_scalar(X1[:, i, :], H[:, i, :], mv[:, i, 0:1], rs[:, i:i + 1], ALU.subtract, ALU.mult)
            link(last)
            for i in range(NP):
                last = ve.bn_stats(st[:, i, :], X1[:, i, :])
            link(last)
            for i in range(NP):
                last = ve.bn_aggr(mv[:, i, :], st[:, i, :])
            link(last)
            ve.tensor_scalar(va[:, :], mv[:, :, 1], EPS, None, ALU.add).then_inc(s_va, 1)
            dve.wait_ge(s_rs, 3)

            def z_norm(i):
                if not (isinstance(i, int) and i == 0):
                    dve.wait_ge(s_zT, i)
                ve.tensor_scalar(z1[:, :].unsqueeze(1), X1[:, bass.ds(i, 1), :],
                                 mv[:, bass.ds(i, 1), 0:1].rearrange("p o n -> p (o n)"),
                                 rs[:, bass.ds(i, 1)], ALU.subtract, ALU.mult).then_inc(s_z, 1)

            def softmax_top(i):
                dve.wait_ge(s_S, i + 1)
                S = ps[0:PR, 3:5, 0:HH * TOK].rearrange("p h (k m) -> p h k m", k=HH)
                m = mx[:, :].rearrange("p (h k) -> p h k", h=2)
                ve.tensor_reduce(m, S, AX.X, ALU.max).then_inc(s_mx, 1)
                dve.wait_ge(s_mx, i + 1)
                if not (isinstance(i, int) and i == 0):
                    dve.wait_ge(s_exp, i)
                for h in range(2):
                    last = ve.tensor_tensor(Sc[:, h * HH:(h + 1) * HH, :], S[:, h],
                                            m[:, h].unsqueeze(2).to_broadcast([PR, HH, TOK]), ALU.subtract)
                last.then_inc(s_sub, 1)

            def k_blocks(i):
                dve.wait_ge(s_k, i + 1)
                for h in range(2):
                    last = ve.tensor_tensor(kb[:, h], ps[0:DC, 1, h * PR:(h + 1) * PR].unsqueeze(1).to_broadcast([DC, HH, PR]),
                                            qkc("mask").unsqueeze(2).to_broadcast([DC, HH, PR]), ALU.mult)
                last.then_inc(s_kb, 1)

            def o_norm(i):
                dve.wait_ge(s_O, i + 1)
                o = ps[0:PR, 5, 0:NH * HV].rearrange("p (h d) -> p h d", h=NH)
                ve.reciprocal(ri[:, :].unsqueeze(2), o[:, :, HD:HV]).then_inc(s_ri, 1)
                dve.wait_ge(s_ri, i + 1)
                if not (isinstance(i, int) and i == 0):
                    dve.wait_ge(s_OT, i)
                ve.tensor_tensor(o1[:, :].rearrange("p (h d) -> p h d", h=NH), o[:, :, 0:HD],
                                 ri[:, :].unsqueeze(2).to_broadcast([PR, NH, HD]), ALU.mult).then_inc(s_o1, 1)

            def add_attention(i):
                dve.wait_ge(s_pj, i + 1)
                if not (isinstance(i, int) and i == 0):
                    dve.wait_ge(s_R, i)
                ve.tensor_tensor(x1[:, :].unsqueeze(1), ps[0:PR, 0, 0:D].unsqueeze(1), X1[:, bass.ds(i, 1), :],
                                 ALU.add).then_inc(s_x1, 1)
                dve.wait_ge(s_x1, i + 1)
                ve.bn_stats(st2[:, 0:6], x1[:, :]).then_inc(s_st, 1)
                dve.wait_ge(s_st, 3 * i + 1)
                ve.memset(st2[:, 10:11], 0.0)
                ve.bn_aggr(st2[:, 6:8], st2[:, 0:6]).then_inc(s_st, 1)
                dve.wait_ge(s_st, 3 * i + 2)
                ve.tensor_scalar(st2[:, 8:9], st2[:, 7:8], EPS, None, ALU.add).then_inc(s_st, 1)
                dve.wait_ge(s_pow, i + 1)
                if not (isinstance(i, int) and i == 0):
                    dve.wait_ge(s_z2T, i)
                ve.tensor_scalar(z2[:, :], x1[:, :], st2[:, 6:7], st2[:, 9:10], ALU.subtract, ALU.mult).then_inc(s_z2, 1)

            def tile(i):
                a, b, c, d, e = stages(i)
                if a:
                    z_norm(i)
                if b:
                    softmax_top(i - 1)
                if a:
                    k_blocks(i)
                if d:
                    add_attention(i - 3)
                if c:
                    o_norm(i - 2)

            for i in range(4):
                tile(i)
            with dve.Fori(4, NP) as i:
                tile(i)
            for i in range(NP, NP + 4):
                tile(i)

            dve.wait_ge(s_lg, 1)
            ve.tensor_copy(lg[:, :, :], ps[0:PT, 1, 0:NP * NE].rearrange("p (i e) -> p i e", i=NP)).then_inc(s_lgc, 1)
            dve.wait_ge(s_lgc, 1)
            for i in range(NP):
                last = ve.max(m8[:, i, :], lg[:, i, :])
            link(last)
            ve.tensor_tensor(sc[:, :, 0], m8[:, :, 1], m8[:, :, 0], ALU.subtract).then_inc(s_d21, 1)
            for i in range(NP):
                last = ve.max_index(i8[:, i, :], m8[:, i, :], lg[:, i, :])
            link(last)
            link(ve.tensor_copy(f8[:, :, :], i8[:, :, 0:2]))
            for r in range(2):
                last = ve.tensor_tensor(oh[:, r], iot[0:PT, :].unsqueeze(1).to_broadcast([PT, NP, NE]),
                                        f8[:, :, r:r + 1].to_broadcast([PT, NP, NE]), ALU.is_equal)
            link(last)
            dve.wait_ge(s_cwe, 1)
            link(ve.tensor_scalar(sc[:, :, 0], sc[:, :, 1], 1.0, None, ALU.add))
            link(ve.reciprocal(sc[:, :, 2], sc[:, :, 0]))
            link(ve.tensor_tensor(sc[:, :, 3], sc[:, :, 1], sc[:, :, 2], ALU.mult))
            for r in range(2):
                last = ve.tensor_tensor(oh[:, r], oh[:, r], sc[:, :, 2 + r:3 + r].to_broadcast([PT, NP, NE]), ALU.mult)
            link(last)
            ve.tensor_tensor(cw[:, :, :], oh[:, 0], oh[:, 1], ALU.add).then_inc(s_cw, 1)
            dve.wait_ge(s_cw, 1)
            for q in range(4):
                dve.wait_ge(s_ct, 4 * q + 4)
                ve.tensor_copy(cT[:, 4 * q:4 * q + 4, :], ps[0:NE, 4 + q, 0:4 * PT].rearrange("p (i n) -> p i n", i=4)
                               ).then_inc(s_cT, 1)
            dve.wait_ge(s_rl, 16)
            for i in range(NP):
                dve.wait_ge(s_acc0, i + 1)
                ve.tensor_tensor(acc[:, i, :], ps[0:PT, 4 + i % 4, 0:D], acc[:, i, :], ALU.add).then_inc(s_b2, 1)
            dve.wait_ge(s_b2, NP)

            def experts(ep):
                for s in range(2 * TG):
                    for j in range(GT):
                        n = step_value((ep, s)) * GT + j
                        i = s % TG * GT + j
                        dve.wait_ge(s_l2, n + 1)
                        if not (isinstance(ep, int) and ep == 0 and s < TG):
                            dve.wait_ge(s_acc, n - NP + 1)
                        w = cw[:, i, bass.ds(ep * 2 + s // TG, 1)]
                        ve.scalar_tensor_tensor(acc[:, i, :], ps[0:PT, 4 + j, 0:D], w, acc[:, i, :],
                                                ALU.mult, ALU.add).then_inc(s_acc, 1)

            experts(0)
            with dve.Fori(1, NE // 2) as ep:
                experts(ep)


def lay_out(a):
    f = np.float32
    t = "L0_tok_"
    x = np.asarray(a["x"])
    xp = np.zeros((B, CI, G * RS + 2, G * RS + 4), f)
    xp[:, :, 1:-1, 2:-2] = x
    xh = np.zeros((G, G, 3, HW + 4, CI, 2, B, RS), f)
    for gx in range(G):
        for gy in range(G):
            for half in range(2):
                for dy in range(3):
                    c0 = RS * gx + HW * half
                    v = xp[:, :, RS * gy + dy:RS * gy + dy + RS, c0:c0 + HW + 4]
                    xh[gx, gy, dy, :, :, half] = v.transpose(3, 1, 0, 2)
    xh = xh.reshape(G * G, KX, 2 * N)

    def rowof(j, c):
        return c * HW + j - 1 if 1 <= j <= HW else MI + (C1 if j else 0) + c

    wdw = np.asarray(a[t + "wdw"]).reshape(G, G, C1, 3, 3)
    wpw = np.asarray(a[t + "wpw"]).reshape(G, G, C1, C1)
    wreg = np.zeros((G, G, MA, WR), f)
    for c in range(C1):
        for w in range(HW):
            for dy in range(3):
                for dx in range(3):
                    wreg[:, :, rowof(w + dx, c), dy * MI + c * HW + w] = wdw[:, :, c, dy, dx].T
            for co in range(C1):
                wreg[:, :, c * HW + w, 3 * MI + co * HW + w] = wpw[:, :, co, c].T
            for n, name in enumerate(("sdw", "bdw", "spw", "bpw")):
                wreg[:, :, c * HW + w, 4 * MI + n] = np.asarray(a[t + name]).reshape(G, G, C1)[:, :, c].T
    wreg = wreg.reshape(G * G, MA, WR)

    pack = np.zeros((128, PKW), f)
    w0, s0, b0 = (np.asarray(a[t + n]) for n in ("w0", "s0", "b0"))
    o = PK["w0"][0]
    v = PK["v"][0]
    for c in range(C1):
        for j in range(HW + 2):
            for dx in range(3):
                for dy in range(3):
                    for ci in range(CI):
                        pack[(dy * (HW + 4) + j + dx) * CI + ci, o + rowof(j, c)] = w0[c, ci, dy, dx]
            if j > 0:
                pack[rowof(j, c), v:v + 2] = s0[c], b0[c]
            if j <= HW:
                pack[rowof(j, c), v + 2:v + 4] = s0[c], b0[c]
    w1, w2, w3 = (np.asarray(a[t + n]) for n in ("w1", "w2", "w3"))
    for ox in range(2):
        for c in range(C1):
            for dx in range(4):
                for dy in range(4):
                    p = PK["w1"][0] + dy * 96 + ox * C2
                    pack[c * HW + ox * 4 + dx, p:p + C2] = w1[:, c, dy, dx]
        pack[ox * C2:ox * C2 + C2, v + 4] = np.asarray(a[t + "s1"])
        pack[ox * C2:ox * C2 + C2, v + 5] = np.asarray(a[t + "b1"])
        pack[ox * 64:ox * 64 + C2, v + 6] = np.asarray(a[t + "s2"])
        pack[ox * 64:ox * 64 + C2, v + 7] = np.asarray(a[t + "b2"])
        for dy in range(2):
            p = PK["w2"][0] + dy * C2
            pack[ox * C2:ox * C2 + C2, p:p + C2] = w2[:, :, dy, ox].T
            p = PK["w3"][0] + dy * D
            pack[ox * 64:ox * 64 + C2, p:p + D] = w3[:, :, dy, ox].T
    p = PK["eye"][0]
    pack[:, p:p + 128] = np.eye(128, dtype=f)

    qp = np.zeros((96, QKW), f)

    def put(name, v, at=0):
        v = np.asarray(v)
        o = QK[name][0] + at
        qp[0:v.shape[0], o:o + v.shape[1]] = v

    n, m = "L0_attn_", "L0_ffn_"
    for h in range(2):
        c = slice(h * DC, (h + 1) * DC)
        put("qkv", np.asarray(a[m + "qkv_w"]).T[c], h * 3 * D)
        put("pw", np.asarray(a[m + "proj_w"]).T[c], h * D)
        put("gate", np.asarray(a[m + "gate_w"]).T[c], h * NE)
        for k, name in enumerate(("ln1_g", "ln1_b", "ln2_g", "ln2_b")):
            put("ln", np.asarray(a[m + name])[c, None], 2 * k + h)
        for k, name in enumerate(("b3", "deltas_abs", "bias")):
            put("k3", np.asarray(a[n + name])[c, None], 2 * k + h)
    put("mask", np.kron(np.eye(HH, dtype=f), np.ones((HD, 1), f)))
    pos = np.linspace(0.0, 1.0, TOK, dtype=f)
    put("t", np.tile(pos, (DC, 1)))
    put("w3", np.asarray(a[n + "w3"]).T)
    ang = 1e-4 * (2.0 * np.pi * np.linspace(0.0, TOK - 1.0, TOK) / TOK)
    put("f", np.asarray(a[n + "w1"]).T, 0)
    put("f", np.stack([pos, np.cos(ang), -np.sin(ang)]).astype(f), 16)
    put("f", np.asarray(a[n + "w2"]).T, 66)
    for k, name in enumerate(("b1", "freq", "b2")):
        put("f", np.asarray(a[n + name])[:, None], 82 + k)

    rows = np.zeros((1 + NE, D + NE + 128), f)
    rows[0, 0:D] = np.asarray(a[m + "proj_b"])
    rows[0, D:D + NE] = np.asarray(a[m + "gate_b"])
    rows[0, D + NE:] = 1.0
    rows[1:, 0:D] = np.asarray(a[m + "b2"])

    ew1 = np.asarray(a[m + "w1"]).reshape(NE, HID, 2, DC).transpose(0, 3, 2, 1).reshape(NE, DC, 2 * HID)
    w2e = np.asarray(a[m + "w2"]).reshape(NE, D, FC, 128).transpose(0, 3, 2, 1).reshape(NE, 128, FC * D)
    b1e = np.asarray(a[m + "b1"]).reshape(NE, FC, 128).transpose(0, 2, 1)
    ew2 = np.concatenate([w2e, b1e], axis=2)
    return dict(xh=xh, wreg=wreg, pack=pack, qpack=qp, rows=rows, ew1=ew1, ew2=ew2,
                cls=np.asarray(a["cls_tok"]).reshape(1, 1, D), s3=np.asarray(a[t + "s3"]).reshape(1, D),
                b3=np.asarray(a[t + "b3"]).reshape(1, D), iota=np.tile(np.arange(NE, dtype=f), (128, 1)))


def kernel(**inputs):
    import concourse.bacc as bacc
    from concourse.bass_utils import run_bass_kernel_spmd

    nc = bacc.Bacc("TRN2", target_bir_lowering=False, num_devices=1)
    arrays, args = {}, []
    for name, v in lay_out(inputs).items():
        v = np.ascontiguousarray(v)
        arrays["in_" + name] = v
        args.append(nc.dram_tensor("in_" + name, v.shape, mybir.dt.from_np(v.dtype), kind="ExternalInput").ap())
    for name, shape in (("kd", (D, KL)), ("td", (TOK, D, TOK)), ("hd", (B, TOK, D)), ("rd", (B, TOK, D))):
        args.append(nc.dram_tensor(name, shape, F32, kind="Internal").ap())
    args.append(nc.dram_tensor("out", (B, TOK, D), F32, kind="ExternalOutput").ap())
    tower(nc, *args)
    return run_bass_kernel_spmd(nc, [arrays], core_ids=[0]).results[0]["out"]
```

```python
import numpy as np
import concourse.bass as bass
from concourse import mybir
from contextlib import ExitStack

F32 = mybir.dt.float32
F32R = mybir.dt.float32r
U32 = mybir.dt.uint32
ALU = mybir.AluOpType
ACT = mybir.ActivationFunctionType
AX = mybir.AxisListType

B = 32
CI, C1, C2, D = 3, 12, 48, 192
G = 7
RS = 16
HW = RS // 2
NT = 2 * G
KX = 3 * (HW + 4) * CI
MA = C1 * (HW + 2)
MI = C1 * HW
N = B * RS
WR = 4 * MI + 4
TOK = G * G + 1
P2 = 64
PR = P2 + TOK
PT = 2 * TOK
NP = B // 2
DC = D // 2
NH, HD = 12, 16
HH = NH // 2
HID, NE = 768, 8
FC = HID // 128
TT = B * TOK // 128 + 1
TP = TT * 128
LAST = B * TOK - (TT - 1) * 128
GROUPS = [(t[0] * 128, min(len(t) * 128, B * TOK - t[0] * 128), t) for t in (range(0, 4), range(4, 7), range(7, 10), range(10, TT))]
NG = len(GROUPS)
LEAD = 3
KL = 2 * TOK
EPS = 1e-5
MAGIC = 12582912.0
TWO_PI_HI = 6.28125
TWO_PI_LO = 2 * np.pi - 6.28125
PI_MAX = 3.1415925

PK = dict(w0=(0, MA), w1=(120, 4 * 96), w2=(504, 2 * C2), w3=(600, 2 * D), eye=(984, 128), v=(1112, 12), g=(1124, 2 * NE))
PKW = 1140
QK = dict(qkv=(0, 2 * 3 * D), pw=(1152, 2 * D), gate=(1536, 2 * NE), ln=(1552, 8), mask=(1560, HH),
          k3=(1566, 6), t=(1572, TOK), w3=(1622, D), f=(1814, 85))
QKW = 1899
HV = HD + 1


def tower(nc, xtiles, wreg, pack, qpack, rows, ew1, ew2, cls, s3, b3, iota, kd, td, hd, rd, out):
    ctx = ExitStack()
    with ctx:
        def sb(name, shape, dt=F32):
            return ctx.enter_context(nc.sbuf_tensor(name, shape, dt))

        def sem(name):
            return ctx.enter_context(nc.semaphore(name))

        pk = sb("pk", [128, PKW])
        qk = sb("qk", [96, QKW])
        row = sb("row", [1, D + NE + 128])
        b2e = sb("b2e", [NE, D])
        s3bc = sb("s3bc", [128, D])
        b3bc = sb("b3bc", [128, D])
        iot = sb("iot", [128, NE])
        hs = sb("hs", [128, 2, D])
        nhalf = sb("nhalf", [PR, NP])
        junk = sb("junk", [1, 1])
        x1 = sb("x1", [PR, D])
        H = sb("H", [PR, NP, D])
        lg = sb("lg", [128, TT, NE])
        m8 = sb("m8", [128, TT, 8])
        i8 = sb("i8", [128, TT, 8], U32)
        f8 = sb("f8", [128, TT, 2])
        sc = sb("sc", [128, TT, 4])
        oh = sb("oh", [128, 2, TT, NE])
        cw = sb("cw", [128, TT, NE])
        b1s = sb("b1s", [128, 2, FC])
        with ExitStack() as now:
            T = now.enter_context(nc.sbuf_tensor("T", [PR, D, TOK], F32))
        xA = sb("xA", [128, TP])
        xB = sb("xB", [128, TP])
        acc = sb("acc", [128, TT, D])
        sb("rest_of_T", [128, D * TOK - 2 * TP - TT * D])
        with ExitStack() as now:
            def early(name, shape, dt=F32):
                return now.enter_context(nc.sbuf_tensor(name, shape, dt))

            xin = early("xin", [KX, G, 2, N])
            xh, xl = early("xh", [KX, 2, N], F32R), early("xl", [KX, 2, N], F32R)
            w0h, w0l = early("w0h", [KX, MA], F32R), early("w0l", [KX, MA], F32R)
            wr = early("wr", [MA, G, WR])
            wh, wl = early("wh", [MA, G, 4 * MI], F32R), early("wl", [MA, G, 4 * MI], F32R)
            A = early("A", [MA, G, B, RS + 2])
            Ah, Al = early("Ah", [MA, 2, B, RS + 2], F32R), early("Al", [MA, 2, B, RS + 2], F32R)
            Bt = early("Bt", [MI, 2, N])
            Bh, Bl = early("Bh", [MI, 2, N], F32R), early("Bl", [MI, 2, N], F32R)
            Ct = early("Ct", [MI, 2, N])
            Dt = early("Dt", [MI, 2, B, RS])
            Et = early("Et", [96, G, 2, B, 4])
            Ft = early("Ft", [112, G, 2 * B])
            fa = early("fa", [16, 6, TOK])
            kp = early("kp", [DC, 2, KL])
            kt = early("kt", [DC, 2, 2, TOK])
        w1f = sb("w1f", [128, 2, HID])
        w2f = sb("w2f", [128, FC * D + FC])
        w1h, w1l = sb("w1h", [128, 2, 2, HID], F32R), sb("w1l", [128, 2, 2, HID], F32R)
        w2s = sb("w2s", [128, 2, FC, 2, D], F32R)
        st = sb("st", [PR, NP, 6])
        mv = sb("mv", [PR, NP, 2])
        va = sb("va", [PR, NP])
        rs = sb("rs", [PR, NP])
        st2 = sb("st2", [PR, 12])
        mx = sb("mx", [PR, NH])
        ri = sb("ri", [PR, NH])
        with ExitStack() as now:
            def middle(name, shape):
                return now.enter_context(nc.sbuf_tensor(name, shape, F32))

            U = middle("U", [PR, D, NP])
            X1 = middle("X1", [PR, NP, D])
            z1 = middle("z1", [PR, D])
            xT = middle("xT", [DC, 2, PR])
            qT = middle("qT", [DC, 2, PR])
            kb = middle("kb", [DC, 2, HH, PR])
            V = middle("V", [PR, NP, NH, HV])
            Sc = middle("Sc", [PR, NH, TOK])
            Pb = middle("Pb", [PR, NH, PR])
            Pt = middle("Pt", [PR, NH, PR])
            o1 = middle("o1", [PR, D])
            oT = middle("oT", [DC, 2, PR])
            z2 = middle("z2", [PR, 256])
        hf = sb("hf", [128, 2, 512])
        hh, hl = sb("hh", [128, 2, FC, 512], F32R), sb("hl", [128, 2, FC, 512], F32R)
        cT = sb("cT", [NE, TP])
        xAh, xAl, xBs = (sb(n, [128, TP], F32R) for n in ("xAh", "xAl", "xBs"))
        ps = ctx.enter_context(nc.psum_tensor("ps", [128, 8, 512], F32))

        def pkc(name, r, a=0, b=None):
            o, w = PK[name]
            return pk[0:r, o + a:o + (w if b is None else b)]

        def qkc(name, a=0, b=None, r=96):
            o, w = QK[name]
            return qk[0:r, o + a:o + (w if b is None else b)]

        s_const = sem("s_const")
        s_cls = sem("s_cls")
        s_x = [sem(f"s_xin{g}") for g in range(G)]
        s_w = [sem(f"s_wreg{g}") for g in range(G)]
        s_init = sem("s_init")
        s_conv0, s_dw, s_pw, s_conv1, s_conv2, s_conv3 = (sem(n) for n in
            ("s_conv0", "s_dw", "s_pw", "s_conv1", "s_conv2", "s_conv3"))
        s_w0s, s_ws, s_xsp, s_Al, s_Bl, s_ph = (sem(n) for n in ("s_w0s", "s_ws", "s_xsp", "s_Al", "s_Bl", "s_ph"))
        s_A, s_B, s_C, s_D, s_E, s_F = (sem(n) for n in ("s_A", "s_B", "s_C", "s_D", "s_E", "s_F"))
        s_hs = sem("s_hs")
        s_hd = sem("s_hd")
        s_fpe, s_fdve, s_fact = sem("s_fpe"), sem("s_fdve"), sem("s_fact")
        s_kd, s_td, s_T = sem("s_kd"), sem("s_td"), sem("s_T")
        s_H = sem("s_H")
        s_ch = sem("s_ch")
        s_U = sem("s_U")
        s_kt = sem("s_kt")
        s_pb0, s_ph2 = sem("s_pb0"), sem("s_ph2")
        s_va, s_rs, s_pow = sem("s_va"), sem("s_rs"), sem("s_pow")
        s_lc, s_lcv = sem("s_lc"), sem("s_lcv")
        s_z, s_zT, s_xT = sem("s_z"), sem("s_zT"), sem("s_xT")
        s_k, s_v, s_q, s_kb, s_V = (sem(n) for n in ("s_k", "s_v", "s_q", "s_kb", "s_V"))
        s_S, s_mx, s_sub, s_exp = (sem(n) for n in ("s_S", "s_mx", "s_sub", "s_exp"))
        s_PT, s_Pt, s_O, s_ri, s_o1, s_OT, s_oT = (sem(n) for n in ("s_PT", "s_Pt", "s_O", "s_ri", "s_o1", "s_OT", "s_oT"))
        s_pj, s_x1, s_st, s_R, s_z2, s_z2T, s_x2T = (sem(n) for n in
            ("s_pj", "s_x1", "s_st", "s_R", "s_z2", "s_z2T", "s_x2T"))
        s_rd, s_rl = sem("s_rd"), sem("s_rl")
        s_lg, s_lgc, s_d21, s_cwe, s_cw, s_ct, s_cT, s_b2 = (sem(n) for n in
            ("s_lg", "s_lgc", "s_d21", "s_cwe", "s_cw", "s_ct", "s_cT", "s_b2"))
        s_acc0 = sem("s_acc0")
        s_wf, s_w1s, s_w2s = sem("s_wf"), sem("s_w1s"), sem("s_w2s")
        s_xs = sem("s_xs")
        s_l1, s_h, s_lo, s_l2, s_acc = sem("s_l1"), sem("s_h"), sem("s_lo"), sem("s_l2"), sem("s_acc")
        s_half = sem("s_half")
        s_out = sem("s_out")

        def stages(i):
            return [not isinstance(i, int) or 0 <= i - j < NP for j in range(5)]

        def chunks_before(step):
            return (step[0] * (2 * NG) + step[1]) * FC

        def tiles_before(step):
            return (step[0] * 2 + step[1] // NG) * TT + GROUPS[step[1] % NG][2][0]

        def expert_of(step):
            return step[0] * 2 + step[1] // NG

        def is_one(step, last):
            return isinstance(step[0], int) and step[0] == 0 and step[1] <= last

        block = ctx.enter_context(nc.Block())

        @block.sync
        def _(sp):
            def load_region(gy, it):
                r = it * G + gy
                sp.dma_start(xin[:, gy], xtiles[bass.ds(r, 1)].rearrange("o p (s n) -> (o p) s n", s=2)).then_inc(s_x[gy], 16)
                sp.dma_start(wr[:, gy], wreg[bass.ds(r, 1)].rearrange("o p n -> (o p) n")).then_inc(s_w[gy], 16)

            def store_tokens(it):
                sp.wait_ge(s_hs, it + 1)
                for g in range(G):
                    sp.dma_start(hd[:, bass.ds(it + 1 + g * G, 1), :],
                                 hs[32 * (g % 4):32 * (g % 4) + B, g // 4, :].rearrange("b (o c) -> b o c", o=1)
                                 ).then_inc(s_hd, 16)

            sp.dma_start(pk[:, :], pack).then_inc(s_const, 16)
            load_region(0, 0)
            sp.dma_start(qk[:, :], qpack).then_inc(s_const, 16)
            sp.dma_start(row[:, :], rows[0:1, :]).then_inc(s_const, 16)
            sp.dma_start(b2e[:, :], rows[1:1 + NE, 0:D]).then_inc(s_const, 16)
            sp.dma_start(s3bc[:, :], s3.to_broadcast([128, D])).then_inc(s_const, 16)
            sp.dma_start(b3bc[:, :], b3.to_broadcast([128, D])).then_inc(s_const, 16)
            sp.dma_start(iot[:, :], iota).then_inc(s_const, 16)
            for gy in range(1, G):
                load_region(gy, 0)
            sp.wait_ge(s_fdve, 15)
            sp.dma_start(kd.rearrange("(h c) l -> c h l", h=2), kp[:, :, :]).then_inc(s_kd, 16)
            sp.wait_ge(s_init, 1)
            for p in range(2):
                sp.dma_start(H[p * P2:p * P2 + 1, :, :], cls.to_broadcast([1, NP, D])).then_inc(s_cls, 16)

            def next_region(gy, it):
                sp.wait_ge(s_D, it * NT + 2 * gy + 2)
                load_region(gy, it + 1)

            for gy in range(2):
                next_region(gy, 0)
            with sp.Fori(0, G - 2) as it:
                for gy in range(2, G):
                    next_region(gy, it)
                next_region(0, it + 1)
                store_tokens(it)
                sp.wait_ge(s_D, (it + 1) * NT + 4)
                sp.wait_ge(s_hd, (it + 1) * 16 * G)
                load_region(1, it + 2)
            for gy in range(2, G):
                next_region(gy, G - 2)
            store_tokens(G - 2)
            store_tokens(G - 1)
            sp.wait_ge(s_hs, G)

            def load_expert(e):
                sp.dma_start(w1f[:, :, :], ew1[bass.ds(e, 1)].rearrange("o p (k n) -> (o p) k n", k=2)).then_inc(s_wf, 16)
                sp.dma_start(w2f[:, :], ew2[bass.ds(e, 1)].rearrange("o p n -> (o p) n")).then_inc(s_wf, 16)

            sp.wait_ge(s_hd, 16 * G * G)
            sp.wait_ge(s_cls, 32)
            hv = hd.rearrange("(i q) t c -> q t i c", q=2)
            for p in range(2):
                sp.dma_start(H[p * P2 + 1:p * P2 + TOK, :, :], hv[p, 1:TOK]).then_inc(s_H, 16)
            load_expert(0)
            sp.wait_ge(s_w2s, 1)
            load_expert(1)
            sp.wait_ge(s_R, NP)
            rv = rd.rearrange("(i q) t c -> q t i c", q=2)
            for p in range(2):
                sp.dma_start(rv[p], H[p * P2:p * P2 + TOK, :, :]).then_inc(s_rd, 16)
            sp.wait_ge(s_rd, 32)
            full = (TT - 1) * 128
            rf, of = rd.rearrange("b t c -> (b t) c"), out.rearrange("b t c -> (b t) c")
            sp.dma_start(acc[:, 0:TT - 1, :], rf[0:full].rearrange("(i p) c -> p i c", p=128)).then_inc(s_rl, 16)
            sp.dma_start(acc[0:LAST, TT - 1, :], rf[full:full + LAST]).then_inc(s_rl, 16)
            with sp.Fori(2, NE) as e:
                sp.wait_ge(s_w2s, e)
                load_expert(e)
            for n, (t0, nt, tiles) in enumerate(GROUPS):
                sp.wait_ge(s_acc, (NE - 1) * TT + tiles[-1] + 1)
                full = nt // 128
                sp.dma_start(of[t0:t0 + full * 128].rearrange("(i p) c -> p i c", p=128),
                             acc[:, tiles[0]:tiles[0] + full, :]).then_inc(s_out, 16)
            sp.dma_start(of[B * TOK - LAST:B * TOK], acc[0:LAST, TT - 1, :]).then_inc(s_out, 16)
            sp.wait_ge(s_out, 16 * (NG + 1))

        @block.tensor
        def _(pe):
            mm = nc.tensor.matmul

            def conv0(k, it):
                t = it * NT + k
                gy, half = k % NT // 2, k % 2
                pe.wait_ge(s_xsp, t + 1)
                if k >= 2:
                    pe.wait_ge(s_A, t - 1)
                o = ps[0:MA, k % 2, 0:N]
                mm(o, w0h[:, :], xh[:, k % 2, :], start=True, stop=False)
                mm(o, w0l[:, :], xh[:, k % 2, :], start=False, stop=False)
                mm(o, w0h[:, :], xl[:, k % 2, :], start=False, stop=True).then_inc(s_conv0, 1)

            def depthwise(k, it):
                t = it * NT + k
                gy = k % NT // 2
                if k % 2 == 0:
                    pe.wait_ge(s_ws, it * G + k // 2 + 1)
                pe.wait_ge(s_A, t + 1)
                if k >= 2:
                    pe.wait_ge(s_B, t - 1)
                o = ps[0:MI, 2 + k % 2, 0:N]
                for w in (wh, wl):
                    for dy in range(3):
                        mm(o, w[:, gy, dy * MI:(dy + 1) * MI], Ah[:, k % 2, :, dy:dy + RS],
                           start=(w is wh and dy == 0), stop=False)
                pe.wait_ge(s_Al, t + 1)
                for dy in range(3):
                    last = mm(o, wh[:, gy, dy * MI:(dy + 1) * MI], Al[:, k % 2, :, dy:dy + RS], start=False, stop=(dy == 2))
                last.then_inc(s_dw, 1)

            def pointwise(k, it):
                t = it * NT + k
                gy = k % NT // 2
                pe.wait_ge(s_B, t + 1)
                if k >= 1:
                    pe.wait_ge(s_C, t)
                o = ps[0:MI, 4, 0:N]
                mm(o, wh[0:MI, gy, 3 * MI:4 * MI], Bh[:, k % 2, :], start=True, stop=False)
                mm(o, wl[0:MI, gy, 3 * MI:4 * MI], Bh[:, k % 2, :], start=False, stop=False)
                pe.wait_ge(s_Bl, t + 1)
                mm(o, wh[0:MI, gy, 3 * MI:4 * MI], Bl[:, k % 2, :], start=False, stop=True).then_inc(s_pw, 1)

            def conv1(k, it):
                t = it * NT + k
                gy, half = k % NT // 2, k % 2
                pe.wait_ge(s_D, t + 1)
                if half == 0 and k >= 4:
                    pe.wait_ge(s_E, it * G + k // 2 - (1 if gy else 0))
                for dy in range(4):
                    last = mm(ps[0:96, 5 + gy % 2, half * 128:half * 128 + 128], pkc("w1", MI, dy * 96, dy * 96 + 96),
                              Dt[:, k % 2, :, dy:RS:4], start=(dy == 0), stop=(dy == 3))
                if half:
                    last.then_inc(s_conv1, 1)

            def conv2(it):
                pe.wait_ge(s_E, (it + 1) * G)
                for half in range(2):
                    for dy in range(2):
                        last = mm(ps[64 * half:64 * half + C2, 7, 0:G * 64], pkc("w2", 96, dy * C2, dy * C2 + C2),
                                  Et[:, :, half].rearrange("p g b (o d) -> p g (b o) d", d=2)[:, :, :, dy],
                                  start=(dy == 0), stop=(dy == 1))
                last.then_inc(s_conv2, 1)

            def conv3(it):
                pe.wait_ge(s_F, it + 1)
                for g, n in ((0, 4), (1, 3)):
                    for dy in range(2):
                        last = mm(ps[0:32 * n, 7, g * D:(g + 1) * D],
                                  Ft[:, 4 * g:4 * g + n, :].rearrange("p g (b d) -> p (g b) d", d=2)[:, :, dy],
                                  pkc("w3", 112, dy * D, dy * D + D), start=(dy == 0), stop=(dy == 1))
                last.then_inc(s_conv3, 1)

            pe.wait_ge(s_const, 16 * 7)
            mm(ps[0:16, 7, 0:TOK], qkc("f", 0, 16, 3), qkc("f", 16, 16 + TOK, 3), start=True, stop=True).then_inc(s_fpe, 1)
            pe.wait_ge(s_init, 1)
            pe.wait_ge(s_w0s, 2)
            conv0(0, 0)
            pe.wait_ge(s_fact, 1)
            mm(ps[0:16, 7, 64:64 + TOK], qkc("f", 66, 82, 16), fa[:, 5, :], start=True, stop=True).then_inc(s_fpe, 1)
            conv0(1, 0)
            depthwise(0, 0)
            conv0(2, 0)
            pe.wait_ge(s_fact, 2)
            for h in range(2):
                last = mm(ps[0:DC, 7, 128 + 64 * h:128 + 64 * h + TOK], qkc("w3", h * DC, h * DC + DC, 16), fa[:, 4, :],
                          start=True, stop=True)
            last.then_inc(s_fpe, 1)
            depthwise(1, 0)
            pointwise(0, 0)

            def slot(k, it, more=4):
                if more > 3:
                    conv0(k + 3, it)
                if more > 2:
                    depthwise(k + 2, it)
                if more > 1:
                    pointwise(k + 1, it)
                conv1(k, it)
                if k == NT:
                    conv2(it)
                if k == NT + 1:
                    conv3(it)

            for k in range(LEAD):
                slot(k, 0)
            with pe.Fori(0, G - 1) as it:
                for k in range(LEAD, NT + LEAD):
                    slot(k, it)
            for k in range(LEAD, NT):
                slot(k, G - 1, NT - k)
            conv2(G - 1)
            conv3(G - 1)

            pe.wait_ge(s_T, 32)
            pe.wait_ge(s_U, 1)
            pe.wait_ge(s_hs, G)
            for j in range(D // 32):
                for p in range(2):
                    n = 2 * j + p
                    if n >= 8:
                        pe.wait_ge(s_lcv, n - 7)
                    for c in range(32):
                        ch = j * 32 + c
                        last = mm(ps[p * P2:p * P2 + TOK, n % 8, c * NP:(c + 1) * NP], T[p * P2:p * P2 + TOK, ch, :],
                                  U[p * P2:p * P2 + TOK, ch, :], start=True, stop=True)
                    last.then_inc(s_lc, 1)
            pe.wait_ge(s_lcv, 12)

            eye = pkc("eye", PR, 0, PR)

            def scores(i):
                pe.wait_ge(s_q, i + 1)
                pe.wait_ge(s_kb, i + 1)
                for p, m in ((0, P2), (1, TOK)):
                    for h in range(2):
                        last = mm(ps[p * P2:p * P2 + m, 3 + h, 0:HH * TOK], qT[:, h, p * P2:p * P2 + m],
                                  kb[:, h, :, p * P2:p * P2 + TOK], start=True, stop=True)
                last.then_inc(s_S, 1)

            def z_transpose(i):
                pe.wait_ge(s_z, i + 1)
                for h in range(2):
                    last = nc.tensor.transpose(ps[0:DC, 0, h * PR:(h + 1) * PR], z1[:, h * DC:(h + 1) * DC], eye)
                last.then_inc(s_zT, 1)

            def p_transpose(i):
                pe.wait_ge(s_exp, i + 1)
                for b in range(3):
                    for h in range(4):
                        last = nc.tensor.transpose(ps[0:PR, 5 + b, h * PR:(h + 1) * PR], Pb[:, b * 4 + h, :], eye)
                    last.then_inc(s_PT, 1)

            def o_transpose(i):
                pe.wait_ge(s_o1, i + 1)
                for h in range(2):
                    last = nc.tensor.transpose(ps[0:DC, 2, h * PR:(h + 1) * PR], o1[:, h * DC:(h + 1) * DC], eye)
                last.then_inc(s_OT, 1)

            def project(c, bank, at):
                for h in range(2):
                    last = mm(ps[0:DC, bank, at:at + PR], qkc("qkv", h * 3 * D + c * DC, h * 3 * D + (c + 1) * DC),
                              xT[:, h, :], start=(h == 0), stop=(h == 1))
                return last

            def project_k(i):
                pe.wait_ge(s_xT, i + 1)
                project(2, 1, 0)
                project(3, 1, PR).then_inc(s_k, 1)

            def project_qv(i):
                project(0, 2, 0)
                project(1, 2, PR)
                for h in range(2):
                    last = mm(ps[0:PR, 2, 256:256 + D], xT[:, h, :], qkc("qkv", h * 3 * D + 2 * D, (h + 1) * 3 * D),
                              start=(h == 0), stop=(h == 1))
                last.then_inc(s_v, 1)

            def project_out(i):
                for h in range(2):
                    mm(ps[0:PR, 0, 0:D], oT[:, h, :], qkc("pw", h * D, (h + 1) * D), start=(h == 0), stop=False)
                mm(ps[0:PR, 0, 0:D], row[0:1, D + NE:D + NE + PR], row[0:1, 0:D], start=False, stop=True).then_inc(s_pj, 1)

            def attend(i):
                pe.wait_ge(s_V, i + 1)
                pe.wait_ge(s_Pt, 3 * i + 3)
                for h in range(NH):
                    last = mm(ps[0:PR, 5, h * HV:(h + 1) * HV], Pt[:, h, :],
                              V[:, bass.ds(i, 1), h, :].rearrange("p o d -> p (o d)"), start=True, stop=True)
                last.then_inc(s_O, 1)

            def z2_transpose(i):
                pe.wait_ge(s_z2, i + 1)
                for h in range(2):
                    last = nc.tensor.transpose(ps[:, 1, h * PR:(h + 1) * PR], z2[:, h * 128:(h + 1) * 128], eye)
                last.then_inc(s_z2T, 1)

            def tile(i):
                a, b, c, d, e = stages(i)
                if b:
                    scores(i - 1)
                if a:
                    if e:
                        pe.wait_ge(s_x1, i - 3)
                    z_transpose(i)
                if c:
                    if d:
                        pe.wait_ge(s_o1, i - 2)
                    p_transpose(i - 2)
                if d:
                    if b:
                        pe.wait_ge(s_V, i)
                    o_transpose(i - 3)
                if a:
                    if b and e:
                        pe.wait_ge(s_x2T, i - 4)
                    project_k(i)
                if d:
                    pe.wait_ge(s_oT, i - 2)
                if a:
                    project_qv(i)
                if d:
                    if a:
                        pe.wait_ge(s_xT, i + 1)
                    else:
                        pe.wait_ge(s_x1, i - 3)
                    project_out(i - 3)
                if c:
                    attend(i - 2)
                if e:
                    if a:
                        pe.wait_ge(s_kb, i + 1)
                    else:
                        pe.wait_ge(s_x2T, i - 4)
                    z2_transpose(i - 4)

            for i in range(4):
                tile(i)
            with pe.Fori(4, NP) as i:
                tile(i)
            for i in range(NP, NP + 4):
                tile(i)

            pe.wait_ge(s_x2T, NP)
            for i in range(TT):
                o = ps[:, 7, i * NE:(i + 1) * NE]
                mm(o, xA[:, i * 128:(i + 1) * 128], pkc("g", 128, 0, NE), start=True, stop=False)
                mm(o, xB[0:D - 128, i * 128:(i + 1) * 128], pkc("g", D - 128, NE, 2 * NE), start=False, stop=False)
                last = mm(o, row[0:1, D + NE:D + NE + 128], row[0:1, D:D + NE], start=False, stop=True)
            last.then_inc(s_lg, 1)

            def layer1(step):
                g, e = step[1] % NG, step[1] // NG % 2
                t0, nt, _ = GROUPS[g]
                if g == 0:
                    pe.wait_ge(s_w1s, expert_of(step) + 1)
                if is_one(step, NG - 1):
                    pe.wait_ge(s_xs, g + 1)
                c64 = D - 128
                for c in range(FC):
                    n = chunks_before(step) + c
                    if not (is_one(step, 0) and c < 4):
                        pe.wait_ge(s_h, n - 3)
                    o = ps[:, (step[1] * FC + c) % 4, 0:nt]
                    k = slice(c * 128, (c + 1) * 128)
                    x = slice(t0, t0 + nt)
                    mm(o, w1h[:, e, 0, k], xAh[:, x], start=True, stop=False)
                    mm(o, w1h[:, e, 0, k], xAl[:, x], start=False, stop=False)
                    mm(o, w1l[:, e, 0, k], xAh[:, x], start=False, stop=False)
                    mm(o, w1h[:, e, 1, k], xBs[:, x], start=False, stop=False)
                    mm(o, w1l[0:c64, e, 1, k], xBs[0:c64, x], start=False, stop=True).then_inc(s_l1, 1)

            def layer2(step):
                e = step[1] // NG
                _, nt, tiles = GROUPS[step[1] % NG]
                pe.wait_ge(s_w2s, expert_of(step) + 1)
                pe.wait_ge(s_lo, chunks_before(step) + FC)
                if not is_one(step, 0):
                    pe.wait_ge(s_acc, tiles_before(step))
                for j, i in enumerate(tiles):
                    p = 128 if i < TT - 1 else LAST
                    for c in range(FC):
                        t = slice(j * 128, j * 128 + p)
                        a, b = hh[:, step[1] % 2, c, t], hl[:, step[1] % 2, c, t]
                        mm(ps[0:p, 4 + j, 0:2 * D], a, w2s[:, e, c].rearrange("p s n -> p (s n)"),
                           start=(c == 0), stop=False, skip_group_check=True)
                        last = mm(ps[0:p, 4 + j, 0:D], b, w2s[:, e, c, 0], start=False, stop=(c == FC - 1),
                                  skip_group_check=True)
                    last.then_inc(s_l2, 1)

            layer1((0, 0))
            pe.wait_ge(s_cw, 1)
            for i in range(TT):
                nc.tensor.transpose(ps[0:NE, 4 + i // 4, (i % 4) * 128:(i % 4 + 1) * 128], cw[:, i, :], pkc("eye", 128)
                                    ).then_inc(s_ct, 1)
            pe.wait_ge(s_cT, 4)
            for i in range(TT):
                p = 128 if i < TT - 1 else LAST
                if i >= 4:
                    pe.wait_ge(s_b2, i - 3)
                mm(ps[0:p, 4 + i % 4, 0:D], cT[:, i * 128:i * 128 + p], b2e[:, :], start=True, stop=True).then_inc(s_acc0, 1)

            def experts(ep, last):
                for s in range(2 * NG):
                    if not (last and s + 1 == 2 * NG):
                        layer1((ep, s + 1))
                    if is_one((ep, s), 0):
                        pe.wait_ge(s_b2, TT)
                    layer2((ep, s))

            experts(0, False)
            with pe.Fori(1, NE // 2 - 1) as ep:
                experts(ep, False)
            experts(NE // 2 - 1, True)

        @block.scalar
        def _(act):
            fn = nc.scalar.activation

            def gelu_conv0(k, it):
                half = k % 2
                act.wait_ge(s_conv0, it * NT + k + 1)
                for o in (Ah[:, k % 2], A[:, k % G]):
                    last = fn(o[:, :, 1:1 + RS], ps[0:MA, k % 2, 0:N].rearrange("p (b r) -> p b r", b=B), ACT.Gelu,
                              scale=pkc("v", MA, 2 * half, 2 * half + 1), bias=pkc("v", MA, 2 * half + 1, 2 * half + 2))
                last.then_inc(s_A, 1)

            def gelu_dw(k, it):
                gy = k % NT // 2
                act.wait_ge(s_dw, it * NT + k + 1)
                for o in (Bh, Bt):
                    last = fn(o[:, k % 2, :], ps[0:MI, 2 + k % 2, 0:N], ACT.Gelu, scale=wr[0:MI, gy, 4 * MI:4 * MI + 1],
                              bias=wr[0:MI, gy, 4 * MI + 1:4 * MI + 2])
                last.then_inc(s_B, 1)

            def gelu_region(k, it):
                gy = k % NT // 2
                act.wait_ge(s_C, it * NT + k + 1)
                fn(Dt[:, k % 2], Ct[:, k % 2, :].rearrange("p (b r) -> p b r", b=B), ACT.Gelu,
                   bias=wr[0:MI, gy, 4 * MI + 3:4 * MI + 4]).then_inc(s_D, 1)

            def gelu_conv1(gy, it):
                act.wait_ge(s_conv1, it * G + gy + 1)
                fn(Et[:, gy % G], ps[0:96, 5 + gy % G % 2, 0:256].rearrange("p (s b o) -> p s b o", s=2, b=B), ACT.Gelu,
                   scale=pkc("v", 96, 4, 5), bias=pkc("v", 96, 5, 6)).then_inc(s_E, 1)

            def gelu_conv2(it):
                act.wait_ge(s_conv2, it + 1)
                for half in range(2):
                    p = slice(64 * half, 64 * half + C2)
                    last = fn(Ft[p, :, :], ps[p, 7, 0:G * 64].rearrange("p (g n) -> p g n", g=G), ACT.Gelu,
                              scale=pk[p, PK["v"][0] + 6:PK["v"][0] + 7], bias=pk[p, PK["v"][0] + 7:PK["v"][0] + 8])
                last.then_inc(s_F, 1)

            act.wait_ge(s_fdve, 6)
            fn(fa[:, 5, :], fa[:, 3, :], ACT.Sin).then_inc(s_fact, 1)
            gelu_conv0(0, 0)
            gelu_conv0(1, 0)
            act.wait_ge(s_fdve, 12)
            fn(fa[:, 4, :], fa[:, 3, :], ACT.Sin).then_inc(s_fact, 1)
            for h in range(2):
                last = fn(kt[:, 1, h, :], qkc("t"), ACT.Exp, scale=kt[:, 0, 0, h:h + 1])
            last.then_inc(s_fact, 1)
            gelu_dw(0, 0)
            gelu_conv0(2, 0)
            gelu_dw(1, 0)

            def slot(k, it, more=4):
                if k % 2 == 0 and k >= 2:
                    gelu_conv1(k // 2 - 1, it)
                if k == NT + 1:
                    gelu_conv2(it)
                if more > 3:
                    gelu_conv0(k + 3, it)
                gelu_region(k, it)
                if more > 2:
                    gelu_dw(k + 2, it)

            for k in range(LEAD):
                slot(k, 0)
            with act.Fori(0, G - 1) as it:
                for k in range(LEAD, NT + LEAD):
                    slot(k, it)
            for k in range(LEAD, NT):
                slot(k, G - 1, NT - k)
            gelu_conv1(G - 1, G - 1)
            gelu_conv2(G - 1)

            act.wait_ge(s_pb0, 2)

            def xT_copy(i):
                act.wait_ge(s_zT, i + 1)
                for h in range(2):
                    last = fn(xT[:, h, :], ps[0:DC, 0, h * PR:(h + 1) * PR], ACT.Identity,
                              scale=qkc("ln", h, h + 1), bias=qkc("ln", 2 + h, 3 + h))
                last.then_inc(s_xT, 1)

            def pt_copy(i):
                for b in range(3):
                    act.wait_ge(s_PT, 3 * i + b + 1)
                    fn(Pt[:, b * 4:b * 4 + 4, :], ps[0:PR, 5 + b, 0:4 * PR].rearrange("p (h n) -> p h n", h=4),
                       ACT.Copy).then_inc(s_Pt, 1)

            def oT_copy(i):
                act.wait_ge(s_OT, i + 1)
                fn(oT[:, :, :], ps[0:DC, 2, 0:2 * PR].rearrange("p (h n) -> p h n", h=2), ACT.Copy).then_inc(s_oT, 1)

            def q_copy(i):
                act.wait_ge(s_v, i + 1)
                if not (isinstance(i, int) and i == 0):
                    act.wait_ge(s_S, i)
                fn(qT[:, :, :], ps[0:DC, 2, 0:2 * PR].rearrange("p (h n) -> p h n", h=2), ACT.Copy).then_inc(s_q, 1)

            def v_copy(i):
                fn(V[:, bass.ds(i, 1), :, 0:HD].rearrange("p o h d -> p (o h) d"),
                   ps[0:PR, 2, 256:256 + D].rearrange("p (h d) -> p h d", h=NH), ACT.Copy).then_inc(s_V, 1)

            def exps(i):
                act.wait_ge(s_sub, i + 1)
                for p in range(2):
                    r = slice(p * P2, p * P2 + TOK)
                    last = fn(Pb[r, :, r], Sc[r, :, :], ACT.Exp, scale=HD ** -0.5)
                last.then_inc(s_exp, 1)

            def x2T_copy(i):
                act.wait_ge(s_z2T, i + 1)
                for h, x in enumerate((xA, xB)):
                    src = ps[:, 1, h * PR:h * PR + 2 * P2].rearrange("p (q t) -> p q t", q=2)[:, :, 0:TOK]
                    last = fn(x[:, bass.ds(i * PT, PT)].rearrange("p (q t) -> p q t", q=2), src, ACT.Identity,
                              scale=pkc("v", 128, 8 + h, 9 + h), bias=pkc("v", 128, 10 + h, 11 + h))
                last.then_inc(s_x2T, 1)

            def tile(i):
                a, b, c, d, e = stages(i)
                if a:
                    xT_copy(i)
                if c:
                    pt_copy(i - 2)
                if d:
                    oT_copy(i - 3)
                if a:
                    q_copy(i)
                    v_copy(i)
                if b:
                    exps(i - 1)
                if e:
                    x2T_copy(i - 4)

            for i in range(4):
                tile(i)
            with act.Fori(4, NP) as i:
                tile(i)
            for i in range(NP, NP + 4):
                tile(i)

            act.wait_ge(s_d21, 1)
            fn(sc[:, :, 1], sc[:, :, 0], ACT.Exp).then_inc(s_cwe, 1)

            def hidden(step):
                nt = GROUPS[step[1] % NG][1]
                e = step[1] // NG
                for c in range(FC):
                    n = chunks_before(step) + c
                    act.wait_ge(s_l1, n + 1)
                    if c == 0 and not is_one(step, 1):
                        back = len(GROUPS[(step[1] - 1) % NG][2])
                        act.wait_ge(s_l2, tiles_before(step) - back)
                    if not (is_one(step, 0) and c < 2):
                        act.wait_ge(s_lo, n - 1)
                    for o in (hh[:, step[1] % 2, c, 0:nt], hf[:, c % 2, 0:nt]):
                        last = fn(o, ps[:, (step[1] * FC + c) % 4, 0:nt], ACT.Gelu, bias=b1s[:, e, c:c + 1])
                    last.then_inc(s_h, 1)

            def experts(ep):
                for s in range(2 * NG):
                    hidden((ep, s))

            experts(0)
            with act.Fori(1, NE // 2) as ep:
                experts(ep)

        @block.gpsimd
        def _(pool):
            gp = nc.gpsimd
            gp.memset(nhalf[:, :], -0.5).then_inc(s_kt, 1)
            pool.wait_ge(s_kt, 1)

            def split_weights(gy, it):
                pool.wait_ge(s_w[gy], (it + 1) * 16)
                gp.tensor_tensor(junk[:, :], nhalf[0:1, 0:1], nhalf[0:1, 0:1], ALU.add)
                gp.tensor_copy(wh[:, gy, :], wr[:, gy, 0:4 * MI]).then_inc(s_ph, 1)
                pool.wait_ge(s_ph, it * G + gy + 1)
                gp.tensor_tensor(wl[:, gy, :], wr[:, gy, 0:4 * MI], wh[:, gy, :].bitcast(F32), ALU.subtract).then_inc(s_ws, 1)

            for gy in range(G):
                split_weights(gy, 0)
            pool.wait_ge(s_kd, 16)
            with pool.Fori(0, TOK) as s:
                pool.dma_start(td[bass.ds(s, 1)], kd[:, bass.ds(TOK - 1 - s, TOK)].rearrange("c (o t) -> o c t", o=1)
                               ).then_inc(s_td, 16)
            with pool.Fori(1, G) as it:
                for gy in range(G):
                    split_weights(gy, it)
            pool.wait_ge(s_td, 16 * TOK)
            for p in range(2):
                pool.dma_start(T[p * P2:p * P2 + TOK, :, :], td).then_inc(s_T, 16)
            pool.wait_ge(s_hs, G)
            gp.memset(V[:, :, :, HD:HV], 1.0)
            gp.memset(Pb[:, :, :], 0.0).then_inc(s_pb0, 1)
            pool.wait_ge(s_pb0, 1)
            gp.memset(Pb[P2 // 2:P2, :, 0:1], 1.0).then_inc(s_pb0, 1)
            pool.wait_ge(s_pb0, 2)

            def split_expert(e, half):
                gp.tensor_tensor(junk[:, :], nhalf[0:1, 0:1], nhalf[0:1, 0:1], ALU.add)
                k = 3 * e
                gp.tensor_copy(w1h[:, half], w1f[:, :, :]).then_inc(s_ph2, 1)
                gp.tensor_copy(b1s[:, half, :], w2f[:, FC * D:FC * D + FC]).then_inc(s_ph2, 1)
                gp.tensor_copy(w2s[:, half, :, 0], w2f[:, 0:FC * D].rearrange("p (c n) -> p c n", c=FC)).then_inc(s_ph2, 1)
                pool.wait_ge(s_ph2, k + 3)
                gp.tensor_tensor(w1l[:, half], w1f[:, :, :], w1h[:, half].bitcast(F32), ALU.subtract).then_inc(s_w1s, 1)
                gp.tensor_tensor(w2s[:, half, :, 1], w2f[:, 0:FC * D].rearrange("p (c n) -> p c n", c=FC),
                                  w2s[:, half, :, 0].bitcast(F32), ALU.subtract).then_inc(s_w2s, 1)

            for n in range(3):
                if n == 1:
                    pool.wait_ge(s_wf, 32)
                    split_expert(0, 0)
                pool.wait_ge(s_va, n + 1)
                nc.gpsimd.tensor_tensor(rs[:, :], va[:, :], nhalf[:, :], ALU.pow).then_inc(s_rs, 1)
            pool.wait_ge(s_wf, 64)
            split_expert(1, 1)
            with pool.Fori(0, NP) as i:
                pool.wait_ge(s_st, 3 * i + 3)
                nc.gpsimd.tensor_tensor(st2[:, 9:10], st2[:, 8:9], nhalf[:, 0:1], ALU.pow).then_inc(s_pow, 1)
                pool.wait_ge(s_x1, i + 1)
                nc.gpsimd.tensor_tensor(H[:, bass.ds(i, 1), :], H[:, bass.ds(i, 1), :],
                                        x1[:, :].unsqueeze(1), ALU.add).then_inc(s_R, 1)
            with pool.Fori(1, NE // 2) as ep:
                for half in range(2):
                    e = ep * 2 + half
                    pool.wait_ge(s_wf, (e + 1) * 32)
                    pool.wait_ge(s_l2, (e - 1) * TT)
                    split_expert(e, half)

        @block.vector
        def _(dve):
            ve = nc.vector
            chain = [0, 0]

            def link(ins):
                chain[1] += 1
                ins.then_inc(s_ch, 1)
                dve.wait_ge(s_ch, chain[0] + chain[1])

            for t in (Ah, Al):
                ve.memset(t[:, :, :, 0:RS + 2:RS + 1].bitcast(F32), 0.0)
            ve.memset(Ft[:, :, :], 0.0)
            ve.memset(kp[:, :, :], 0.0)
            ve.memset(H[:, :, :], 0.0).then_inc(s_init, 1)
            dve.wait_ge(s_init, 1)
            dve.wait_ge(s_const, 16 * 7)
            ve.tensor_copy(w0h[:, :], pkc("w0", KX)).then_inc(s_w0s, 1)
            dve.wait_ge(s_w0s, 1)
            ve.tensor_tensor(w0l[:, :], pkc("w0", KX), w0h[:, :].bitcast(F32), ALU.subtract).then_inc(s_w0s, 1)
            for h in range(2):
                ve.tensor_scalar(kt[:, 0, 0, h:h + 1], qkc("k3", 2 + h, 3 + h), -1.0, None, ALU.mult)

            done = [0]

            def mark(ins):
                done[0] += 1
                ins.then_inc(s_fdve, 1)
                dve.wait_ge(s_fdve, done[0])

            def filter_sine(layer):
                dve.wait_ge(s_fpe, layer + 1)
                mark(ve.tensor_scalar(fa[:, 0, :], ps[0:16, 7, 64 * layer:64 * layer + TOK],
                                      qkc("f", 82 + 2 * layer, 83 + 2 * layer, 16),
                                      qkc("f", 83, 84, 16), ALU.add, ALU.mult))
                mark(ve.tensor_scalar(fa[:, 1, :], fa[:, 0, :], float(1 / (2 * np.pi)), MAGIC, ALU.mult, ALU.add))
                mark(ve.tensor_scalar(fa[:, 1, :], fa[:, 1, :], MAGIC, None, ALU.subtract))
                mark(ve.scalar_tensor_tensor(fa[:, 2, :], fa[:, 1, :], -TWO_PI_HI, fa[:, 0, :], ALU.mult, ALU.add))
                mark(ve.scalar_tensor_tensor(fa[:, 0, :], fa[:, 1, :], -TWO_PI_LO, fa[:, 2, :], ALU.mult, ALU.add))
                mark(ve.tensor_scalar(fa[:, 3, :], fa[:, 0, :], PI_MAX, -PI_MAX, ALU.min, ALU.max))

            def split_input(k, it):
                gy, half = k % NT // 2, k % 2
                t = it * NT + k
                if half == 0:
                    dve.wait_ge(s_x[gy], (it + k // NT + 1) * 16)
                if k >= 2:
                    dve.wait_ge(s_conv0, t - 1)
                link(ve.tensor_copy(xh[:, k % 2, :], xin[:, gy, half, :]))
                ve.tensor_tensor(xl[:, k % 2, :], xin[:, gy, half, :], xh[:, k % 2, :].bitcast(F32), ALU.subtract
                                 ).then_inc(s_xsp, 1)

            def split_conv0(k, it):
                dve.wait_ge(s_A, it * NT + k + 1)
                ve.tensor_tensor(Al[:, k % 2, :, 1:1 + RS], A[:, k % G, :, 1:1 + RS], Ah[:, k % 2, :, 1:1 + RS].bitcast(F32),
                                 ALU.subtract).then_inc(s_Al, 1)

            def split_dw(k, it):
                dve.wait_ge(s_B, it * NT + k + 1)
                ve.tensor_tensor(Bl[:, k % 2, :], Bt[:, k % 2, :], Bh[:, k % 2, :].bitcast(F32), ALU.subtract).then_inc(s_Bl, 1)

            def add_input(k, it):
                dve.wait_ge(s_pw, it * NT + k + 1)
                gy = k % NT // 2
                ve.scalar_tensor_tensor(Ct[:, k % 2, :].rearrange("p (b r) -> p b r", b=B),
                                        ps[0:MI, 4, 0:N].rearrange("p (b r) -> p b r", b=B),
                                        wr[0:MI, gy, 4 * MI + 2:4 * MI + 3], A[0:MI, k % G, :, 1:1 + RS],
                                        ALU.mult, ALU.add).then_inc(s_C, 1)

            def tokens(it):
                dve.wait_ge(s_conv3, it + 1)
                for g, n in ((0, 128), (1, 96)):
                    last = ve.tensor_tensor(hs[0:n, g, :], ps[0:n, 7, g * D:(g + 1) * D], s3bc[0:n, :], ALU.mult)
                link(last)
                for g, n in ((0, 128), (1, 96)):
                    last = ve.tensor_tensor(hs[0:n, g, :], hs[0:n, g, :], b3bc[0:n, :], ALU.add)
                last.then_inc(s_hs, 1)

            filter_sine(0)
            for k in range(2):
                split_input(k, 0)
            split_conv0(0, 0)
            filter_sine(1)
            split_input(2, 0)
            split_conv0(1, 0)
            split_input(3, 0)
            dve.wait_ge(s_fpe, 3)
            dve.wait_ge(s_fact, 3)
            for h in range(2):
                last = ve.scalar_tensor_tensor(kp[:, h, TOK - 1:2 * TOK - 1], ps[0:DC, 7, 128 + 64 * h:128 + 64 * h + TOK],
                                               qkc("k3", h, h + 1), kt[:, 1, h, :], ALU.add, ALU.mult)
            mark(last)
            mark(ve.tensor_scalar(kp[:, :, :], kp[:, :, :], 1.0 / KL, None, ALU.mult))
            mark(ve.tensor_tensor(kp[:, :, TOK - 1:TOK], kp[:, :, TOK - 1:TOK],
                                  qkc("k3", 4, 6).unsqueeze(2), ALU.add))
            split_conv0(2, 0)
            split_dw(0, 0)
            add_input(0, 0)

            def slot(k, it, more=5):
                if k == NT + 2:
                    tokens(it)
                if more > 1:
                    split_dw(k + 1, it)
                if more > 4:
                    split_input(k + 4, it)
                if more > 3:
                    split_conv0(k + 3, it)
                if more > 1:
                    add_input(k + 1, it)

            for k in range(LEAD):
                slot(k, 0)
            before = chain[1]
            with dve.Fori(0, G - 1) as it:
                chain[0], chain[1] = it * (NT + 1) + before, 0
                for k in range(LEAD, NT + LEAD):
                    slot(k, it)
            assert chain[1] == NT + 1
            chain[0], chain[1] = (G - 1) * (NT + 1) + before, 0
            for k in range(LEAD, NT):
                slot(k, G - 1, NT - k)
            dve.wait_ge(s_hd, 16 * G * (G - 1))
            tokens(G - 1)

            dve.wait_ge(s_H, 32)
            dve.wait_ge(s_cls, 32)
            for i in range(NP):
                last = ve.bn_stats(st[:, i, :], H[:, i, :])
            link(last)
            for i in range(NP):
                last = ve.bn_aggr(mv[:, i, :], st[:, i, :])
            link(last)
            ve.tensor_scalar(va[:, :], mv[:, :, 1], EPS, None, ALU.add).then_inc(s_va, 1)
            dve.wait_ge(s_rs, 1)
            for i in range(NP):
                last = ve.tensor_scalar(U[:, :, i], H[:, i, :], mv[:, i, 0:1], rs[:, i:i + 1], ALU.subtract, ALU.mult)
            last.then_inc(s_U, 1)
            for j in range(D // 32):
                for p in range(2):
                    n = 2 * j + p
                    dve.wait_ge(s_lc, n + 1)
                    r = slice(p * P2, p * P2 + TOK)
                    ve.tensor_tensor(H[r, :, j * 32:(j + 1) * 32], ps[r, n % 8, :].rearrange("p (c i) -> p i c", c=32),
                                     H[r, :, j * 32:(j + 1) * 32], ALU.add).then_inc(s_lcv, 1)
            dve.wait_ge(s_lcv, 12)
            ve.memset(xA[:, B * TOK:TP], 0.0)
            ve.memset(xB[:, B * TOK:TP], 0.0)
            for i in range(NP):
                last = ve.bn_stats(st[:, i, :], H[:, i, :])
            link(last)
            for i in range(NP):
                last = ve.bn_aggr(mv[:, i, :], st[:, i, :])
            link(last)
            ve.tensor_scalar(va[:, :], mv[:, :, 1], EPS, None, ALU.add).then_inc(s_va, 1)
            dve.wait_ge(s_rs, 2)
            for i in range(NP):
                last = ve.tensor_scalar(X1[:, i, :], H[:, i, :], mv[:, i, 0:1], rs[:, i:i + 1], ALU.subtract, ALU.mult)
            link(last)
            for i in range(NP):
                last = ve.bn_stats(st[:, i, :], X1[:, i, :])
            link(last)
            for i in range(NP):
                last = ve.bn_aggr(mv[:, i, :], st[:, i, :])
            link(last)
            ve.tensor_scalar(va[:, :], mv[:, :, 1], EPS, None, ALU.add).then_inc(s_va, 1)
            dve.wait_ge(s_rs, 3)

            def z_norm(i):
                if not (isinstance(i, int) and i == 0):
                    dve.wait_ge(s_zT, i)
                ve.tensor_scalar(z1[:, :].unsqueeze(1), X1[:, bass.ds(i, 1), :],
                                 mv[:, bass.ds(i, 1), 0:1].rearrange("p o n -> p (o n)"),
                                 rs[:, bass.ds(i, 1)], ALU.subtract, ALU.mult).then_inc(s_z, 1)

            def softmax_top(i):
                dve.wait_ge(s_S, i + 1)
                S = ps[0:PR, 3:5, 0:HH * TOK].rearrange("p h (k m) -> p h k m", k=HH)
                m = mx[:, :].rearrange("p (h k) -> p h k", h=2)
                ve.tensor_reduce(m, S, AX.X, ALU.max).then_inc(s_mx, 1)
                dve.wait_ge(s_mx, i + 1)
                if not (isinstance(i, int) and i == 0):
                    dve.wait_ge(s_exp, i)
                for h in range(2):
                    last = ve.tensor_tensor(Sc[:, h * HH:(h + 1) * HH, :], S[:, h],
                                            m[:, h].unsqueeze(2).to_broadcast([PR, HH, TOK]), ALU.subtract)
                last.then_inc(s_sub, 1)

            def k_blocks(i):
                dve.wait_ge(s_k, i + 1)
                for h in range(2):
                    last = ve.tensor_tensor(kb[:, h], ps[0:DC, 1, h * PR:(h + 1) * PR].unsqueeze(1).to_broadcast([DC, HH, PR]),
                                            qkc("mask").unsqueeze(2).to_broadcast([DC, HH, PR]), ALU.mult)
                last.then_inc(s_kb, 1)

            def o_norm(i):
                dve.wait_ge(s_O, i + 1)
                o = ps[0:PR, 5, 0:NH * HV].rearrange("p (h d) -> p h d", h=NH)
                ve.reciprocal(ri[:, :].unsqueeze(2), o[:, :, HD:HV]).then_inc(s_ri, 1)
                dve.wait_ge(s_ri, i + 1)
                if not (isinstance(i, int) and i == 0):
                    dve.wait_ge(s_OT, i)
                ve.tensor_tensor(o1[:, :].rearrange("p (h d) -> p h d", h=NH), o[:, :, 0:HD],
                                 ri[:, :].unsqueeze(2).to_broadcast([PR, NH, HD]), ALU.mult).then_inc(s_o1, 1)

            def add_attention(i):
                dve.wait_ge(s_pj, i + 1)
                if not (isinstance(i, int) and i == 0):
                    dve.wait_ge(s_R, i)
                ve.tensor_tensor(x1[:, :].unsqueeze(1), ps[0:PR, 0, 0:D].unsqueeze(1), X1[:, bass.ds(i, 1), :],
                                 ALU.add).then_inc(s_x1, 1)
                dve.wait_ge(s_x1, i + 1)
                ve.bn_stats(st2[:, 0:6], x1[:, :]).then_inc(s_st, 1)
                dve.wait_ge(s_st, 3 * i + 1)
                ve.memset(st2[:, 10:11], 0.0)
                ve.bn_aggr(st2[:, 6:8], st2[:, 0:6]).then_inc(s_st, 1)
                dve.wait_ge(s_st, 3 * i + 2)
                ve.tensor_scalar(st2[:, 8:9], st2[:, 7:8], EPS, None, ALU.add).then_inc(s_st, 1)
                dve.wait_ge(s_pow, i + 1)
                if not (isinstance(i, int) and i == 0):
                    dve.wait_ge(s_z2T, i)
                ve.tensor_scalar(z2[:, D:256], x1[:, 128:D], st2[:, 6:7], st2[:, 9:10], ALU.subtract, ALU.mult)
                ve.tensor_scalar(z2[:, 0:D], x1[:, :], st2[:, 6:7], st2[:, 9:10], ALU.subtract, ALU.mult).then_inc(s_z2, 1)

            def tile(i):
                a, b, c, d, e = stages(i)
                if a:
                    z_norm(i)
                if b:
                    softmax_top(i - 1)
                if a:
                    k_blocks(i)
                if d:
                    add_attention(i - 3)
                if c:
                    o_norm(i - 2)

            for i in range(4):
                tile(i)
            with dve.Fori(4, NP) as i:
                tile(i)
            for i in range(NP, NP + 4):
                tile(i)

            def split_group(g):
                t0, nt, _ = GROUPS[g]
                t = slice(t0, t0 + nt)
                ve.tensor_copy(xAh[:, t], xA[:, t])
                link(ve.tensor_copy(xBs[:, t], xB[:, t]))
                ve.tensor_tensor(xAl[:, t], xA[:, t], xAh[:, t].bitcast(F32), ALU.subtract)
                ve.tensor_tensor(xBs[D - 128:, t], xB[D - 128:, t], xBs[D - 128:, t].bitcast(F32), ALU.subtract).then_inc(s_xs, 1)

            dve.wait_ge(s_x2T, NP)
            split_group(0)
            dve.wait_ge(s_lg, 1)
            ve.tensor_copy(lg[:, :, :], ps[:, 7, 0:TT * NE].rearrange("p (i e) -> p i e", i=TT)).then_inc(s_lgc, 1)
            dve.wait_ge(s_lgc, 1)
            for i in range(TT):
                last = ve.max(m8[:, i, :], lg[:, i, :])
            link(last)
            ve.tensor_tensor(sc[:, :, 0], m8[:, :, 1], m8[:, :, 0], ALU.subtract).then_inc(s_d21, 1)
            for i in range(TT):
                last = ve.max_index(i8[:, i, :], m8[:, i, :], lg[:, i, :])
            link(last)
            link(ve.tensor_copy(f8[:, :, :], i8[:, :, 0:2]))
            for r in range(2):
                last = ve.tensor_tensor(oh[:, r], iot[:, :].unsqueeze(1).to_broadcast([128, TT, NE]),
                                        f8[:, :, r:r + 1].to_broadcast([128, TT, NE]), ALU.is_equal)
            link(last)
            dve.wait_ge(s_cwe, 1)
            link(ve.tensor_scalar(sc[:, :, 0], sc[:, :, 1], 1.0, None, ALU.add))
            link(ve.reciprocal(sc[:, :, 2], sc[:, :, 0]))
            link(ve.tensor_tensor(sc[:, :, 3], sc[:, :, 1], sc[:, :, 2], ALU.mult))
            for r in range(2):
                last = ve.tensor_tensor(oh[:, r], oh[:, r], sc[:, :, 2 + r:3 + r].to_broadcast([128, TT, NE]), ALU.mult)
            link(last)
            ve.tensor_tensor(cw[:, :, :], oh[:, 0], oh[:, 1], ALU.add).then_inc(s_cw, 1)
            dve.wait_ge(s_cw, 1)
            for q in range(4):
                n = min(4, TT - 4 * q)
                dve.wait_ge(s_ct, 4 * q + n)
                ve.tensor_copy(cT[:, 512 * q:512 * q + n * 128], ps[0:NE, 4 + q, 0:n * 128]).then_inc(s_cT, 1)
            split_group(1)
            dve.wait_ge(s_rl, 32)
            for i in range(TT):
                p = 128 if i < TT - 1 else LAST
                dve.wait_ge(s_acc0, i + 1)
                ve.tensor_tensor(acc[0:p, i, :], ps[0:p, 4 + i % 4, 0:D], acc[0:p, i, :], ALU.add).then_inc(s_b2, 1)
            dve.wait_ge(s_b2, TT)

            def hidden_low(step):
                nt = GROUPS[step[1] % NG][1]
                for c in range(FC):
                    dve.wait_ge(s_h, chunks_before(step) + c + 1)
                    h = step[1] % 2
                    ve.tensor_tensor(hl[:, h, c, 0:nt], hf[:, c % 2, 0:nt], hh[:, h, c, 0:nt].bitcast(F32), ALU.subtract
                                     ).then_inc(s_lo, 1)

            def add_outputs(step):
                tiles = GROUPS[step[1] % NG][2]
                for j, i in enumerate(tiles):
                    p = 128 if i < TT - 1 else LAST
                    n = tiles_before(step) + j
                    dve.wait_ge(s_l2, n + 1)
                    if not is_one(step, NG - 1):
                        dve.wait_ge(s_acc, n - TT + 1)
                    ve.scalar_tensor_tensor(acc[0:p, i, :], ps[0:p, 4 + j, 0:D], cw[0:p, i, bass.ds(expert_of(step), 1)],
                                            acc[0:p, i, :], ALU.mult, ALU.add).then_inc(s_half, 1)
                for j, i in enumerate(tiles):
                    p = 128 if i < TT - 1 else LAST
                    n = tiles_before(step) + j
                    dve.wait_ge(s_half, n + 1)
                    ve.scalar_tensor_tensor(acc[0:p, i, :], ps[0:p, 4 + j, D:2 * D], cw[0:p, i, bass.ds(expert_of(step), 1)],
                                            acc[0:p, i, :], ALU.mult, ALU.add).then_inc(s_acc, 1)

            hidden_low((0, 0))
            split_group(2)
            split_group(3)

            def experts(ep, last):
                for s in range(2 * NG):
                    if not (last and s + 1 == 2 * NG):
                        hidden_low((ep, (s + 1)))
                    add_outputs((ep, s))

            experts(0, False)
            with dve.Fori(1, NE // 2 - 1) as ep:
                experts(ep, False)
            experts(NE // 2 - 1, True)


def lay_out(a):
    f = np.float32
    t = "L0_tok_"
    x = np.asarray(a["x"])
    xp = np.zeros((B, CI, G * RS + 2, G * RS + 4), f)
    xp[:, :, 1:-1, 2:-2] = x
    xh = np.zeros((G, G, 3, HW + 4, CI, 2, B, RS), f)
    for gx in range(G):
        for gy in range(G):
            for half in range(2):
                for dy in range(3):
                    c0 = RS * gx + HW * half
                    v = xp[:, :, RS * gy + dy:RS * gy + dy + RS, c0:c0 + HW + 4]
                    xh[gx, gy, dy, :, :, half] = v.transpose(3, 1, 0, 2)
    xh = xh.reshape(G * G, KX, 2 * N)

    def rowof(j, c):
        return c * HW + j - 1 if 1 <= j <= HW else MI + (C1 if j else 0) + c

    wdw = np.asarray(a[t + "wdw"]).reshape(G, G, C1, 3, 3)
    wpw = np.asarray(a[t + "wpw"]).reshape(G, G, C1, C1)
    wreg = np.zeros((G, G, MA, WR), f)
    for c in range(C1):
        for w in range(HW):
            for dy in range(3):
                for dx in range(3):
                    wreg[:, :, rowof(w + dx, c), dy * MI + c * HW + w] = wdw[:, :, c, dy, dx].T
            for co in range(C1):
                wreg[:, :, c * HW + w, 3 * MI + co * HW + w] = wpw[:, :, co, c].T
            for n, name in enumerate(("sdw", "bdw", "spw", "bpw")):
                wreg[:, :, c * HW + w, 4 * MI + n] = np.asarray(a[t + name]).reshape(G, G, C1)[:, :, c].T
    wreg = wreg.reshape(G * G, MA, WR)

    pack = np.zeros((128, PKW), f)
    w0, s0, b0 = (np.asarray(a[t + n]) for n in ("w0", "s0", "b0"))
    o = PK["w0"][0]
    v = PK["v"][0]
    for c in range(C1):
        for j in range(HW + 2):
            for dx in range(3):
                for dy in range(3):
                    for ci in range(CI):
                        pack[(dy * (HW + 4) + j + dx) * CI + ci, o + rowof(j, c)] = w0[c, ci, dy, dx]
            if j > 0:
                pack[rowof(j, c), v:v + 2] = s0[c], b0[c]
            if j <= HW:
                pack[rowof(j, c), v + 2:v + 4] = s0[c], b0[c]
    w1, w2, w3 = (np.asarray(a[t + n]) for n in ("w1", "w2", "w3"))
    for ox in range(2):
        for c in range(C1):
            for dx in range(4):
                for dy in range(4):
                    p = PK["w1"][0] + dy * 96 + ox * C2
                    pack[c * HW + ox * 4 + dx, p:p + C2] = w1[:, c, dy, dx]
        pack[ox * C2:ox * C2 + C2, v + 4] = np.asarray(a[t + "s1"])
        pack[ox * C2:ox * C2 + C2, v + 5] = np.asarray(a[t + "b1"])
        pack[ox * 64:ox * 64 + C2, v + 6] = np.asarray(a[t + "s2"])
        pack[ox * 64:ox * 64 + C2, v + 7] = np.asarray(a[t + "b2"])
        for dy in range(2):
            p = PK["w2"][0] + dy * C2
            pack[ox * C2:ox * C2 + C2, p:p + C2] = w2[:, :, dy, ox].T
            p = PK["w3"][0] + dy * D
            pack[ox * 64:ox * 64 + C2, p:p + D] = w3[:, :, dy, ox].T
    p = PK["eye"][0]
    pack[:, p:p + 128] = np.eye(128, dtype=f)
    m = "L0_ffn_"
    for k, name in enumerate(("ln2_g", "ln2_b")):
        g = np.asarray(a[m + name])
        pack[:, v + 8 + 2 * k] = g[0:128]
        pack[:, v + 9 + 2 * k] = np.tile(g[128:], 2)
    gw = np.asarray(a[m + "gate_w"]).T
    pack[:, PK["g"][0]:PK["g"][0] + NE] = gw[0:128]
    pack[0:D - 128, PK["g"][0] + NE:PK["g"][0] + 2 * NE] = gw[128:]

    qp = np.zeros((96, QKW), f)

    def put(name, v, at=0):
        v = np.asarray(v)
        o = QK[name][0] + at
        qp[0:v.shape[0], o:o + v.shape[1]] = v

    n, m = "L0_attn_", "L0_ffn_"
    for h in range(2):
        c = slice(h * DC, (h + 1) * DC)
        put("qkv", np.asarray(a[m + "qkv_w"]).T[c], h * 3 * D)
        put("pw", np.asarray(a[m + "proj_w"]).T[c], h * D)
        for k, name in enumerate(("ln1_g", "ln1_b")):
            put("ln", np.asarray(a[m + name])[c, None], 2 * k + h)
        for k, name in enumerate(("b3", "deltas_abs", "bias")):
            put("k3", np.asarray(a[n + name])[c, None], 2 * k + h)
    put("mask", np.kron(np.eye(HH, dtype=f), np.ones((HD, 1), f)))
    pos = np.linspace(0.0, 1.0, TOK, dtype=f)
    put("t", np.tile(pos, (DC, 1)))
    put("w3", np.asarray(a[n + "w3"]).T)
    ang = 1e-4 * (2.0 * np.pi * np.linspace(0.0, TOK - 1.0, TOK) / TOK)
    put("f", np.asarray(a[n + "w1"]).T, 0)
    put("f", np.stack([pos, np.cos(ang), -np.sin(ang)]).astype(f), 16)
    put("f", np.asarray(a[n + "w2"]).T, 66)
    for k, name in enumerate(("b1", "freq", "b2")):
        put("f", np.asarray(a[n + name])[:, None], 82 + k)

    rows = np.zeros((1 + NE, D + NE + 128), f)
    rows[0, 0:D] = np.asarray(a[m + "proj_b"])
    rows[0, D:D + NE] = np.asarray(a[m + "gate_b"])
    rows[0, D + NE:] = 1.0
    rows[1:, 0:D] = np.asarray(a[m + "b2"])

    w1t = np.asarray(a[m + "w1"]).transpose(0, 2, 1)
    ew1 = np.concatenate([w1t[:, 0:128], np.tile(w1t[:, 128:], (1, 2, 1))], axis=2)
    w2e = np.asarray(a[m + "w2"]).reshape(NE, D, FC, 128).transpose(0, 3, 2, 1).reshape(NE, 128, FC * D)
    b1e = np.asarray(a[m + "b1"]).reshape(NE, FC, 128).transpose(0, 2, 1)
    ew2 = np.concatenate([w2e, b1e], axis=2)
    return dict(xh=xh, wreg=wreg, pack=pack, qpack=qp, rows=rows, ew1=ew1, ew2=ew2,
                cls=np.asarray(a["cls_tok"]).reshape(1, 1, D), s3=np.asarray(a[t + "s3"]).reshape(1, D),
                b3=np.asarray(a[t + "b3"]).reshape(1, D), iota=np.tile(np.arange(NE, dtype=f), (128, 1)))


def kernel(**inputs):
    import concourse.bacc as bacc
    from concourse.bass_utils import run_bass_kernel_spmd

    nc = bacc.Bacc("TRN2", target_bir_lowering=False, num_devices=1)
    arrays, args = {}, []
    for name, v in lay_out(inputs).items():
        v = np.ascontiguousarray(v)
        arrays["in_" + name] = v
        args.append(nc.dram_tensor("in_" + name, v.shape, mybir.dt.from_np(v.dtype), kind="ExternalInput").ap())
    for name, shape in (("kd", (D, KL)), ("td", (TOK, D, TOK)), ("hd", (B, TOK, D)), ("rd", (B, TOK, D))):
        args.append(nc.dram_tensor(name, shape, F32, kind="Internal").ap())
    args.append(nc.dram_tensor("out", (B, TOK, D), F32, kind="ExternalOutput").ap())
    tower(nc, *args)
    return run_bass_kernel_spmd(nc, [arrays], core_ids=[0]).results[0]["out"]
```

```python
import numpy as np
import concourse.bass as bass
from concourse import mybir
from contextlib import ExitStack

F32 = mybir.dt.float32
F32R = mybir.dt.float32r
U32 = mybir.dt.uint32
ALU = mybir.AluOpType
ACT = mybir.ActivationFunctionType
AX = mybir.AxisListType

B = 32
CI, C1, C2, D = 3, 12, 48, 192
G = 7
RS = 16
HW = RS // 2
NT = 2 * G
KX = 3 * (HW + 4) * CI
MA = C1 * (HW + 2)
MI = C1 * HW
N = B * RS
WR = 4 * MI + 4
TOK = G * G + 1
P2 = 64
PR = P2 + TOK
PT = 2 * TOK
NP = B // 2
LCC = 512 // B
QP = 4
DC = D // 2
NH, HD = 12, 16
HH = NH // 2
HID, NE = 768, 8
FC = HID // 128
TT = B * TOK // 128 + 1
TP = TT * 128
LAST = B * TOK - (TT - 1) * 128
GROUPS = [(t[0] * 128, min(len(t) * 128, B * TOK - t[0] * 128), t) for t in (range(0, 4), range(4, 7), range(7, 10), range(10, TT))]
NG = len(GROUPS)
LEAD = 3
KL = 2 * TOK
EPS = 1e-5
MAGIC = 12582912.0
TWO_PI_HI = 6.28125
TWO_PI_LO = 2 * np.pi - 6.28125
PI_MAX = 3.1415925

PK = dict(w0=(0, MA), w1=(120, 4 * 96), w2=(504, 2 * C2), w3=(600, 2 * D), eye=(984, 128), v=(1112, 12), g=(1124, 2 * NE), gb=(1140, NE))
PKW = 1148
QK = dict(qkv=(0, 2 * 3 * D), pw=(1152, 2 * D), ln=(1552, 8), mask=(1560, HH),
          k3=(1566, 6), t=(1572, TOK), w3=(1622, D), f=(1814, 85))
QKW = 1899
VS = DC + HD


def tower(nc, xtiles, wreg, pack, qpack, rows, b2, ew1, ew2, cls, s3, b3, iota, kd, td, hd, rd, out):
    ctx = ExitStack()
    with ctx:
        def sb(name, shape, dt=F32):
            return ctx.enter_context(nc.sbuf_tensor(name, shape, dt))

        def sem(name):
            return ctx.enter_context(nc.semaphore(name))

        pk = sb("pk", [128, PKW])
        qk = sb("qk", [96, QKW])
        row = sb("row", [1, D + 128])
        s3bc = sb("s3bc", [128, D])
        b3bc = sb("b3bc", [128, D])
        iot = sb("iot", [128, NE])
        hs = sb("hs", [128, 2, D])
        nhalf = sb("nhalf", [PR, NP])
        junk = sb("junk", [1, 1])
        x1 = sb("x1", [PR, D])
        H = sb("H", [PR, NP, D])
        lg = sb("lg", [128, TT, NE])
        m8 = sb("m8", [128, TT, 8])
        i8 = sb("i8", [128, TT, 8], U32)
        f8 = sb("f8", [128, TT, 2])
        sc = sb("sc", [128, TT, 4])
        oh = sb("oh", [128, 2, TT, NE])
        cw = sb("cw", [128, TT, NE])
        b1s = sb("b1s", [128, 2, FC])
        with ExitStack() as now:
            T = now.enter_context(nc.sbuf_tensor("T", [PR, D, TOK], F32))
        xA = sb("xA", [128, TP])
        xB = sb("xB", [128, TP])
        acc = sb("acc", [128, TT, D])
        b2x, b2s = sb("b2x", [128, NE, D]), sb("b2s", [128, NE, D], F32R)
        minus = sb("minus", [128, 128], F32R)
        sb("rest_of_T", [128, D * TOK - 2 * TP - TT * D - 2 * NE * D - 128])
        with ExitStack() as now:
            def early(name, shape, dt=F32):
                return now.enter_context(nc.sbuf_tensor(name, shape, dt))

            xin = early("xin", [KX, G, 2, N])
            xh, xl = early("xh", [KX, 2, N], F32R), early("xl", [KX, 2, N], F32R)
            w0h, w0l = early("w0h", [KX, MA], F32R), early("w0l", [KX, MA], F32R)
            wr = early("wr", [MA, G, WR])
            wh, wl = early("wh", [MA, G, 4 * MI], F32R), early("wl", [MA, G, 4 * MI], F32R)
            A = early("A", [MA, G, B, RS + 2])
            Ah, Al = early("Ah", [MA, 2, B, RS + 2], F32R), early("Al", [MA, 2, B, RS + 2], F32R)
            Bt = early("Bt", [MI, 2, N])
            Bh, Bl = early("Bh", [MI, 2, N], F32R), early("Bl", [MI, 2, N], F32R)
            Ct = early("Ct", [MI, 2, N])
            Dt = early("Dt", [MI, 2, B, RS])
            Et = early("Et", [96, G, 2, B, 4])
            Ft = early("Ft", [112, G, 2 * B])
            fa = early("fa", [16, 6, TOK])
            kp = early("kp", [DC, 2, KL])
            kt = early("kt", [DC, 2, 2, TOK])
        w1f = sb("w1f", [128, 2, HID])
        w2f = sb("w2f", [128, FC * D + FC])
        w1h, w1l = sb("w1h", [128, 2, 2, HID], F32R), sb("w1l", [128, 2, 2, HID], F32R)
        w2s = sb("w2s", [128, 2, FC, 2, D], F32R)
        st = sb("st", [PR, NP, 6])
        mv = sb("mv", [PR, NP, 2])
        va = sb("va", [PR, NP])
        rs = sb("rs", [PR, NP])
        nb = sb("nb", [PR, NP])
        st2 = sb("st2", [PR, 12])
        mx = sb("mx", [PR, NH])
        sm = sb("sm", [PR, NH])
        ri = sb("ri", [PR, NH])
        xAh, xAl, xBs = (sb(n, [128, TP], F32R) for n in ("xAh", "xAl", "xBs"))
        with ExitStack() as now:
            def middle(name, shape):
                return now.enter_context(nc.sbuf_tensor(name, shape, F32))

            with ExitStack() as before:
                U = before.enter_context(nc.sbuf_tensor("U", [PR, D, 2, NP], F32))
            X1 = middle("X1", [PR, NP, D])
            z1 = middle("z1", [PR, D])
            xT = middle("xT", [DC, 2, PR])
            qT = middle("qT", [DC, 2, PR])
            kb = middle("kb", [DC, 2, HH, PR])
            Sc = middle("Sc", [PR, NH, TOK])
            middle("rest_of_U", [PR, D * B - (NP + 1) * D - 4 * PR - NH * PR - NH * TOK])
            V = middle("V", [PR, 2, 2, HH * VS])
            Pb = middle("Pb", [PR, NH, PR])
            Pt = middle("Pt", [PR, NH, PR])
            oT = middle("oT", [DC, 2, 2, PR])
            z2 = middle("z2", [PR, 256])
        hf = sb("hf", [128, 2, 512])
        hh, hl = sb("hh", [128, 2, FC, 512], F32R), sb("hl", [128, 2, FC, 512], F32R)
        ps = ctx.enter_context(nc.psum_tensor("ps", [128, 8, 512], F32))

        def pkc(name, r, a=0, b=None):
            o, w = PK[name]
            return pk[0:r, o + a:o + (w if b is None else b)]

        def qkc(name, a=0, b=None, r=96):
            o, w = QK[name]
            return qk[0:r, o + a:o + (w if b is None else b)]

        s_pk, s_const = sem("s_pk"), sem("s_const")
        s_cls = sem("s_cls")
        s_x = [sem(f"s_xin{g}") for g in range(G)]
        s_w = [sem(f"s_wreg{g}") for g in range(G)]
        s_init = sem("s_init")
        s_conv0, s_dw, s_pw, s_conv1, s_conv2, s_conv3 = (sem(n) for n in
            ("s_conv0", "s_dw", "s_pw", "s_conv1", "s_conv2", "s_conv3"))
        s_w0s, s_ws, s_xsp, s_Al, s_Bl, s_ph = (sem(n) for n in ("s_w0s", "s_ws", "s_xsp", "s_Al", "s_Bl", "s_ph"))
        s_A, s_B, s_C, s_D, s_E, s_F = (sem(n) for n in ("s_A", "s_B", "s_C", "s_D", "s_E", "s_F"))
        s_hs = sem("s_hs")
        s_hd = sem("s_hd")
        s_fpe, s_fdve, s_fact = sem("s_fpe"), sem("s_fdve"), sem("s_fact")
        s_kd, s_td, s_T = sem("s_kd"), sem("s_td"), sem("s_T")
        s_H = sem("s_H")
        s_ch = sem("s_ch")
        s_U0, s_nb, s_U, s_U1, s_T0 = (sem(n) for n in ("s_U0", "s_nb", "s_U", "s_U1", "s_T0"))
        s_kt = sem("s_kt")
        s_pb0, s_ph2 = sem("s_pb0"), sem("s_ph2")
        s_va, s_rs, s_pow = sem("s_va"), sem("s_rs"), sem("s_pow")
        s_lc, s_lcv = sem("s_lc"), sem("s_lcv")
        s_z, s_zT, s_xT = sem("s_z"), sem("s_zT"), sem("s_xT")
        s_k, s_v, s_q, s_kb, s_V = (sem(n) for n in ("s_k", "s_v", "s_q", "s_kb", "s_V"))
        s_S, s_mx, s_sub, s_exp = (sem(n) for n in ("s_S", "s_mx", "s_sub", "s_exp"))
        s_PT, s_Pt, s_O, s_oT = (sem(n) for n in ("s_PT", "s_Pt", "s_O", "s_oT"))
        s_sum, s_ri, s_P0, s_P1 = (sem(n) for n in ("s_sum", "s_ri", "s_P0", "s_P1"))
        s_pj, s_x1, s_st, s_R, s_z2, s_z2T, s_x2T = (sem(n) for n in
            ("s_pj", "s_x1", "s_st", "s_R", "s_z2", "s_z2T", "s_x2T"))
        s_rd, s_rl = sem("s_rd"), sem("s_rl")
        s_lg, s_lgc, s_d21, s_cwe, s_cw, s_b2, s_b2h, s_b2s = (sem(n) for n in ("s_lg", "s_lgc", "s_d21", "s_cwe", "s_cw", "s_b2", "s_b2h", "s_b2s"))
        s_wf, s_w1s, s_w2s = sem("s_wf"), sem("s_w1s"), sem("s_w2s")
        s_xs = sem("s_xs")
        s_l1, s_h, s_lo, s_l2, s_acc = sem("s_l1"), sem("s_h"), sem("s_lo"), sem("s_l2"), sem("s_acc")
        s_half = sem("s_half")
        s_out = sem("s_out")

        def stages(i):
            return [not isinstance(i, int) or 0 <= i - j < NP for j in range(6)]

        def chunks_before(step):
            return (step[0] * (2 * NG) + step[1]) * FC

        def tiles_before(step):
            return (step[0] * 2 + step[1] // NG) * TT + GROUPS[step[1] % NG][2][0]

        def expert_of(step):
            return step[0] * 2 + step[1] // NG

        def is_one(step, last):
            return isinstance(step[0], int) and step[0] == 0 and step[1] <= last

        block = ctx.enter_context(nc.Block())

        @block.sync
        def _(sp):
            def load_region(gy, it):
                r = it * G + gy
                sp.dma_start(xin[:, gy], xtiles[bass.ds(r, 1)].rearrange("o p (s n) -> (o p) s n", s=2)).then_inc(s_x[gy], 16)
                sp.dma_start(wr[:, gy], wreg[bass.ds(r, 1)].rearrange("o p n -> (o p) n")).then_inc(s_w[gy], 16)

            def store_tokens(it):
                sp.wait_ge(s_hs, it + 1)
                for g in range(G):
                    sp.dma_start(hd[:, bass.ds(it + 1 + g * G, 1), :],
                                 hs[32 * (g % 4):32 * (g % 4) + B, g // 4, :].rearrange("b (o c) -> b o c", o=1)
                                 ).then_inc(s_hd, 16)

            sp.dma_start(pk[:, :], pack).then_inc(s_pk, 16)
            load_region(0, 0)
            sp.dma_start(qk[:, :], qpack).then_inc(s_const, 16)
            sp.dma_start(row[:, :], rows[0:1, :]).then_inc(s_const, 16)
            sp.dma_start(s3bc[:, :], s3.to_broadcast([128, D])).then_inc(s_const, 16)
            sp.dma_start(b3bc[:, :], b3.to_broadcast([128, D])).then_inc(s_const, 16)
            sp.dma_start(iot[:, :], iota).then_inc(s_const, 16)
            for gy in range(1, G):
                load_region(gy, 0)
            sp.wait_ge(s_fdve, 15)
            sp.dma_start(kd.rearrange("(h c) l -> c h l", h=2), kp[:, :, :]).then_inc(s_kd, 16)
            sp.wait_ge(s_init, 2)
            for p in range(2):
                sp.dma_start(H[p * P2:p * P2 + 1, :, :], cls.to_broadcast([1, NP, D])).then_inc(s_cls, 16)

            def next_region(gy, it):
                sp.wait_ge(s_D, it * NT + 2 * gy + 2)
                load_region(gy, it + 1)

            for gy in range(2):
                next_region(gy, 0)
            with sp.Fori(0, G - 2) as it:
                for gy in range(2, G):
                    next_region(gy, it)
                next_region(0, it + 1)
                store_tokens(it)
                sp.wait_ge(s_D, (it + 1) * NT + 4)
                sp.wait_ge(s_hd, (it + 1) * 16 * G)
                load_region(1, it + 2)
            for gy in range(2, G):
                next_region(gy, G - 2)
            store_tokens(G - 2)
            sp.wait_ge(s_hd, 16 * G * (G - 1))
            sp.wait_ge(s_cls, 32)
            hv = hd.rearrange("(i q) t c -> q t i c", q=2)
            for p in range(2):
                for g in range(G):
                    t = slice(g * G + 1, g * G + G)
                    sp.dma_start(H[p * P2 + t.start:p * P2 + t.stop, :, :], hv[p, t]).then_inc(s_H, 16)
            store_tokens(G - 1)
            sp.wait_ge(s_hs, G)

            def load_expert(e):
                sp.dma_start(w1f[:, :, :], ew1[bass.ds(e, 1)].rearrange("o p (k n) -> (o p) k n", k=2)).then_inc(s_wf, 16)
                sp.dma_start(w2f[:, :], ew2[bass.ds(e, 1)].rearrange("o p n -> (o p) n")).then_inc(s_wf, 16)

            sp.wait_ge(s_hd, 16 * G * G)
            for p in range(2):
                sp.dma_start(H[p * P2 + G:p * P2 + TOK:G, :, :], hv[p, G:TOK:G]).then_inc(s_H, 16)
            load_expert(0)
            sp.wait_ge(s_w2s, 1)
            load_expert(1)
            sp.wait_ge(s_lc, D // LCC)
            sp.dma_start(b2x[:, :, :], b2.to_broadcast([128, NE, D])).then_inc(s_b2, 16)
            sp.wait_ge(s_R, NP)
            rv = rd.rearrange("(i q) t c -> q t i c", q=2)
            for p in range(2):
                sp.dma_start(rv[p], H[p * P2:p * P2 + TOK, :, :]).then_inc(s_rd, 16)
            sp.wait_ge(s_rd, 32)
            full = (TT - 1) * 128
            rf, of = rd.rearrange("b t c -> (b t) c"), out.rearrange("b t c -> (b t) c")
            sp.dma_start(acc[:, 0:TT - 1, :], rf[0:full].rearrange("(i p) c -> p i c", p=128)).then_inc(s_rl, 16)
            sp.dma_start(acc[0:LAST, TT - 1, :], rf[full:full + LAST]).then_inc(s_rl, 16)
            with sp.Fori(2, NE) as e:
                sp.wait_ge(s_w2s, e)
                load_expert(e)
            for n, (t0, nt, tiles) in enumerate(GROUPS):
                sp.wait_ge(s_acc, (NE - 1) * TT + tiles[-1] + 1)
                full = nt // 128
                sp.dma_start(of[t0:t0 + full * 128].rearrange("(i p) c -> p i c", p=128),
                             acc[:, tiles[0]:tiles[0] + full, :]).then_inc(s_out, 16)
            sp.dma_start(of[B * TOK - LAST:B * TOK], acc[0:LAST, TT - 1, :]).then_inc(s_out, 16)
            sp.wait_ge(s_out, 16 * (NG + 1))

        @block.tensor
        def _(pe):
            mm = nc.tensor.matmul

            def conv0(k, it):
                t = it * NT + k
                gy, half = k % NT // 2, k % 2
                pe.wait_ge(s_xsp, t + 1)
                if k >= 2:
                    pe.wait_ge(s_A, t - 1)
                o = ps[0:MA, k % 2, 0:N]
                mm(o, w0h[:, :], xh[:, k % 2, :], start=True, stop=False)
                mm(o, w0l[:, :], xh[:, k % 2, :], start=False, stop=False)
                mm(o, w0h[:, :], xl[:, k % 2, :], start=False, stop=True).then_inc(s_conv0, 1)

            def depthwise(k, it):
                t = it * NT + k
                gy = k % NT // 2
                if k % 2 == 0:
                    pe.wait_ge(s_ws, it * G + k // 2 + 1)
                pe.wait_ge(s_A, t + 1)
                if k >= 2:
                    pe.wait_ge(s_B, t - 1)
                o = ps[0:MI, 2 + k % 2, 0:N]
                for w in (wh, wl):
                    for dy in range(3):
                        mm(o, w[:, gy, dy * MI:(dy + 1) * MI], Ah[:, k % 2, :, dy:dy + RS],
                           start=(w is wh and dy == 0), stop=False)
                pe.wait_ge(s_Al, t + 1)
                for dy in range(3):
                    last = mm(o, wh[:, gy, dy * MI:(dy + 1) * MI], Al[:, k % 2, :, dy:dy + RS], start=False, stop=(dy == 2))
                last.then_inc(s_dw, 1)

            def pointwise(k, it):
                t = it * NT + k
                gy = k % NT // 2
                pe.wait_ge(s_B, t + 1)
                if k >= 1:
                    pe.wait_ge(s_C, t)
                o = ps[0:MI, 4, 0:N]
                mm(o, wh[0:MI, gy, 3 * MI:4 * MI], Bh[:, k % 2, :], start=True, stop=False)
                mm(o, wl[0:MI, gy, 3 * MI:4 * MI], Bh[:, k % 2, :], start=False, stop=False)
                pe.wait_ge(s_Bl, t + 1)
                mm(o, wh[0:MI, gy, 3 * MI:4 * MI], Bl[:, k % 2, :], start=False, stop=True).then_inc(s_pw, 1)

            def conv1(k, it):
                t = it * NT + k
                gy, half = k % NT // 2, k % 2
                pe.wait_ge(s_D, t + 1)
                if half == 0 and k >= 4:
                    pe.wait_ge(s_E, it * G + k // 2 - (1 if gy else 0))
                for dy in range(4):
                    last = mm(ps[0:96, 5 + gy % 2, half * 128:half * 128 + 128], pkc("w1", MI, dy * 96, dy * 96 + 96),
                              Dt[:, k % 2, :, dy:RS:4], start=(dy == 0), stop=(dy == 3))
                if half:
                    last.then_inc(s_conv1, 1)

            def conv2(it):
                pe.wait_ge(s_E, (it + 1) * G)
                for half in range(2):
                    for dy in range(2):
                        last = mm(ps[64 * half:64 * half + C2, 7, 0:G * 64], pkc("w2", 96, dy * C2, dy * C2 + C2),
                                  Et[:, :, half].rearrange("p g b (o d) -> p g (b o) d", d=2)[:, :, :, dy],
                                  start=(dy == 0), stop=(dy == 1))
                last.then_inc(s_conv2, 1)

            def conv3(it):
                pe.wait_ge(s_F, it + 1)
                for g, n in ((0, 4), (1, 3)):
                    for dy in range(2):
                        last = mm(ps[0:32 * n, 7, g * D:(g + 1) * D],
                                  Ft[:, 4 * g:4 * g + n, :].rearrange("p g (b d) -> p (g b) d", d=2)[:, :, dy],
                                  pkc("w3", 112, dy * D, dy * D + D), start=(dy == 0), stop=(dy == 1))
                last.then_inc(s_conv3, 1)

            pe.wait_ge(s_init, 1)
            pe.wait_ge(s_w0s, 2)
            conv0(0, 0)
            pe.wait_ge(s_const, 16 * 5)
            mm(ps[0:16, 7, 0:TOK], qkc("f", 0, 16, 3), qkc("f", 16, 16 + TOK, 3), start=True, stop=True).then_inc(s_fpe, 1)
            conv0(1, 0)
            depthwise(0, 0)
            pe.wait_ge(s_fact, 1)
            mm(ps[0:16, 7, 64:64 + TOK], qkc("f", 66, 82, 16), fa[:, 5, :], start=True, stop=True).then_inc(s_fpe, 1)
            conv0(2, 0)
            pe.wait_ge(s_fact, 2)
            for h in range(2):
                last = mm(ps[0:DC, 7, 128 + 64 * h:128 + 64 * h + TOK], qkc("w3", h * DC, h * DC + DC, 16), fa[:, 4, :],
                          start=True, stop=True)
            last.then_inc(s_fpe, 1)
            depthwise(1, 0)
            pointwise(0, 0)

            def slot(k, it, more=4):
                if more > 3:
                    conv0(k + 3, it)
                if more > 2:
                    depthwise(k + 2, it)
                if more > 1:
                    pointwise(k + 1, it)
                conv1(k, it)
                if k == NT:
                    conv2(it)
                if k == NT + 1:
                    conv3(it)

            for k in range(LEAD):
                slot(k, 0)
            with pe.Fori(0, G - 1) as it:
                for k in range(LEAD, NT + LEAD):
                    slot(k, it)
            for k in range(LEAD, NT):
                slot(k, G - 1, NT - k)
            conv2(G - 1)
            conv3(G - 1)

            pe.wait_ge(s_T, 32)
            pe.wait_ge(s_U, 1)
            pe.wait_ge(s_U1, 2)
            for n in range(D // LCC):
                if n >= 8:
                    pe.wait_ge(s_lcv, 2 * (n - 7))
                for c in range(LCC):
                    ch = n * LCC + c
                    last = mm(ps[0:TOK, n % 8, c * B:(c + 1) * B], T[:, ch, :], U[:, ch].rearrange("p q i -> p (q i)"),
                              start=True, stop=True)
                last.then_inc(s_lc, 1)
            pe.wait_ge(s_lcv, 2 * D // LCC)

            eye = pkc("eye", PR, 0, PR)

            def scores(i):
                pe.wait_ge(s_q, i + 1)
                pe.wait_ge(s_kb, i + 1)
                for p, m in ((0, P2), (1, TOK)):
                    for h in range(2):
                        last = mm(ps[p * P2:p * P2 + m, 3 + h, 0:HH * TOK], qT[:, h, p * P2:p * P2 + m],
                                  kb[:, h, :, p * P2:p * P2 + TOK], start=True, stop=True)
                last.then_inc(s_S, 1)

            def z_transpose(i):
                pe.wait_ge(s_z, i + 1)
                for h in range(2):
                    last = nc.tensor.transpose(ps[0:DC, 0, h * PR:(h + 1) * PR], z1[:, h * DC:(h + 1) * DC], eye)
                last.then_inc(s_zT, 1)

            def p_transpose(i):
                pe.wait_ge(s_P0, i + 1)
                pe.wait_ge(s_P1, i + 1)
                for b in range(3):
                    for h in range(4):
                        last = nc.tensor.transpose(ps[0:PR, 5 + b, h * PR:(h + 1) * PR], Pb[:, b * 4 + h, :], eye)
                    last.then_inc(s_PT, 1)

            def project(c, bank, at):
                for h in range(2):
                    last = mm(ps[0:DC, bank, at:at + PR], qkc("qkv", h * 3 * D + c * DC, h * 3 * D + (c + 1) * DC),
                              xT[:, h, :], start=(h == 0), stop=(h == 1))
                return last

            def project_k(i):
                pe.wait_ge(s_xT, i + 1)
                project(2, 1, 0)
                project(3, 1, PR).then_inc(s_k, 1)

            def project_qv(i):
                project(0, 2, 0)
                project(1, 2, PR)
                for h in range(2):
                    last = mm(ps[0:PR, 2, 256:256 + D], xT[:, h, :], qkc("qkv", h * 3 * D + 2 * D, (h + 1) * 3 * D),
                              start=(h == 0), stop=(h == 1))
                last.then_inc(s_v, 1)

            def project_out(i, par):
                for h in range(2):
                    mm(ps[0:PR, 0, 0:D], oT[:, par, h, :], qkc("pw", h * D, (h + 1) * D), start=(h == 0), stop=False)
                mm(ps[0:PR, 0, 0:D], row[0:1, D:D + PR], row[0:1, 0:D], start=False, stop=True).then_inc(s_pj, 1)

            def attend(i, par):
                pe.wait_ge(s_V, i + 1)
                pe.wait_ge(s_Pt, 3 * i + 3)
                for h in range(2):
                    for k in range(HH):
                        last = mm(ps[0:DC, 2, h * PR:(h + 1) * PR], V[:, par, h, k * DC:(k + 1) * DC], Pt[:, h * HH + k, :],
                                  start=(k == 0), stop=(k == HH - 1))
                last.then_inc(s_O, 1)

            def z2_transpose(i):
                pe.wait_ge(s_z2, i + 1)
                for h in range(2):
                    last = nc.tensor.transpose(ps[:, 1, h * PR:(h + 1) * PR], z2[:, h * 128:(h + 1) * 128], eye)
                last.then_inc(s_z2T, 1)

            def tile(i, par):
                a, b, c, d, e, f = stages(i)
                if a:
                    if e:
                        pe.wait_ge(s_x1, i - 3)
                    z_transpose(i)
                if b:
                    scores(i - 1)
                if c:
                    p_transpose(i - 2)
                if a:
                    if f:
                        pe.wait_ge(s_x2T, i - 4)
                    project_k(i)
                if c:
                    if b:
                        pe.wait_ge(s_V, i)
                    attend(i - 2, par)
                if d:
                    if not a and e:
                        pe.wait_ge(s_x1, i - 3)
                    pe.wait_ge(s_oT, i - 2)
                    project_out(i - 3, 1 - par)
                if a:
                    if c:
                        pe.wait_ge(s_oT, i - 1)
                    project_qv(i)
                if e:
                    if a:
                        pe.wait_ge(s_kb, i + 1)
                    elif f:
                        pe.wait_ge(s_x2T, i - 4)
                    z2_transpose(i - 4)

            for i in range(5):
                tile(i, i % 2)
            with pe.Fori(2, NP // 2 - 1) as j:
                tile(j * 2 + 1, 1)
                tile(j * 2 + 2, 0)

            def gate(tiles):
                pe.wait_ge(s_sub, NP)
                for i in tiles:
                    pe.wait_ge(s_x2T, min(-(-(i + 1) * 128 // PT), NP))
                    o = ps[:, 4, i * NE:(i + 1) * NE]
                    mm(o, xA[:, i * 128:(i + 1) * 128], pkc("g", 128, 0, NE), start=True, stop=False)
                    last = mm(o, xB[0:D - 128, i * 128:(i + 1) * 128], pkc("g", D - 128, NE, 2 * NE), start=False, stop=True)
                return last

            for i in range(NP - 1, NP + 4):
                tile(i, i % 2)
                if i >= NP + 1:
                    gate(range((i - NP - 1) * 4, min((i - NP) * 4, TT - 2)))
            gate(range(TT - 2, TT)).then_inc(s_lg, 1)

            def layer1(step):
                g, e = step[1] % NG, step[1] // NG % 2
                t0, nt, _ = GROUPS[g]
                if g == 0:
                    pe.wait_ge(s_w1s, expert_of(step) + 1)
                if is_one(step, NG - 1):
                    pe.wait_ge(s_xs, g + 1)
                c64 = D - 128
                for c in range(FC):
                    n = chunks_before(step) + c
                    if not (is_one(step, 0) and c < 4):
                        pe.wait_ge(s_h, n - 3)
                    o = ps[:, (step[1] * FC + c) % 4, 0:nt]
                    k = slice(c * 128, (c + 1) * 128)
                    x = slice(t0, t0 + nt)
                    mm(o, w1h[:, e, 0, k], xAh[:, x], start=True, stop=False)
                    mm(o, w1h[:, e, 0, k], xAl[:, x], start=False, stop=False)
                    mm(o, w1l[:, e, 0, k], xAh[:, x], start=False, stop=False)
                    mm(o, w1h[:, e, 1, k], xBs[:, x], start=False, stop=False)
                    mm(o, w1l[0:c64, e, 1, k], xBs[0:c64, x], start=False, stop=True).then_inc(s_l1, 1)

            def layer2(step):
                e = step[1] // NG
                _, nt, tiles = GROUPS[step[1] % NG]
                pe.wait_ge(s_w2s, expert_of(step) + 1)
                pe.wait_ge(s_lo, chunks_before(step) + FC)
                if not is_one(step, 0):
                    pe.wait_ge(s_acc, tiles_before(step))
                else:
                    pe.wait_ge(s_b2s, 1)
                for j, i in enumerate(tiles):
                    p = 128 if i < TT - 1 else LAST
                    for c in range(FC):
                        t = slice(j * 128, j * 128 + p)
                        a, b = hh[:, step[1] % 2, c, t], hl[:, step[1] % 2, c, t]
                        mm(ps[0:p, 4 + j, 0:2 * D], a, w2s[:, e, c].rearrange("p s n -> p (s n)"),
                           start=(c == 0), stop=False, skip_group_check=True)
                        mm(ps[0:p, 4 + j, 0:D], b, w2s[:, e, c, 0], start=False, stop=False, skip_group_check=True)
                    last = mm(ps[0:p, 4 + j, 0:D], minus[:, 0:p],
                              b2s[:, bass.ds(expert_of(step), 1), :].rearrange("p o n -> p (o n)"), start=False, stop=True,
                              skip_group_check=True)
                    last.then_inc(s_l2, 1)

            layer1((0, 0))

            def experts(ep, last):
                for s in range(2 * NG):
                    if not (last and s + 1 == 2 * NG):
                        layer1((ep, s + 1))
                    layer2((ep, s))

            experts(0, False)
            with pe.Fori(1, NE // 2 - 1) as ep:
                experts(ep, False)
            experts(NE // 2 - 1, True)

        @block.scalar
        def _(act):
            fn = nc.scalar.activation

            def gelu_conv0(k, it):
                half = k % 2
                act.wait_ge(s_conv0, it * NT + k + 1)
                for o in (Ah[:, k % 2], A[:, k % G]):
                    last = fn(o[:, :, 1:1 + RS], ps[0:MA, k % 2, 0:N].rearrange("p (b r) -> p b r", b=B), ACT.Gelu,
                              scale=pkc("v", MA, 2 * half, 2 * half + 1), bias=pkc("v", MA, 2 * half + 1, 2 * half + 2))
                last.then_inc(s_A, 1)

            def gelu_dw(k, it):
                gy = k % NT // 2
                act.wait_ge(s_dw, it * NT + k + 1)
                for o in (Bh, Bt):
                    last = fn(o[:, k % 2, :], ps[0:MI, 2 + k % 2, 0:N], ACT.Gelu, scale=wr[0:MI, gy, 4 * MI:4 * MI + 1],
                              bias=wr[0:MI, gy, 4 * MI + 1:4 * MI + 2])
                last.then_inc(s_B, 1)

            def gelu_region(k, it):
                gy = k % NT // 2
                act.wait_ge(s_C, it * NT + k + 1)
                fn(Dt[:, k % 2], Ct[:, k % 2, :].rearrange("p (b r) -> p b r", b=B), ACT.Gelu,
                   bias=wr[0:MI, gy, 4 * MI + 3:4 * MI + 4]).then_inc(s_D, 1)

            def gelu_conv1(gy, it):
                act.wait_ge(s_conv1, it * G + gy + 1)
                fn(Et[:, gy % G], ps[0:96, 5 + gy % G % 2, 0:256].rearrange("p (s b o) -> p s b o", s=2, b=B), ACT.Gelu,
                   scale=pkc("v", 96, 4, 5), bias=pkc("v", 96, 5, 6)).then_inc(s_E, 1)

            def gelu_conv2(it):
                act.wait_ge(s_conv2, it + 1)
                for half in range(2):
                    p = slice(64 * half, 64 * half + C2)
                    last = fn(Ft[p, :, :], ps[p, 7, 0:G * 64].rearrange("p (g n) -> p g n", g=G), ACT.Gelu,
                              scale=pk[p, PK["v"][0] + 6:PK["v"][0] + 7], bias=pk[p, PK["v"][0] + 7:PK["v"][0] + 8])
                last.then_inc(s_F, 1)

            gelu_conv0(0, 0)
            gelu_conv0(1, 0)
            act.wait_ge(s_fdve, 6)
            fn(fa[:, 5, :], fa[:, 3, :], ACT.Sin).then_inc(s_fact, 1)
            gelu_dw(0, 0)
            act.wait_ge(s_fdve, 12)
            fn(fa[:, 4, :], fa[:, 3, :], ACT.Sin).then_inc(s_fact, 1)
            for h in range(2):
                last = fn(kt[:, 1, h, :], qkc("t"), ACT.Exp, scale=kt[:, 0, 0, h:h + 1])
            last.then_inc(s_fact, 1)
            gelu_conv0(2, 0)
            gelu_dw(1, 0)

            def slot(k, it, more=4):
                if k % 2 == 0 and k >= 2:
                    gelu_conv1(k // 2 - 1, it)
                if k == NT + 1:
                    gelu_conv2(it)
                if more > 3:
                    gelu_conv0(k + 3, it)
                gelu_region(k, it)
                if more > 2:
                    gelu_dw(k + 2, it)

            for k in range(LEAD):
                slot(k, 0)
            with act.Fori(0, G - 1) as it:
                for k in range(LEAD, NT + LEAD):
                    slot(k, it)
            for k in range(LEAD, NT):
                slot(k, G - 1, NT - k)
            gelu_conv1(G - 1, G - 1)
            gelu_conv2(G - 1)

            r = slice(P2, PR)
            for h in range(2):
                act.wait_ge(s_nb, h + 1)
                for i in range(h * NP // 2, (h + 1) * NP // 2):
                    last = fn(U[r, :, 1, i], H[r, i, :], ACT.Identity, scale=rs[r, i:i + 1], bias=nb[r, i:i + 1])
                last.then_inc(s_U1, 1)
            act.wait_ge(s_pb0, 1)

            def xT_copy(i):
                act.wait_ge(s_zT, i + 1)
                for h in range(2):
                    last = fn(xT[:, h, :], ps[0:DC, 0, h * PR:(h + 1) * PR], ACT.Identity,
                              scale=qkc("ln", h, h + 1), bias=qkc("ln", 2 + h, 3 + h))
                last.then_inc(s_xT, 1)

            def pt_copy(i):
                for b in range(3):
                    act.wait_ge(s_PT, 3 * i + b + 1)
                    fn(Pt[:, b * 4:b * 4 + 4, :], ps[0:PR, 5 + b, 0:4 * PR].rearrange("p (h n) -> p h n", h=4),
                       ACT.Copy).then_inc(s_Pt, 1)

            def oT_copy(i, par):
                act.wait_ge(s_O, i + 1)
                fn(oT[:, par], ps[0:DC, 2, 0:2 * PR].rearrange("p (h n) -> p h n", h=2), ACT.Copy).then_inc(s_oT, 1)

            def q_copy(i):
                act.wait_ge(s_v, i + 1)
                fn(qT[:, :, :], ps[0:DC, 2, 0:2 * PR].rearrange("p (h n) -> p h n", h=2), ACT.Copy).then_inc(s_q, 1)

            def v_copy(i, par):
                fn(V[:, par].rearrange("p h (k w) -> p h k w", w=VS)[:, :, :, 0:HD],
                   ps[0:PR, 2, 256:256 + D].rearrange("p (h k d) -> p h k d", h=2, k=HH), ACT.Copy).then_inc(s_V, 1)

            def exps(i):
                act.wait_ge(s_sub, i + 1)
                fn(Sc[:, :, :], Sc[:, :, :], ACT.Exp, scale=HD ** -0.5).then_inc(s_exp, 1)

            def x2T_copy(i):
                act.wait_ge(s_z2T, i + 1)
                for h, (x, first) in enumerate(((xA, xAh), (xB, xBs))):
                    src = ps[:, 1, h * PR:h * PR + 2 * P2].rearrange("p (q t) -> p q t", q=2)[:, :, 0:TOK]
                    for o in (x, first):
                        last = fn(o[:, bass.ds(i * PT, PT)].rearrange("p (q t) -> p q t", q=2), src, ACT.Identity,
                                  scale=pkc("v", 128, 8 + h, 9 + h), bias=pkc("v", 128, 10 + h, 11 + h))
                last.then_inc(s_x2T, 1)

            def tile(i, par):
                a, b, c, d, e, f = stages(i)
                if a:
                    xT_copy(i)
                if f:
                    x2T_copy(i - 5)
                if c:
                    pt_copy(i - 2)
                if b:
                    exps(i - 1)
                if c:
                    oT_copy(i - 2, par)
                if a:
                    q_copy(i)
                    v_copy(i, par)

            for i in range(5):
                tile(i, i % 2)
            with act.Fori(2, NP // 2 - 1) as j:
                tile(j * 2 + 1, 1)
                tile(j * 2 + 2, 0)
            for i in range(NP - 1, NP + 5):
                tile(i, i % 2)

            act.wait_ge(s_d21, 1)
            fn(sc[:, :, 1], sc[:, :, 0], ACT.Exp).then_inc(s_cwe, 1)

            def hidden(step):
                nt = GROUPS[step[1] % NG][1]
                e = step[1] // NG
                for c in range(FC):
                    n = chunks_before(step) + c
                    act.wait_ge(s_l1, n + 1)
                    if c == 0 and not is_one(step, 1):
                        back = len(GROUPS[(step[1] - 1) % NG][2])
                        act.wait_ge(s_l2, tiles_before(step) - back)
                    if not (is_one(step, 0) and c < 2):
                        act.wait_ge(s_lo, n - 1)
                    for o in (hh[:, step[1] % 2, c, 0:nt], hf[:, c % 2, 0:nt]):
                        last = fn(o, ps[:, (step[1] * FC + c) % 4, 0:nt], ACT.Gelu, bias=b1s[:, e, c:c + 1])
                    last.then_inc(s_h, 1)

            def experts(ep):
                for s in range(2 * NG):
                    hidden((ep, s))

            experts(0)
            with act.Fori(1, NE // 2) as ep:
                experts(ep)

        @block.gpsimd
        def _(pool):
            gp = nc.gpsimd
            gp.memset(nhalf[:, :], -0.5).then_inc(s_kt, 1)
            pool.wait_ge(s_kt, 1)

            def split_weights(gy, it):
                pool.wait_ge(s_w[gy], (it + 1) * 16)
                gp.tensor_tensor(junk[:, :], nhalf[0:1, 0:1], nhalf[0:1, 0:1], ALU.add)
                gp.tensor_copy(wh[:, gy, :], wr[:, gy, 0:4 * MI]).then_inc(s_ph, 1)
                pool.wait_ge(s_ph, it * G + gy + 1)
                gp.tensor_tensor(wl[:, gy, :], wr[:, gy, 0:4 * MI], wh[:, gy, :].bitcast(F32), ALU.subtract).then_inc(s_ws, 1)

            for gy in range(G):
                split_weights(gy, 0)
            pool.wait_ge(s_kd, 16)
            rows_each = -(-TOK // G)
            for gy in range(G):
                split_weights(gy, 1)
                with pool.Fori(gy * rows_each, min((gy + 1) * rows_each, TOK)) as s:
                    pool.dma_start(td[bass.ds(s, 1)], kd[:, bass.ds(TOK - 1 - s, TOK)].rearrange("c (o t) -> o c t", o=1)
                                   ).then_inc(s_td, 16)
            with pool.Fori(2, G) as it:
                for gy in range(G):
                    split_weights(gy, it)
            pool.wait_ge(s_td, 16 * TOK)
            pool.wait_ge(s_ws, G * G)
            gp.memset(T[P2 // 2:P2, :, :], 0.0).then_inc(s_T0, 1)
            pool.wait_ge(s_T0, 1)
            for p in range(2):
                pool.dma_start(T[p * P2:p * P2 + TOK, :, :], td).then_inc(s_T, 16)
            pool.wait_ge(s_hs, G)
            gp.memset(U[:, :, :, :], 0.0).then_inc(s_U0, 1)
            gp.memset(V[:, :, :, :], 0.0)
            gp.memset(Pb[:, :, :], 0.0).then_inc(s_pb0, 1)

            def split_expert(e, half):
                gp.tensor_tensor(junk[:, :], nhalf[0:1, 0:1], nhalf[0:1, 0:1], ALU.add)
                k = 3 * e
                gp.tensor_copy(w1h[:, half], w1f[:, :, :]).then_inc(s_ph2, 1)
                gp.tensor_copy(b1s[:, half, :], w2f[:, FC * D:FC * D + FC]).then_inc(s_ph2, 1)
                gp.tensor_copy(w2s[:, half, :, 0], w2f[:, 0:FC * D].rearrange("p (c n) -> p c n", c=FC)).then_inc(s_ph2, 1)
                pool.wait_ge(s_ph2, k + 3)
                gp.tensor_tensor(w1l[:, half], w1f[:, :, :], w1h[:, half].bitcast(F32), ALU.subtract).then_inc(s_w1s, 1)
                gp.tensor_tensor(w2s[:, half, :, 1], w2f[:, 0:FC * D].rearrange("p (c n) -> p c n", c=FC),
                                  w2s[:, half, :, 0].bitcast(F32), ALU.subtract).then_inc(s_w2s, 1)

            def power(pairs, n):
                pool.wait_ge(s_va, n)
                gp.tensor_tensor(rs[:, pairs], va[:, pairs], nhalf[:, pairs], ALU.pow).then_inc(s_rs, 1)

            for h in range(2):
                power(slice(h * NP // 2, (h + 1) * NP // 2), h + 1)
            for e in range(2):
                pool.wait_ge(s_wf, 32 * (e + 1))
                split_expert(e, e)
            def probabilities(i):
                pool.wait_ge(s_ri, i + 1)
                if not (isinstance(i, int) and i == 0):
                    pool.wait_ge(s_PT, 3 * i)
                gp.tensor_tensor(Pb[P2:PR, :, P2:PR], Sc[P2:PR, :, :], ri[P2:PR, :].unsqueeze(2).to_broadcast([TOK, NH, TOK]),
                                 ALU.mult).then_inc(s_P1, 1)

            def finish(i):
                pool.wait_ge(s_st, 3 * i + 3)
                gp.tensor_tensor(st2[:, 9:10], st2[:, 8:9], nhalf[:, 0:1], ALU.pow).then_inc(s_pow, 1)
                pool.wait_ge(s_x1, i + 1)
                gp.tensor_tensor(H[:, bass.ds(i, 1), :], H[:, bass.ds(i, 1), :], x1[:, :].unsqueeze(1), ALU.add
                                 ).then_inc(s_R, 1)

            def tile(i):
                _, b, _, d, e, _ = stages(i)
                if b:
                    if e:
                        pool.wait_ge(s_R, i - 3)
                    probabilities(i - 1)
                    pool.wait_ge(s_P1, i)
                if d:
                    finish(i - 3)

            def powers(q):
                for n in range(2):
                    power(slice(q * QP, (q + 1) * QP), 3 + 2 * q + n)
                pool.wait_ge(s_rs, 4 + 2 * q)

            powers(0)
            for i in range(5):
                if i + 1 < NP // QP:
                    powers(i + 1)
                tile(i)
            with pool.Fori(2, NP // 2 - 1) as j:
                tile(j * 2 + 1)
                tile(j * 2 + 2)
            for i in range(NP - 1, NP + 3):
                tile(i)
            pool.wait_ge(s_R, NP)
            pool.wait_ge(s_b2, 16)
            gp.memset(minus[:, :].bitcast(F32), 0.0).then_inc(s_b2h, 1)
            gp.tensor_copy(b2s[:, :, :], b2x[:, :, :])
            pool.wait_ge(s_b2h, 1)
            gp.memset(minus[0:2, :].bitcast(F32), -1.0).then_inc(s_b2h, 1)
            with pool.Fori(1, NE // 2) as ep:
                for half in range(2):
                    e = ep * 2 + half
                    pool.wait_ge(s_wf, (e + 1) * 32)
                    pool.wait_ge(s_l2, (e - 1) * TT)
                    split_expert(e, half)

        @block.vector
        def _(dve):
            ve = nc.vector
            chain = [0, 0]

            def link(ins):
                chain[1] += 1
                ins.then_inc(s_ch, 1)
                dve.wait_ge(s_ch, chain[0] + chain[1])

            ve.memset(Ah[:, :, :, 0:RS + 2:RS + 1].bitcast(F32), 0.0)
            ve.memset(Al[:, :, :, 0:RS + 2:RS + 1].bitcast(F32), 0.0).then_inc(s_init, 1)
            dve.wait_ge(s_pk, 16)
            ve.tensor_copy(w0h[:, :], pkc("w0", KX)).then_inc(s_w0s, 1)
            dve.wait_ge(s_w0s, 1)
            ve.tensor_tensor(w0l[:, :], pkc("w0", KX), w0h[:, :].bitcast(F32), ALU.subtract).then_inc(s_w0s, 1)

            done = [0]

            def mark(ins):
                done[0] += 1
                ins.then_inc(s_fdve, 1)
                dve.wait_ge(s_fdve, done[0])

            def filter_sine(layer):
                dve.wait_ge(s_fpe, layer + 1)
                mark(ve.tensor_scalar(fa[:, 0, :], ps[0:16, 7, 64 * layer:64 * layer + TOK],
                                      qkc("f", 82 + 2 * layer, 83 + 2 * layer, 16),
                                      qkc("f", 83, 84, 16), ALU.add, ALU.mult))
                mark(ve.tensor_scalar(fa[:, 1, :], fa[:, 0, :], float(1 / (2 * np.pi)), MAGIC, ALU.mult, ALU.add))
                mark(ve.tensor_scalar(fa[:, 1, :], fa[:, 1, :], MAGIC, None, ALU.subtract))
                mark(ve.scalar_tensor_tensor(fa[:, 2, :], fa[:, 1, :], -TWO_PI_HI, fa[:, 0, :], ALU.mult, ALU.add))
                mark(ve.scalar_tensor_tensor(fa[:, 0, :], fa[:, 1, :], -TWO_PI_LO, fa[:, 2, :], ALU.mult, ALU.add))
                mark(ve.tensor_scalar(fa[:, 3, :], fa[:, 0, :], PI_MAX, -PI_MAX, ALU.min, ALU.max))

            def split_input(k, it):
                gy, half = k % NT // 2, k % 2
                t = it * NT + k
                if half == 0:
                    dve.wait_ge(s_x[gy], (it + k // NT + 1) * 16)
                if k >= 2:
                    dve.wait_ge(s_conv0, t - 1)
                link(ve.tensor_copy(xh[:, k % 2, :], xin[:, gy, half, :]))
                ve.tensor_tensor(xl[:, k % 2, :], xin[:, gy, half, :], xh[:, k % 2, :].bitcast(F32), ALU.subtract
                                 ).then_inc(s_xsp, 1)

            def split_conv0(k, it):
                dve.wait_ge(s_A, it * NT + k + 1)
                ve.tensor_tensor(Al[:, k % 2, :, 1:1 + RS], A[:, k % G, :, 1:1 + RS], Ah[:, k % 2, :, 1:1 + RS].bitcast(F32),
                                 ALU.subtract).then_inc(s_Al, 1)

            def split_dw(k, it):
                dve.wait_ge(s_B, it * NT + k + 1)
                ve.tensor_tensor(Bl[:, k % 2, :], Bt[:, k % 2, :], Bh[:, k % 2, :].bitcast(F32), ALU.subtract).then_inc(s_Bl, 1)

            def add_input(k, it):
                dve.wait_ge(s_pw, it * NT + k + 1)
                gy = k % NT // 2
                ve.scalar_tensor_tensor(Ct[:, k % 2, :].rearrange("p (b r) -> p b r", b=B),
                                        ps[0:MI, 4, 0:N].rearrange("p (b r) -> p b r", b=B),
                                        wr[0:MI, gy, 4 * MI + 2:4 * MI + 3], A[0:MI, k % G, :, 1:1 + RS],
                                        ALU.mult, ALU.add).then_inc(s_C, 1)

            def tokens(it):
                dve.wait_ge(s_conv3, it + 1)
                for g, n in ((0, 128), (1, 96)):
                    last = ve.tensor_tensor(hs[0:n, g, :], ps[0:n, 7, g * D:(g + 1) * D], s3bc[0:n, :], ALU.mult)
                link(last)
                for g, n in ((0, 128), (1, 96)):
                    last = ve.tensor_tensor(hs[0:n, g, :], hs[0:n, g, :], b3bc[0:n, :], ALU.add)
                last.then_inc(s_hs, 1)

            split_input(0, 0)
            split_input(1, 0)
            ve.memset(Ft[:, :, :], 0.0)
            ve.memset(kp[:, :, :], 0.0)
            split_conv0(0, 0)
            dve.wait_ge(s_const, 16 * 5)
            for h in range(2):
                ve.tensor_scalar(kt[:, 0, 0, h:h + 1], qkc("k3", 2 + h, 3 + h), -1.0, None, ALU.mult)
            filter_sine(0)
            split_conv0(1, 0)
            split_input(2, 0)
            filter_sine(1)
            split_input(3, 0)
            ve.memset(H[:, :, :], 0.0).then_inc(s_init, 1)
            dve.wait_ge(s_init, 2)
            dve.wait_ge(s_fpe, 3)
            dve.wait_ge(s_fact, 3)
            for h in range(2):
                last = ve.scalar_tensor_tensor(kp[:, h, TOK - 1:2 * TOK - 1], ps[0:DC, 7, 128 + 64 * h:128 + 64 * h + TOK],
                                               qkc("k3", h, h + 1), kt[:, 1, h, :], ALU.add, ALU.mult)
            mark(last)
            mark(ve.tensor_scalar(kp[:, :, :], kp[:, :, :], 1.0 / KL, None, ALU.mult))
            mark(ve.tensor_tensor(kp[:, :, TOK - 1:TOK], kp[:, :, TOK - 1:TOK],
                                  qkc("k3", 4, 6).unsqueeze(2), ALU.add))
            split_conv0(2, 0)
            split_dw(0, 0)
            add_input(0, 0)

            def slot(k, it, more=5):
                if k == NT + 2:
                    tokens(it)
                if more > 1:
                    split_dw(k + 1, it)
                if more > 4:
                    split_input(k + 4, it)
                if more > 3:
                    split_conv0(k + 3, it)
                if more > 1:
                    add_input(k + 1, it)

            for k in range(LEAD):
                slot(k, 0)
            before = chain[1]
            with dve.Fori(0, G - 1) as it:
                chain[0], chain[1] = it * (NT + 1) + before, 0
                for k in range(LEAD, NT + LEAD):
                    slot(k, it)
            assert chain[1] == NT + 1
            chain[0], chain[1] = (G - 1) * (NT + 1) + before, 0
            for k in range(LEAD, NT):
                slot(k, G - 1, NT - k)
            dve.wait_ge(s_hd, 16 * G * (G - 1))
            tokens(G - 1)

            dve.wait_ge(s_H, 16 * 2 * (G + 1))
            dve.wait_ge(s_cls, 32)
            def variances(x, pairs):
                for i in pairs:
                    last = ve.bn_stats(st[:, i, :], x[:, i, :])
                link(last)
                for i in pairs:
                    last = ve.bn_aggr(mv[:, i, :], st[:, i, :])
                link(last)
                r = slice(pairs[0], pairs[-1] + 1)
                ve.tensor_scalar(va[:, r], mv[:, r, 1], EPS, None, ALU.add).then_inc(s_va, 1)

            halves = range(0, NP // 2), range(NP // 2, NP)
            for h in halves:
                variances(H, h)
            for n, h in enumerate(halves):
                dve.wait_ge(s_rs, n + 1)
                q = slice(h[0], h[-1] + 1)
                ve.scalar_tensor_tensor(nb[:, q], mv[:, q, 0], -1.0, rs[:, q], ALU.mult, ALU.mult).then_inc(s_nb, 1)
                dve.wait_ge(s_U0, 1)
                for i in h:
                    last = ve.tensor_scalar(U[0:TOK, :, 0, i], H[0:TOK, i, :], mv[0:TOK, i, 0:1], rs[0:TOK, i:i + 1],
                                            ALU.subtract, ALU.mult)
            last.then_inc(s_U, 1)
            for n in range(D // LCC):
                dve.wait_ge(s_lc, n + 1)
                y = ps[0:TOK, n % 8, :].rearrange("p (c q i) -> p q i c", c=LCC, q=2)
                for p in range(2):
                    r = slice(p * P2, p * P2 + TOK)
                    ve.tensor_tensor(H[r, :, n * LCC:(n + 1) * LCC], y[:, p], H[r, :, n * LCC:(n + 1) * LCC], ALU.add
                                     ).then_inc(s_lcv, 1)
            dve.wait_ge(s_lcv, 2 * D // LCC)
            ve.memset(xA[:, B * TOK:TP], 0.0)
            ve.memset(xB[:, B * TOK:TP], 0.0)
            def norm_in(q):
                variances(H, range(q * QP, (q + 1) * QP))

            def norm_out(q):
                pairs = range(q * QP, (q + 1) * QP)
                dve.wait_ge(s_rs, 3 + 2 * q)
                for i in pairs:
                    last = ve.tensor_scalar(X1[:, i, :], H[:, i, :], mv[:, i, 0:1], rs[:, i:i + 1], ALU.subtract, ALU.mult)
                link(last)
                variances(X1, pairs)

            def z_norm(i):
                if not (isinstance(i, int) and i == 0):
                    dve.wait_ge(s_zT, i)
                ve.tensor_scalar(z1[:, :].unsqueeze(1), X1[:, bass.ds(i, 1), :],
                                 mv[:, bass.ds(i, 1), 0:1].rearrange("p o n -> p (o n)"),
                                 rs[:, bass.ds(i, 1)], ALU.subtract, ALU.mult).then_inc(s_z, 1)

            def softmax_top(i):
                dve.wait_ge(s_S, i + 1)
                S = ps[0:PR, 3:5, 0:HH * TOK].rearrange("p h (k m) -> p h k m", k=HH)
                m = mx[:, :].rearrange("p (h k) -> p h k", h=2)
                ve.tensor_reduce(m, S, AX.X, ALU.max).then_inc(s_mx, 1)
                dve.wait_ge(s_mx, i + 1)
                if not (isinstance(i, int) and i == 0):
                    dve.wait_ge(s_P0, i)
                    dve.wait_ge(s_P1, i)
                for h in range(2):
                    last = ve.tensor_tensor(Sc[:, h * HH:(h + 1) * HH, :], S[:, h],
                                            m[:, h].unsqueeze(2).to_broadcast([PR, HH, TOK]), ALU.subtract)
                last.then_inc(s_sub, 1)

            def k_blocks(i):
                dve.wait_ge(s_k, i + 1)
                for h in range(2):
                    last = ve.tensor_tensor(kb[:, h], ps[0:DC, 1, h * PR:(h + 1) * PR].unsqueeze(1).to_broadcast([DC, HH, PR]),
                                            qkc("mask").unsqueeze(2).to_broadcast([DC, HH, PR]), ALU.mult)
                last.then_inc(s_kb, 1)

            def probabilities(i):
                dve.wait_ge(s_exp, i + 1)
                ve.tensor_reduce(sm[:, :], Sc[:, :, :], AX.X, ALU.add).then_inc(s_sum, 1)
                dve.wait_ge(s_sum, i + 1)
                ve.reciprocal(ri[:, :], sm[:, :]).then_inc(s_ri, 1)
                dve.wait_ge(s_ri, i + 1)
                if not (isinstance(i, int) and i == 0):
                    dve.wait_ge(s_PT, 3 * i)
                ve.tensor_tensor(Pb[0:TOK, :, 0:TOK], Sc[0:TOK, :, :], ri[0:TOK, :].unsqueeze(2).to_broadcast([TOK, NH, TOK]),
                                 ALU.mult).then_inc(s_P0, 1)

            def add_attention(i):
                dve.wait_ge(s_pj, i + 1)
                if not (isinstance(i, int) and i == 0):
                    dve.wait_ge(s_R, i)
                    dve.wait_ge(s_z2, i)
                ve.tensor_tensor(x1[:, :].unsqueeze(1), ps[0:PR, 0, 0:D].unsqueeze(1), X1[:, bass.ds(i, 1), :],
                                 ALU.add).then_inc(s_x1, 1)
                dve.wait_ge(s_x1, i + 1)
                ve.bn_stats(st2[:, 0:6], x1[:, :]).then_inc(s_st, 1)
                dve.wait_ge(s_st, 3 * i + 1)
                ve.memset(st2[:, 10:11], 0.0)
                ve.bn_aggr(st2[:, 6:8], st2[:, 0:6]).then_inc(s_st, 1)
                dve.wait_ge(s_st, 3 * i + 2)
                ve.tensor_scalar(st2[:, 8:9], st2[:, 7:8], EPS, None, ALU.add).then_inc(s_st, 1)
                dve.wait_ge(s_pow, i + 1)
                if not (isinstance(i, int) and i == 0):
                    dve.wait_ge(s_z2T, i)
                ve.tensor_scalar(z2[:, D:256], x1[:, 128:D], st2[:, 6:7], st2[:, 9:10], ALU.subtract, ALU.mult)
                ve.tensor_scalar(z2[:, 0:D], x1[:, :], st2[:, 6:7], st2[:, 9:10], ALU.subtract, ALU.mult).then_inc(s_z2, 1)

            def tile(i, par):
                a, b, c, d, e, f = stages(i)
                group = i + 1 if isinstance(i, int) and i + 1 < NP // QP else None
                if b:
                    softmax_top(i - 1)
                if group:
                    norm_in(group)
                if a:
                    k_blocks(i)
                if group:
                    norm_out(group)
                if b:
                    probabilities(i - 1)
                if isinstance(i, int) and i + 1 == NP // QP:
                    dve.wait_ge(s_rs, 2 + 2 * (NP // QP))
                if a and not (isinstance(i, int) and i + 1 == NP):
                    z_norm(i + 1)
                if d:
                    add_attention(i - 3)

            norm_in(0)
            norm_out(0)
            dve.wait_ge(s_rs, 4)
            z_norm(0)
            for i in range(5):
                tile(i, i % 2)
            with dve.Fori(2, NP // 2 - 1) as j:
                tile(j * 2 + 1, 1)
                tile(j * 2 + 2, 0)

            def split_group(g):
                t0, nt, _ = GROUPS[g]
                dve.wait_ge(s_x2T, min(-(-(t0 + nt) // PT), NP))
                t = slice(t0, t0 + nt)
                ve.tensor_tensor(xAl[:, t], xA[:, t], xAh[:, t].bitcast(F32), ALU.subtract)
                ve.tensor_tensor(xBs[D - 128:, t], xB[D - 128:, t], xBs[D - 128:, t].bitcast(F32), ALU.subtract
                                 ).then_inc(s_xs, 1)

            for i in range(NP - 1, NP + 4):
                tile(i, i % 2)
                if i >= NP:
                    split_group(i - NP)
            def hidden_low(step, chunks=range(FC)):
                nt = GROUPS[step[1] % NG][1]
                for c in chunks:
                    dve.wait_ge(s_h, chunks_before(step) + c + 1)
                    h = step[1] % 2
                    ve.tensor_tensor(hl[:, h, c, 0:nt], hf[:, c % 2, 0:nt], hh[:, h, c, 0:nt].bitcast(F32), ALU.subtract
                                     ).then_inc(s_lo, 1)

            dve.wait_ge(s_lg, 1)
            ve.tensor_tensor(lg[:, :, :], ps[:, 4, 0:TT * NE].rearrange("p (i e) -> p i e", i=TT),
                             pkc("gb", 128).unsqueeze(1).to_broadcast([128, TT, NE]), ALU.add).then_inc(s_lgc, 1)
            dve.wait_ge(s_lgc, 1)
            for i in range(TT):
                last = ve.max(m8[:, i, :], lg[:, i, :])
            link(last)
            ve.tensor_tensor(sc[:, :, 0], m8[:, :, 1], m8[:, :, 0], ALU.subtract).then_inc(s_d21, 1)
            hidden_low((0, 0), range(0, 2))
            for i in range(TT):
                last = ve.max_index(i8[:, i, :], m8[:, i, :], lg[:, i, :])
            link(last)
            link(ve.tensor_copy(f8[:, :, :], i8[:, :, 0:2]))
            for r in range(2):
                last = ve.tensor_tensor(oh[:, r], iot[:, :].unsqueeze(1).to_broadcast([128, TT, NE]),
                                        f8[:, :, r:r + 1].to_broadcast([128, TT, NE]), ALU.is_equal)
            link(last)
            hidden_low((0, 0), range(2, 4))
            dve.wait_ge(s_cwe, 1)
            link(ve.tensor_scalar(sc[:, :, 0], sc[:, :, 1], 1.0, None, ALU.add))
            link(ve.reciprocal(sc[:, :, 2], sc[:, :, 0]))
            link(ve.tensor_tensor(sc[:, :, 3], sc[:, :, 1], sc[:, :, 2], ALU.mult))
            for r in range(2):
                last = ve.tensor_tensor(oh[:, r], oh[:, r], sc[:, :, 2 + r:3 + r].to_broadcast([128, TT, NE]), ALU.mult)
            link(last)
            ve.tensor_tensor(cw[:, :, :], oh[:, 0], oh[:, 1], ALU.add).then_inc(s_cw, 1)
            hidden_low((0, 0), range(4, FC))
            dve.wait_ge(s_b2h, 2)
            ve.scalar_tensor_tensor(b2s[:, :, :], b2s[:, :, :].bitcast(F32), pkc("eye", 128, 1, 2), b2x[:, :, :],
                                    ALU.mult, ALU.subtract).then_inc(s_b2s, 1)

            def add_outputs(step):
                tiles = GROUPS[step[1] % NG][2]
                for j, i in enumerate(tiles):
                    p = 128 if i < TT - 1 else LAST
                    n = tiles_before(step) + j
                    dve.wait_ge(s_l2, n + 1)
                    if not is_one(step, NG - 1):
                        dve.wait_ge(s_acc, n - TT + 1)
                    ve.scalar_tensor_tensor(acc[0:p, i, :], ps[0:p, 4 + j, 0:D], cw[0:p, i, bass.ds(expert_of(step), 1)],
                                            acc[0:p, i, :], ALU.mult, ALU.add).then_inc(s_half, 1)
                for j, i in enumerate(tiles):
                    p = 128 if i < TT - 1 else LAST
                    n = tiles_before(step) + j
                    dve.wait_ge(s_half, n + 1)
                    ve.scalar_tensor_tensor(acc[0:p, i, :], ps[0:p, 4 + j, D:2 * D], cw[0:p, i, bass.ds(expert_of(step), 1)],
                                            acc[0:p, i, :], ALU.mult, ALU.add).then_inc(s_acc, 1)

            def experts(ep, last):
                for s in range(2 * NG):
                    if not (last and s + 1 == 2 * NG):
                        hidden_low((ep, (s + 1)))
                    if is_one((ep, s), 0):
                        dve.wait_ge(s_cw, 1)
                        dve.wait_ge(s_rl, 32)
                    add_outputs((ep, s))

            experts(0, False)
            with dve.Fori(1, NE // 2 - 1) as ep:
                experts(ep, False)
            experts(NE // 2 - 1, True)


def lay_out(a):
    f = np.float32
    t = "L0_tok_"
    x = np.asarray(a["x"])
    xp = np.zeros((B, CI, G * RS + 2, G * RS + 4), f)
    xp[:, :, 1:-1, 2:-2] = x
    xh = np.zeros((G, G, 3, HW + 4, CI, 2, B, RS), f)
    for gx in range(G):
        for gy in range(G):
            for half in range(2):
                for dy in range(3):
                    c0 = RS * gx + HW * half
                    v = xp[:, :, RS * gy + dy:RS * gy + dy + RS, c0:c0 + HW + 4]
                    xh[gx, gy, dy, :, :, half] = v.transpose(3, 1, 0, 2)
    xh = xh.reshape(G * G, KX, 2 * N)

    def rowof(j, c):
        return c * HW + j - 1 if 1 <= j <= HW else MI + (C1 if j else 0) + c

    wdw = np.asarray(a[t + "wdw"]).reshape(G, G, C1, 3, 3)
    wpw = np.asarray(a[t + "wpw"]).reshape(G, G, C1, C1)
    wreg = np.zeros((G, G, MA, WR), f)
    for c in range(C1):
        for w in range(HW):
            for dy in range(3):
                for dx in range(3):
                    wreg[:, :, rowof(w + dx, c), dy * MI + c * HW + w] = wdw[:, :, c, dy, dx].T
            for co in range(C1):
                wreg[:, :, c * HW + w, 3 * MI + co * HW + w] = wpw[:, :, co, c].T
            for n, name in enumerate(("sdw", "bdw", "spw", "bpw")):
                wreg[:, :, c * HW + w, 4 * MI + n] = np.asarray(a[t + name]).reshape(G, G, C1)[:, :, c].T
    wreg = wreg.reshape(G * G, MA, WR)

    pack = np.zeros((128, PKW), f)
    w0, s0, b0 = (np.asarray(a[t + n]) for n in ("w0", "s0", "b0"))
    o = PK["w0"][0]
    v = PK["v"][0]
    for c in range(C1):
        for j in range(HW + 2):
            for dx in range(3):
                for dy in range(3):
                    for ci in range(CI):
                        pack[(dy * (HW + 4) + j + dx) * CI + ci, o + rowof(j, c)] = w0[c, ci, dy, dx]
            if j > 0:
                pack[rowof(j, c), v:v + 2] = s0[c], b0[c]
            if j <= HW:
                pack[rowof(j, c), v + 2:v + 4] = s0[c], b0[c]
    w1, w2, w3 = (np.asarray(a[t + n]) for n in ("w1", "w2", "w3"))
    for ox in range(2):
        for c in range(C1):
            for dx in range(4):
                for dy in range(4):
                    p = PK["w1"][0] + dy * 96 + ox * C2
                    pack[c * HW + ox * 4 + dx, p:p + C2] = w1[:, c, dy, dx]
        pack[ox * C2:ox * C2 + C2, v + 4] = np.asarray(a[t + "s1"])
        pack[ox * C2:ox * C2 + C2, v + 5] = np.asarray(a[t + "b1"])
        pack[ox * 64:ox * 64 + C2, v + 6] = np.asarray(a[t + "s2"])
        pack[ox * 64:ox * 64 + C2, v + 7] = np.asarray(a[t + "b2"])
        for dy in range(2):
            p = PK["w2"][0] + dy * C2
            pack[ox * C2:ox * C2 + C2, p:p + C2] = w2[:, :, dy, ox].T
            p = PK["w3"][0] + dy * D
            pack[ox * 64:ox * 64 + C2, p:p + D] = w3[:, :, dy, ox].T
    p = PK["eye"][0]
    pack[:, p:p + 128] = np.eye(128, dtype=f)
    m = "L0_ffn_"
    for k, name in enumerate(("ln2_g", "ln2_b")):
        g = np.asarray(a[m + name])
        pack[:, v + 8 + 2 * k] = g[0:128]
        pack[:, v + 9 + 2 * k] = np.tile(g[128:], 2)
    gw = np.asarray(a[m + "gate_w"]).T
    pack[:, PK["g"][0]:PK["g"][0] + NE] = gw[0:128]
    pack[0:D - 128, PK["g"][0] + NE:PK["g"][0] + 2 * NE] = gw[128:]
    pack[:, PK["gb"][0]:PK["gb"][0] + NE] = np.asarray(a[m + "gate_b"])

    qp = np.zeros((96, QKW), f)

    def put(name, v, at=0):
        v = np.asarray(v)
        o = QK[name][0] + at
        qp[0:v.shape[0], o:o + v.shape[1]] = v

    n, m = "L0_attn_", "L0_ffn_"
    for h in range(2):
        c = slice(h * DC, (h + 1) * DC)
        put("qkv", np.asarray(a[m + "qkv_w"]).T[c], h * 3 * D)
        put("pw", np.asarray(a[m + "proj_w"]).T[c], h * D)
        for k, name in enumerate(("ln1_g", "ln1_b")):
            put("ln", np.asarray(a[m + name])[c, None], 2 * k + h)
        for k, name in enumerate(("b3", "deltas_abs", "bias")):
            put("k3", np.asarray(a[n + name])[c, None], 2 * k + h)
    put("mask", np.kron(np.eye(HH, dtype=f), np.ones((HD, 1), f)))
    pos = np.linspace(0.0, 1.0, TOK, dtype=f)
    put("t", np.tile(pos, (DC, 1)))
    put("w3", np.asarray(a[n + "w3"]).T)
    ang = 1e-4 * (2.0 * np.pi * np.linspace(0.0, TOK - 1.0, TOK) / TOK)
    put("f", np.asarray(a[n + "w1"]).T, 0)
    put("f", np.stack([pos, np.cos(ang), -np.sin(ang)]).astype(f), 16)
    put("f", np.asarray(a[n + "w2"]).T, 66)
    for k, name in enumerate(("b1", "freq", "b2")):
        put("f", np.asarray(a[n + name])[:, None], 82 + k)

    rows = np.zeros((1, D + 128), f)
    rows[0, 0:D] = np.asarray(a[m + "proj_b"])
    rows[0, D:] = 1.0

    w1t = np.asarray(a[m + "w1"]).transpose(0, 2, 1)
    ew1 = np.concatenate([w1t[:, 0:128], np.tile(w1t[:, 128:], (1, 2, 1))], axis=2)
    w2e = np.asarray(a[m + "w2"]).reshape(NE, D, FC, 128).transpose(0, 3, 2, 1).reshape(NE, 128, FC * D)
    b1e = np.asarray(a[m + "b1"]).reshape(NE, FC, 128).transpose(0, 2, 1)
    ew2 = np.concatenate([w2e, b1e], axis=2)
    return dict(xh=xh, wreg=wreg, pack=pack, qpack=qp, rows=rows, b2=np.asarray(a[m + "b2"]).reshape(1, NE, D), ew1=ew1, ew2=ew2,
                cls=np.asarray(a["cls_tok"]).reshape(1, 1, D), s3=np.asarray(a[t + "s3"]).reshape(1, D),
                b3=np.asarray(a[t + "b3"]).reshape(1, D), iota=np.tile(np.arange(NE, dtype=f), (128, 1)))


def kernel(**inputs):
    import concourse.bacc as bacc
    from concourse.bass_utils import run_bass_kernel_spmd

    nc = bacc.Bacc("TRN2", target_bir_lowering=False, num_devices=1)
    arrays, args = {}, []
    for name, v in lay_out(inputs).items():
        v = np.ascontiguousarray(v)
        arrays["in_" + name] = v
        args.append(nc.dram_tensor("in_" + name, v.shape, mybir.dt.from_np(v.dtype), kind="ExternalInput").ap())
    for name, shape in (("kd", (D, KL)), ("td", (TOK, D, TOK)), ("hd", (B, TOK, D)), ("rd", (B, TOK, D))):
        args.append(nc.dram_tensor(name, shape, F32, kind="Internal").ap())
    args.append(nc.dram_tensor("out", (B, TOK, D), F32, kind="ExternalOutput").ap())
    tower(nc, *args)
    return run_bass_kernel_spmd(nc, [arrays], core_ids=[0]).results[0]["out"]
```
